# Optimizing a Trainium2 kernel written in Bass

```python
import numpy as np
import jax
import jax.numpy as jnp

def _softmax(x, axis=-1):
    return jax.nn.softmax(x, axis=axis)

def _gelu(x):
    return jax.nn.gelu(x, approximate=True)

def _silu(x):
    return jax.nn.silu(x)

def _sigmoid(x):
    return jax.nn.sigmoid(x)

def _layernorm(x, axis=-1, eps=1e-05):
    m = jnp.mean(x, axis=axis, keepdims=True)
    v = jnp.var(x, axis=axis, keepdims=True)
    return (x - m) / jnp.sqrt(v + eps)

def _scatter_add(tgt, idx, src, axis=0):
    return tgt.at[idx].add(src)

def _segment_sum(src, seg, n):
    return jax.ops.segment_sum(src, seg, n)
kernel_name = 'mk_decoder_postln_d1_seqx_r8_3bea43'

def setup_inputs(seed: int=0):
    np.random.seed(seed)
    _w = jnp.asarray

    def _rec_inputs():
        import jax
        import jax.numpy as jnp
        _rk = jax.random.key(seed)
        x = 7.22e-05 + 1 * jax.random.normal(jax.random.fold_in(_rk, 1), (64, 128, 128), jnp.float32)
        _lenS = 128 - jax.random.randint(jax.random.fold_in(_rk, 7), (64,), 0, max(1, 128 // 4) + 1, jnp.int32)
        _lenS2 = 120 - jax.random.randint(jax.random.fold_in(_rk, 8), (64,), 0, max(1, 120 // 4) + 1, jnp.int32)
        _ctx_1024P = jax.random.normal(jax.random.fold_in(_rk, 11), (64, 16, 128), jnp.float32)
        _ctx_1024c = jax.random.dirichlet(jax.random.fold_in(_rk, 511), 0.3 * jnp.ones((16,), jnp.float32), (64, 120))
        _ctx_1024t = jnp.einsum('bsk,bkd->bsd', _ctx_1024c, _ctx_1024P)
        _ctx_1024t = _ctx_1024t * jax.lax.rsqrt(jnp.mean(jnp.square(_ctx_1024t)) + 1e-12) * 0.953939
        ctx_1024 = 4.13588e-05 + 0.999923 * (_ctx_1024t + 0.3 * jax.random.normal(jax.random.fold_in(_rk, 611), (64, 120, 128), jnp.float32))
        return (x, ctx_1024)
    x, ctx_1024 = _rec_inputs()

    def _L0_attn_setup():
        import jax, jax.numpy as jnp
        import numpy as np
        import math
        DIM = 128
        K = 3
        NUM_LAYERS = 1
        RES_SCALE = 1.0 / math.sqrt(NUM_LAYERS)

        def rmsnorm(x, gamma):
            n = jnp.sqrt(jnp.sum(x * x, axis=-1, keepdims=True))
            return x / jnp.maximum(n, 1e-12) * x.shape[-1] ** 0.5 * (gamma + 1.0)

        def causal_dwconv(x, w_dw, b_dw, w_pw, b_pw):
            xt = jnp.transpose(x, (0, 2, 1))
            xt = jnp.pad(xt, ((0, 0), (0, 0), (K - 1, 0)))
            y = jax.lax.conv_general_dilated(xt, w_dw, window_strides=(1,), padding='VALID', feature_group_count=xt.shape[1], dimension_numbers=('NCH', 'OIH', 'NCH'))
            y = y + b_dw[None, :, None]
            y = jnp.transpose(y, (0, 2, 1))
            return jnp.einsum('bld,ed->ble', y, w_pw) + b_pw

        def log_g(x):
            return jnp.where(x >= 0, jnp.log(jax.nn.relu(x) + 0.5), -jax.nn.softplus(-x))

        def heinsen_scan_log(log_coeffs, log_values):
            a_star = jnp.cumsum(log_coeffs, axis=1)
            log_h = a_star + jax.lax.cumlogsumexp(log_values - a_star, axis=1)
            return jnp.exp(log_h)

        def min_gru(x, w_hg):
            hg = jnp.einsum('bld,ed->ble', x, w_hg)
            hidden, gate = jnp.split(hg, 2, axis=-1)
            log_coeffs = -jax.nn.softplus(gate)
            log_values = -jax.nn.softplus(-gate) + log_g(hidden)
            out = heinsen_scan_log(log_coeffs, log_values)
            next_hidden = out[:, -1:]
            return (out, next_hidden)

        def _reference_tuple_inner(x, conv_dw_w, conv_dw_b, conv_pw_w, conv_pw_b, conv_norm_g, gru_norm_g, gru_w, ff_norm_g, ff_w1, ff_b1, ff_w2, ff_b2):
            x = causal_dwconv(rmsnorm(x, conv_norm_g), conv_dw_w, conv_dw_b, conv_pw_w, conv_pw_b) * RES_SCALE + x
            gru_out, next_hidden = min_gru(rmsnorm(x, gru_norm_g), gru_w)
            x = gru_out * RES_SCALE + x
            h = rmsnorm(x, ff_norm_g)
            h = jax.nn.gelu(jnp.einsum('bld,ed->ble', h, ff_w1) + ff_b1, approximate=False)
            h = jnp.einsum('ble,de->bld', h, ff_w2) + ff_b2
            x = h * RES_SCALE + x
            return (x, next_hidden)
        key = jax.random.key(seed)
        ks = jax.random.split(key, 12)
        D = DIM
        s = 0.02
        return {'x': jax.random.normal(ks[0], (4, 512, D), jnp.float32), 'conv_dw_w': jax.random.normal(ks[1], (D, 1, K), jnp.float32) * s, 'conv_dw_b': jax.random.normal(ks[2], (D,), jnp.float32) * s, 'conv_pw_w': jax.random.normal(ks[3], (D, D), jnp.float32) * s, 'conv_pw_b': jax.random.normal(ks[4], (D,), jnp.float32) * s, 'conv_norm_g': jax.random.normal(ks[5], (D,), jnp.float32) * s, 'gru_norm_g': jax.random.normal(ks[6], (D,), jnp.float32) * s, 'gru_w': jax.random.normal(ks[7], (2 * D, D), jnp.float32) * s, 'ff_norm_g': jax.random.normal(ks[8], (D,), jnp.float32) * s, 'ff_w1': jax.random.normal(ks[9], (4 * D, D), jnp.float32) * s, 'ff_b1': jax.random.normal(ks[10], (4 * D,), jnp.float32) * s, 'ff_w2': jax.random.normal(ks[11], (D, 4 * D), jnp.float32) * s, 'ff_b2': jnp.zeros((D,), jnp.float32)}
    _L0_attn_all = _L0_attn_setup()
    _L0_attn_in = {k: v for k, v in _L0_attn_all.items() if k in ('conv_dw_w', 'conv_dw_b', 'conv_pw_w', 'conv_pw_b', 'conv_norm_g', 'gru_norm_g', 'gru_w', 'ff_norm_g', 'ff_w1', 'ff_b1', 'ff_w2', 'ff_b2')}
    del _L0_attn_all

    def _L0_xattn_setup():
        import jax, jax.numpy as jnp
        import numpy as np
        NUM_HEADS = 16
        KEY_DIM = 64
        VALUE_DIM = 64
        D_MODEL = 128
        NEG_INF = -10000000000.0
        key = jax.random.key(seed)
        ks = jax.random.split(key, 8)
        B, T, S, D = (4, 256, 256, D_MODEL)
        w_scale = 1.0 / np.sqrt(D)
        inp = {'query': jax.random.normal(ks[0], (B, T, D), jnp.float32), 'key': jax.random.normal(ks[1], (B, S, D), jnp.float32), 'value': jax.random.normal(ks[2], (B, S, D), jnp.float32), 'Wq': jax.random.normal(ks[3], (D, NUM_HEADS * KEY_DIM), jnp.float32) * w_scale, 'bq': jnp.zeros((NUM_HEADS * KEY_DIM,), jnp.float32), 'Wk': jax.random.normal(ks[4], (D, NUM_HEADS * KEY_DIM), jnp.float32) * w_scale, 'bk': jnp.zeros((NUM_HEADS * KEY_DIM,), jnp.float32), 'Wv': jax.random.normal(ks[5], (D, NUM_HEADS * VALUE_DIM), jnp.float32) * w_scale, 'bv': jnp.zeros((NUM_HEADS * VALUE_DIM,), jnp.float32), 'Wo': jax.random.normal(ks[6], (NUM_HEADS * VALUE_DIM, D), jnp.float32) * w_scale, 'bo': jnp.zeros((D,), jnp.float32)}
        return inp
    _L0_xattn_all = _L0_xattn_setup()
    _L0_xattn_in = {k: v for k, v in _L0_xattn_all.items() if k in ('Wq', 'bq', 'Wk', 'bk', 'Wv', 'bv', 'Wo', 'bo')}
    del _L0_xattn_all

    def _L0_ffn_setup():
        import jax, jax.numpy as jnp
        import numpy as np
        B, S, D = (2, 256, 128)
        I = 64
        E = 16
        TOP_K = 2

        def _mlp(x, wg, wu, wd):
            return jnp.einsum('bsi,id->bsd', jax.nn.silu(x @ wg) * (x @ wu), wd)
        key = jax.random.key(seed)
        ks = jax.random.split(key, 10)
        sc_d = 1.0 / np.sqrt(D)
        sc_i = 1.0 / np.sqrt(I)
        return {'x': jax.random.normal(ks[0], (B, S, D), dtype=jnp.float32), 'gate_w': jax.random.normal(ks[1], (D, E), dtype=jnp.float32) * sc_d, 'gate_b': jnp.zeros((E,), dtype=jnp.float32), 'shared_wg': jax.random.normal(ks[2], (D, I), dtype=jnp.float32) * sc_d, 'shared_wu': jax.random.normal(ks[3], (D, I), dtype=jnp.float32) * sc_d, 'shared_wd': jax.random.normal(ks[4], (I, D), dtype=jnp.float32) * sc_i, 'experts_wg': jax.random.normal(ks[5], (E, D, I), dtype=jnp.float32) * sc_d, 'experts_wu': jax.random.normal(ks[6], (E, D, I), dtype=jnp.float32) * sc_d, 'experts_wd': jax.random.normal(ks[7], (E, I, D), dtype=jnp.float32) * sc_i}
    _L0_ffn_all = _L0_ffn_setup()
    _L0_ffn_in = {k: v for k, v in _L0_ffn_all.items() if k in ('gate_w', 'gate_b', 'shared_wg', 'shared_wu', 'shared_wd', 'experts_wg', 'experts_wu', 'experts_wd')}
    del _L0_ffn_all
    return {'x': x, 'ctx_1024': ctx_1024, 'L0_attn_conv_dw_w': _L0_attn_in['conv_dw_w'], 'L0_attn_conv_dw_b': _L0_attn_in['conv_dw_b'], 'L0_attn_conv_pw_w': _L0_attn_in['conv_pw_w'], 'L0_attn_conv_pw_b': _L0_attn_in['conv_pw_b'], 'L0_attn_conv_norm_g': _L0_attn_in['conv_norm_g'], 'L0_attn_gru_norm_g': _L0_attn_in['gru_norm_g'], 'L0_attn_gru_w': _L0_attn_in['gru_w'], 'L0_attn_ff_norm_g': _L0_attn_in['ff_norm_g'], 'L0_attn_ff_w1': _L0_attn_in['ff_w1'], 'L0_attn_ff_b1': _L0_attn_in['ff_b1'], 'L0_attn_ff_w2': _L0_attn_in['ff_w2'], 'L0_attn_ff_b2': _L0_attn_in['ff_b2'], 'L0_xattn_Wq': _L0_xattn_in['Wq'], 'L0_xattn_bq': _L0_xattn_in['bq'], 'L0_xattn_Wk': _L0_xattn_in['Wk'], 'L0_xattn_bk': _L0_xattn_in['bk'], 'L0_xattn_Wv': _L0_xattn_in['Wv'], 'L0_xattn_bv': _L0_xattn_in['bv'], 'L0_xattn_Wo': _L0_xattn_in['Wo'], 'L0_xattn_bo': _L0_xattn_in['bo'], 'L0_ffn_gate_w': _L0_ffn_in['gate_w'], 'L0_ffn_gate_b': _L0_ffn_in['gate_b'], 'L0_ffn_shared_wg': _L0_ffn_in['shared_wg'], 'L0_ffn_shared_wu': _L0_ffn_in['shared_wu'], 'L0_ffn_shared_wd': _L0_ffn_in['shared_wd'], 'L0_ffn_experts_wg': _L0_ffn_in['experts_wg'], 'L0_ffn_experts_wu': _L0_ffn_in['experts_wu'], 'L0_ffn_experts_wd': _L0_ffn_in['experts_wd']}

def reference(x, ctx_1024, L0_attn_conv_dw_w, L0_attn_conv_dw_b, L0_attn_conv_pw_w, L0_attn_conv_pw_b, L0_attn_conv_norm_g, L0_attn_gru_norm_g, L0_attn_gru_w, L0_attn_ff_norm_g, L0_attn_ff_w1, L0_attn_ff_b1, L0_attn_ff_w2, L0_attn_ff_b2, L0_xattn_Wq, L0_xattn_bq, L0_xattn_Wk, L0_xattn_bk, L0_xattn_Wv, L0_xattn_bv, L0_xattn_Wo, L0_xattn_bo, L0_ffn_gate_w, L0_ffn_gate_b, L0_ffn_shared_wg, L0_ffn_shared_wu, L0_ffn_shared_wd, L0_ffn_experts_wg, L0_ffn_experts_wu, L0_ffn_experts_wd):
    import jax
    import jax.numpy as jnp

    def _L0_attn_ref(x, conv_dw_w, conv_dw_b, conv_pw_w, conv_pw_b, conv_norm_g, gru_norm_g, gru_w, ff_norm_g, ff_w1, ff_b1, ff_w2, ff_b2):
        import jax, jax.numpy as jnp
        import numpy as np
        import math
        DIM = 128
        K = 3
        NUM_LAYERS = 1
        RES_SCALE = 1.0 / math.sqrt(NUM_LAYERS)

        def rmsnorm(x, gamma):
            n = jnp.sqrt(jnp.sum(x * x, axis=-1, keepdims=True))
            return x / jnp.maximum(n, 1e-12) * x.shape[-1] ** 0.5 * (gamma + 1.0)

        def causal_dwconv(x, w_dw, b_dw, w_pw, b_pw):
            xt = jnp.transpose(x, (0, 2, 1))
            xt = jnp.pad(xt, ((0, 0), (0, 0), (K - 1, 0)))
            y = jax.lax.conv_general_dilated(xt, w_dw, window_strides=(1,), padding='VALID', feature_group_count=xt.shape[1], dimension_numbers=('NCH', 'OIH', 'NCH'))
            y = y + b_dw[None, :, None]
            y = jnp.transpose(y, (0, 2, 1))
            return jnp.einsum('bld,ed->ble', y, w_pw) + b_pw

        def log_g(x):
            return jnp.where(x >= 0, jnp.log(jax.nn.relu(x) + 0.5), -jax.nn.softplus(-x))

        def heinsen_scan_log(log_coeffs, log_values):
            a_star = jnp.cumsum(log_coeffs, axis=1)
            log_h = a_star + jax.lax.cumlogsumexp(log_values - a_star, axis=1)
            return jnp.exp(log_h)

        def min_gru(x, w_hg):
            hg = jnp.einsum('bld,ed->ble', x, w_hg)
            hidden, gate = jnp.split(hg, 2, axis=-1)
            log_coeffs = -jax.nn.softplus(gate)
            log_values = -jax.nn.softplus(-gate) + log_g(hidden)
            out = heinsen_scan_log(log_coeffs, log_values)
            next_hidden = out[:, -1:]
            return (out, next_hidden)

        def _reference_tuple_inner(x, conv_dw_w, conv_dw_b, conv_pw_w, conv_pw_b, conv_norm_g, gru_norm_g, gru_w, ff_norm_g, ff_w1, ff_b1, ff_w2, ff_b2):
            x = causal_dwconv(rmsnorm(x, conv_norm_g), conv_dw_w, conv_dw_b, conv_pw_w, conv_pw_b) * RES_SCALE + x
            gru_out, next_hidden = min_gru(rmsnorm(x, gru_norm_g), gru_w)
            x = gru_out * RES_SCALE + x
            h = rmsnorm(x, ff_norm_g)
            h = jax.nn.gelu(jnp.einsum('bld,ed->ble', h, ff_w1) + ff_b1, approximate=False)
            h = jnp.einsum('ble,de->bld', h, ff_w2) + ff_b2
            x = h * RES_SCALE + x
            return (x, next_hidden)
        return _reference_tuple_inner(x, conv_dw_w, conv_dw_b, conv_pw_w, conv_pw_b, conv_norm_g, gru_norm_g, gru_w, ff_norm_g, ff_w1, ff_b1, ff_w2, ff_b2)[0]

    def _L0_xattn_ref(query, key, value, Wq, bq, Wk, bk, Wv, bv, Wo, bo):
        import jax, jax.numpy as jnp
        import numpy as np
        NUM_HEADS = 16
        KEY_DIM = 64
        VALUE_DIM = 64
        D_MODEL = 128
        NEG_INF = -10000000000.0
        B, T, _ = query.shape
        S = key.shape[1]
        H, Dk, Dv = (NUM_HEADS, KEY_DIM, VALUE_DIM)
        q = (query @ Wq + bq).reshape(B, T, H, Dk)
        k = (key @ Wk + bk).reshape(B, S, H, Dk)
        v = (value @ Wv + bv).reshape(B, S, H, Dv)
        q = q * (1.0 / jnp.sqrt(jnp.asarray(Dk, q.dtype)))
        scores = jnp.einsum('bthd,bshd->bhts', q, k)
        causal = jnp.tril(jnp.ones((T, S), scores.dtype))
        scores = scores + NEG_INF * (1.0 - causal)
        attn = jax.nn.softmax(scores, axis=-1)
        ctx = jnp.einsum('bhts,bshd->bthd', attn, v).reshape(B, T, H * Dv)
        out = ctx @ Wo + bo
        return out

    def _L0_ffn_ref(x, gate_w, gate_b, shared_wg, shared_wu, shared_wd, experts_wg, experts_wu, experts_wd):
        import jax, jax.numpy as jnp
        import numpy as np
        B, S, D = (2, 256, 128)
        I = 64
        E = 16
        TOP_K = 2

        def _mlp(x, wg, wu, wd):
            return jnp.einsum('bsi,id->bsd', jax.nn.silu(x @ wg) * (x @ wu), wd)
        router_logits = jax.nn.sigmoid(x @ gate_w + gate_b)
        expert_values, expert_indices = jax.lax.top_k(router_logits, k=TOP_K)
        expert_values = expert_values / jnp.sum(expert_values, axis=-1, keepdims=True)
        hg = jnp.einsum('bsd,edi->bsei', x, experts_wg)
        hu = jnp.einsum('bsd,edi->bsei', x, experts_wu)
        all_outputs = jnp.einsum('bsei,eid->bsed', jax.nn.silu(hg) * hu, experts_wd)
        selected = jnp.take_along_axis(all_outputs, expert_indices[..., None], axis=2)
        expert_weighted = jnp.sum(expert_values[..., None] * selected, axis=2)
        return x + _mlp(x, shared_wg, shared_wu, shared_wd) + expert_weighted
    x = _layernorm(x + _L0_attn_ref(x, L0_attn_conv_dw_w, L0_attn_conv_dw_b, L0_attn_conv_pw_w, L0_attn_conv_pw_b, L0_attn_conv_norm_g, L0_attn_gru_norm_g, L0_attn_gru_w, L0_attn_ff_norm_g, L0_attn_ff_w1, L0_attn_ff_b1, L0_attn_ff_w2, L0_attn_ff_b2), axis=-1)
    x = _layernorm(x + _L0_xattn_ref(x, ctx_1024, ctx_1024, L0_xattn_Wq, L0_xattn_bq, L0_xattn_Wk, L0_xattn_bk, L0_xattn_Wv, L0_xattn_bv, L0_xattn_Wo, L0_xattn_bo), axis=-1)
    x = _layernorm(x + _L0_ffn_ref(x, L0_ffn_gate_w, L0_ffn_gate_b, L0_ffn_shared_wg, L0_ffn_shared_wu, L0_ffn_shared_wd, L0_ffn_experts_wg, L0_ffn_experts_wu, L0_ffn_experts_wd), axis=-1)
    return x

_drawn_inputs = setup_inputs


def setup_inputs(seed=0):
    import zlib

    import numpy as np

    out = dict(_drawn_inputs(seed))
    spreads = {'L0_attn_ff_b2': (0.0, 0.1),
     'L0_xattn_bq': (0.0, 0.1),
     'L0_xattn_bk': (0.0, 2.0),
     'L0_xattn_bv': (0.0, 0.1),
     'L0_xattn_bo': (0.0, 0.1),
     'L0_ffn_gate_b': (0.0, 0.1)}
    factors = {'L0_attn_conv_dw_w': 6.132,
     'L0_attn_conv_dw_b': 7.162,
     'L0_attn_conv_pw_w': 5.995,
     'L0_attn_conv_pw_b': 3.388,
     'L0_attn_conv_norm_g': 8.0,
     'L0_attn_gru_norm_g': 29.802,
     'L0_attn_ff_norm_g': 41.726,
     'L0_attn_ff_b1': 7.435}
    for name, (base, spread) in spreads.items():
        noise = np.random.default_rng([zlib.crc32(name.encode()), seed]).standard_normal(out[name].shape)
        drawn = base * np.exp(spread * noise) if base else spread * noise
        out[name] = jnp.asarray(drawn.astype(out[name].dtype))
    for name, factor in factors.items():
        out[name] = (out[name] * factor).astype(out[name].dtype)
    return out
```

```python
from contextlib import ExitStack

import concourse.bass as bass
from concourse import mybir

ALU = mybir.AluOpType
ACT = mybir.ActivationFunctionType
F32 = mybir.dt.float32
BF16 = mybir.dt.bfloat16
U32 = mybir.dt.uint32
AX_X = mybir.AxisListType.X

P = 128
T = 128
NSEQ = 64
SEQ = 4
G = NSEQ // SEQ
S = 120
H = 16
DK = 64
NCH = H * DK // P
E = 16
I = 64
F = 512
FCH = F // P
W = SEQ * T
SW = SEQ * S
PAIRS = 2 * SEQ
RS = E + 2 * I

COLS = ["dw0", "dw1", "dw2", "dwb", "g_conv", "g_gru", "g_ff"] + [f"b1_{c}" for c in range(FCH)] + \
    [f"bq{j}" for j in range(NCH)] + [f"bk{j}" for j in range(NCH)] + [f"bv{j}" for j in range(NCH)]
ROWS = 3 * P + E

PER_GROUP = {
    "x_loaded": 16, "ctx_loaded": 16, "out0_stored": 16, "out1_stored": 16, "out2_stored": 16, "out3_stored": 16,
    "squares": 3, "sums": 3, "floored": 3, "rms": 3, "normed": 3, "x_bpw": 1, "x_bff": 1, "x_all": 1,
    "a_bank": 13, "normT": 3, "conv2": 1, "conv1": 1, "conv0": 1, "mixed": 1,
    "gate_tanh": 1, "hid_tanh": 1, "keep": 1, "keep0": 1, "inp": 1, "sig": 1, "cand": 1, "drive": 1, "scan": 1,
    "gru_sum": 1, "gelu": 4, "mixer": 1,
    "ln1_stats": 4, "ln1_mv": 4, "ln1_eps": 1, "ln1_rstd": 1, "ln1_out": 4, "x1T": 1, "x1_bo": 1,
    "proj": 24, "proj_act": 12, "proj_dve": 12, "scores": 16, "negmax": 16, "probs": 16,
    "probsT": 16, "probsT_sb": 16, "rinv": 16, "normal": 16, "pv": 8, "headsT_sb": 8,
    "wo": 4, "attn_sum": 4, "ln2_stats": 4, "ln2_mv": 4, "ln2_eps": 4, "ln2_rstd": 4, "ln2_out": 4,
    "x2T": 1, "x2T_sb": 1, "rs": 2, "logits": 2, "route_tanh": 1, "route_sig": 1, "top": 4, "top_at": 4,
    "top_f": 1, "top_sum": 1, "top_rec": 1, "top_w": 1, "one0": 1, "one1": 1, "w0": 1, "w1": 1, "gates": 1,
    "sh_tanh": 2, "sh_gate": 2, "sh_act": 2, "shT": 1, "shT_sb": 1,
    "eg": 8, "eu": 8, "e_tanh": 8, "e_gate": 8, "e_act": 8, "e_weighted": 8, "eT": 8, "eT_sb": 8,
    "down": 4, "moe_sum": 4, "ln3_stats": 4, "ln3_mv": 4, "ln3_eps": 4, "ln3_rstd": 4, "ln3_out": 4,
}
ONCE = ["waits_held", "weights", "ident", "identb", "mask0", "mask", "iota", "iotaf", "ones", "gammas", "bq8", "powers", "pads"]

A_USE = {n: k for k, n in enumerate(
    ["T0", "pw", "T1", "gate", "hid", "Th", "T2"] + [f"up{k}" for k in range(FCH)] + ["ff2", "Tx1"])}


def layer_kernel(nc, x, ctxT, w_pw, w_gru, w_ff1, w_ff2, cols, rows, w_q, w_k, w_v, w_o, w_g, w_u, w_rs, w_d, w_sd, out):
    with ExitStack() as ctx:
        def sb(name, shape, dt=F32):
            return ctx.enter_context(nc.sbuf_tensor(name, shape, dt))

        sem = {n: ctx.enter_context(nc.semaphore(n)) for n in [*PER_GROUP, *ONCE]}

        def later(g):
            return not (isinstance(g, int) and g == 0)

        def upto(name, g, k=0):
            return g * PER_GROUP[name] + (k + 1) * (16 if name.endswith(("loaded", "stored")) else 1)

        def whole(name, g):
            return g * PER_GROUP[name] + PER_GROUP[name]

        def settle(eng):
            eng.sem_inc(sem["waits_held"], 1)

        pw = sb("pw", [P, P]); gru = sb("gru", [P, 2 * P]); ff1 = sb("ff1", [P, F]); ff2 = sb("ff2", [P, FCH, P])
        wq = sb("wq", [P, H * DK]); wk = sb("wk", [P, H * DK]); wv = sb("wv", [P, H * DK]); wo = sb("wo", [P, NCH, P])
        wg = sb("wg", [P, E * I]); wu = sb("wu", [P, E * I]); wrs = sb("wrs", [P, RS])
        wd = sb("wd", [P, E // 2, P]); wsd = sb("wsd", [I, P])
        col = sb("col", [P, len(COLS)]); row = sb("row", [P, ROWS])
        ident = sb("ident_f", [P, P]); identb = sb("ident_b", [P, P], BF16); maskb = sb("mask_b", [P, S], BF16)
        iota_i = sb("iota_i", [P, E], mybir.dt.int32); iota = sb("iota_f", [P, E])
        power = sb("power", [P, SEQ])

        eps = sb("eps", [P, SEQ])
        xt = sb("xt", [P, SEQ, P]); sq = sb("sq", [P, SEQ, P]); ss = sb("ss", [P, SEQ]); ssf = sb("ssf", [P, SEQ])
        rr = sb("rr", [P, SEQ]); xn = sb("xn", [P, SEQ, P]); xb = sb("xb", [P, SEQ, P]); xf = sb("xf", [P, SEQ, P])
        xc = sb("xc", [P, SEQ, T + 2])
        cv2 = sb("cv2", [P, SEQ, T]); cv1 = sb("cv1", [P, SEQ, T]); cv = sb("cv", [P, SEQ, T])
        xm = sb("xm", [P, SEQ, P]); nT = sb("nT", [P, W])
        tg = sb("tg", [P, W]); th = sb("th", [P, W]); keep = sb("keep_sb", [P, SEQ, T]); inp = sb("inp_sb", [P, W])
        sg = sb("sg", [P, W]); cand = sb("cand_sb", [P, W]); drive = sb("drive_sb", [P, W]); hs = sb("hs", [P, W])
        xg = sb("xg", [P, SEQ, P]); xz = sb("xz", [P, SEQ, P]); hf = sb("hf", [P, FCH, W]); xr = sb("xr", [P, SEQ, P])
        st1 = sb("st1", [P, SEQ, 6]); mv1 = sb("mv1", [P, SEQ, 2]); ve1 = sb("ve1", [P, SEQ]); rs1 = sb("rs1", [P, SEQ])
        x1 = sb("x1", [P, SEQ, P]); x1T = sb("x1T_s", [P, W]); x1b = sb("x1b", [P, SEQ, P])
        cT = sb("cT", [P, SW]); vv = sb("vv", [S, SEQ, H * DK]); kT = sb("kT", [P, NCH, SW]); qT = sb("qT", [P, NCH, W])
        nm = sb("nm", [P, 2, 2, 4]); pr = sb("pr", [P, 2, 2, 4, S]); rsum = sb("rsum", [P, 2, 2, 4, 1])
        pT = sb("pT", [S, 8, T]); ri = sb("ri", [P, 2, 2, 4, 1]); hT = sb("hT", [P, NCH, T])
        xa = sb("xa", [P, P]); st2 = sb("st2", [P, 6]); mv2 = sb("mv2", [P, 2]); ve2 = sb("ve2", [P, 1]); rs2 = sb("rs2", [P, 1])
        x2 = sb("x2", [P, SEQ, P])
        x2T = sb("x2T_s", [P, W]); lg = sb("lg", [P, SEQ, E]); rt = sb("rt", [P, SEQ, E]); sg8 = sb("sg8", [P, SEQ, E])
        mx = sb("mx", [P, SEQ, 8]); mi = sb("mi", [P, SEQ, 8], U32); mf = sb("mf", [P, SEQ, 2])
        tsum = sb("tsum", [P, SEQ, 1]); trec = sb("trec", [P, SEQ, 1]); tw = sb("tw", [P, SEQ, 2])
        o0 = sb("o0", [P, SEQ, E]); o1 = sb("o1", [P, SEQ, E]); q0 = sb("q0", [P, SEQ, E]); q1 = sb("q1", [P, SEQ, E])
        gw = sb("gw", [P, SEQ, E])
        tsh = sb("tsh", [P, SEQ, I]); gsh = sb("gsh", [P, SEQ, I]); ash = sb("ash", [P, SEQ, I]); sT = sb("sT", [I, W])
        et = sb("et", [P, 512]); e1 = sb("e1", [P, 512]); e3 = sb("e3", [P, 2, 512]); ew = sb("ew", [P, E * I])
        eT = sb("eT_s", [P, E // 2, T]); ys = sb("ys", [P, P])
        st3 = sb("st3", [P, 6]); mv3 = sb("mv3", [P, 2]); ve3 = sb("ve3", [P, 1]); rs3 = sb("rs3", [P, 1])
        y = sb("y", [P, SEQ, P])

        def bank(name):
            return ctx.enter_context(nc.psum_tensor(name, [P, 512], F32))

        sE, sO, t0, t1, pvb = bank("sE"), bank("sO"), bank("t0"), bank("t1"), bank("pvb")
        m0, m1 = bank("m0"), bank("m1")
        ma = bank("ma")
        proj_banks = [sE, sO, t0, t1, pvb]
        score_banks = [sE, sO]

        def seqs(ap, n=SEQ):
            return ap.rearrange("p (b n) -> p b n", b=n)

        def c_(name, n=1):
            k = COLS.index(name)
            return col[:, k:k + n]

        brow = {"pw": row[:, 0:P], "ff2": row[:, P:2 * P], "bo": row[:, 2 * P:3 * P], "gate": row[:, 3 * P:3 * P + E]}

        def over_seqs(ap):
            return ap.unsqueeze(1).to_broadcast([P, SEQ, ap.shape[1]])

        weight_loads = [(pw[:], w_pw), (gru[:], w_gru), (ff1[:], w_ff1), (ff2[:], w_ff2), (wq[:], w_q), (wk[:], w_k),
                        (wv[:], w_v), (wo[:], w_o), (wg[:], w_g), (wu[:], w_u), (wrs[:], w_rs), (wd[:], w_d),
                        (wsd[:], w_sd), (col[:], cols), (row[:], rows.to_broadcast([P, ROWS]))]
        NWL = len(weight_loads)
        WEIGHTS = 16 * NWL

        block = ctx.enter_context(nc.Block())

        def pipeline(eng, body):
            body(0, None, None)
            body(1, 0, None)
            body(2, 1, 0)
            with eng.Fori(2, G - 1) as i:
                body(i + 1, i, i - 1)
            body(None, G - 1, G - 2)
            body(None, None, G - 1)

        @block.sync
        def _(sp):
            for dst, src in weight_loads:
                sp.dma_start(dst, src).then_inc(sem["weights"], 16)

            def body(a, b, c):
                if a is not None:
                    for n in ("squares", "normed", "x_bpw", "x_bff"):
                        if later(a):
                            sp.wait_ge(sem[n], upto(n, a - 1, 0))
                        settle(sp)
                    sp.dma_start(xt[:], x[bass.ds(a * SEQ, SEQ)].rearrange("b t d -> t b d")).then_inc(sem["x_loaded"], 16)
                    if later(a):
                        sp.wait_ge(sem["proj"], upto("proj", a - 1, 15))
                    settle(sp)
                    sp.dma_start(cT[:], ctxT[bass.ds(a, 1)].rearrange("o d s -> d (o s)")).then_inc(sem["ctx_loaded"], 16)
                if c is not None:
                    for q in range(SEQ):
                        sp.wait_ge(sem["ln3_out"], upto("ln3_out", c, q))
                        settle(sp)
                        sp.dma_start(out[bass.ds(c * SEQ + q, 1)].rearrange("b t d -> (b t) d"),
                                     y[:, q, :]).then_inc(sem[f"out{q}_stored"], 16)

            pipeline(sp, body)
            for q in range(SEQ):
                if later(G):
                    sp.wait_ge(sem[f"out{q}_stored"], whole(f"out{q}_stored", G - 1))

        @block.tensor
        def _(pe):
            mm = nc.tensor.matmul
            pe.wait_ge(sem["weights"], WEIGHTS)
            pe.wait_ge(sem["ident"], 1)
            pe.wait_ge(sem["identb"], 1)
            pe.wait_ge(sem["mask"], 1)

            def turn(dst, src):
                return nc.tensor.transpose(dst, src, ident[0:src.shape[0], 0:src.shape[0]])

            def a_norm_T(a, n):
                pe.wait_ge(sem["normed"], upto("normed", a, n))
                if n == 0:
                    if later(a):
                        pe.wait_ge(sem["x1T"], whole("x1T", a - 1))
                elif n == 1:
                    pe.wait_ge(sem["mixed"], upto("mixed", a))
                else:
                    pe.wait_ge(sem["gru_sum"], upto("gru_sum", a))
                for q in range(SEQ):
                    ins = turn(ma[:, q * P:(q + 1) * P], xn[:, q, :])
                ins.then_inc(sem["a_bank"], 1)

            def a_pw(a):
                pe.wait_ge(sem["conv0"], upto("conv0", a))
                pe.wait_ge(sem["normT"], upto("normT", a, 0))
                for q in range(SEQ):
                    ins = mm(ma[:, q * P:(q + 1) * P], cv[:, q, :], pw[:], start=True, stop=True)
                ins.then_inc(sem["a_bank"], 1)

            def a_gate(a):
                pe.wait_ge(sem["normT"], upto("normT", a, 1))
                mm(ma[:], gru[:, P:2 * P], nT[:], start=True, stop=True).then_inc(sem["a_bank"], 1)

            def a_hid(a):
                pe.wait_ge(sem["gate_tanh"], upto("gate_tanh", a))
                mm(ma[:], gru[:, 0:P], nT[:], start=True, stop=True).then_inc(sem["a_bank"], 1)

            def a_scan_T(a):
                pe.wait_ge(sem["scan"], upto("scan", a))
                pe.wait_ge(sem["hid_tanh"], upto("hid_tanh", a))
                for q in range(SEQ):
                    ins = turn(ma[:, q * P:(q + 1) * P], hs[:, q * T:(q + 1) * T])
                ins.then_inc(sem["a_bank"], 1)

            def a_ff1(a, f):
                if f == 0:
                    pe.wait_ge(sem["normT"], upto("normT", a, 2))
                else:
                    pe.wait_ge(sem["gelu"], upto("gelu", a, f - 1))
                mm(ma[:], ff1[:, f * P:(f + 1) * P], nT[:], start=True, stop=True).then_inc(sem["a_bank"], 1)

            def a_ff2(a):
                pe.wait_ge(sem["gelu"], whole("gelu", a))
                for q in range(SEQ):
                    for f in range(FCH):
                        ins = mm(ma[:, q * P:(q + 1) * P], hf[:, f, q * T:(q + 1) * T], ff2[:, f, :],
                                 start=(f == 0), stop=(f == FCH - 1))
                ins.then_inc(sem["a_bank"], 1)

            def a_x1_T(a):
                pe.wait_ge(sem["ln1_out"], whole("ln1_out", a))
                for q in range(SEQ):
                    ins = turn(ma[:, q * P:(q + 1) * P], x1[:, q, :])
                ins.then_inc(sem["a_bank"], 1)

            def proj_free(b, n):
                if n >= 5:
                    other = "proj_dve" if (n - 5) % 2 else "proj_act"
                    pe.wait_ge(sem[other], upto(other, b, (n - 5) // 2))
                elif n < 2:
                    if later(b):
                        pe.wait_ge(sem["probs"], upto("probs", b - 1, 14 + n))
                elif n < 4:
                    if later(b):
                        pe.wait_ge(sem["probsT_sb"], upto("probsT_sb", b - 1, 14 + n - 2))
                else:
                    if later(b):
                        pe.wait_ge(sem["attn_sum"], whole("attn_sum", b - 1))

            def b_project(b, lo, hi):
                for n in range(lo, hi):
                    proj_free(b, n)
                    dst = proj_banks[n % 5]
                    if n < 8:
                        q, half = n // 2, (n % 2) * 512
                        if n == 0:
                            pe.wait_ge(sem["ctx_loaded"], whole("ctx_loaded", b))
                        ins = mm(dst[0:S, :], cT[:, q * S:(q + 1) * S], wv[:, half:half + 512], start=True, stop=True)
                    elif n < 16:
                        j = n - 8
                        ins = mm(dst[:, 0:SW], wk[:, j * P:(j + 1) * P], cT[:], start=True, stop=True)
                    else:
                        j = n - 16
                        if j == 0:
                            pe.wait_ge(sem["x1T"], whole("x1T", b))
                        ins = mm(dst[:], wq[:, j * P:(j + 1) * P], x1T[:], start=True, stop=True)
                    ins.then_inc(sem["proj"], 1)

            def b_scores(b, p):
                q, half = p // 2, p % 2
                if p == 0:
                    pe.wait_ge(sem["proj_act"], whole("proj_act", b))
                    pe.wait_ge(sem["proj_dve"], whole("proj_dve", b))
                else:
                    pe.wait_ge(sem["probs"], upto("probs", b, 2 * p - 1))
                for r in range(2):
                    mm(score_banks[r][:, 0:4 * S], identb[:], maskb[:].unsqueeze(1).to_broadcast([P, 4, S]),
                       start=True, stop=False, skip_group_check=True)
                for i in range(4):
                    j = 4 * half + i
                    for r in range(2):
                        ins = mm(score_banks[r][:, i * S:(i + 1) * S], qT[r * DK:(r + 1) * DK, j, q * T:(q + 1) * T],
                                 kT[r * DK:(r + 1) * DK, j, q * S:(q + 1) * S], start=False, stop=True,
                                 skip_group_check=True)
                        if i == 3:
                            ins.then_inc(sem["scores"], 1)

            def b_probs_T(b, p):
                for r in range(2):
                    if p:
                        pe.wait_ge(sem["probsT_sb"], upto("probsT_sb", b, 2 * p - 2 + r))
                    pe.wait_ge(sem["normal"], upto("normal", b, 2 * p + r))
                    for i in range(4):
                        ins = turn((t0, t1)[r][0:S, i * T:(i + 1) * T], pr[:, p % 2, r, i, :])
                    ins.then_inc(sem["probsT"], 1)

            def b_pv(b, p):
                q, half = p // 2, p % 2
                pe.wait_ge(sem["probsT_sb"], upto("probsT_sb", b, 2 * p + 1))
                if half:
                    pe.wait_ge(sem["headsT_sb"], upto("headsT_sb", b, p - 1))
                elif p:
                    pe.wait_ge(sem["attn_sum"], upto("attn_sum", b, q - 1))
                for k in range(8):
                    h, r = 8 * half + k, k % 2
                    ins = mm(pvb[r * DK:(r + 1) * DK, (k // 2) * T:(k // 2 + 1) * T], vv[:, q, h * DK:(h + 1) * DK],
                             pT[:, 4 * r + k // 2, :], start=True, stop=True)
                ins.then_inc(sem["pv"], 1)

            def b_wo(b, q):
                pe.wait_ge(sem["headsT_sb"], upto("headsT_sb", b, 2 * q + 1))
                for j in range(NCH):
                    ins = mm(pvb[:, 0:P], hT[:, j, :], wo[:, j, :], start=(j == 0), stop=(j == NCH - 1))
                ins.then_inc(sem["wo"], 1)

            def c_x2_T(c):
                pe.wait_ge(sem["ln2_out"], whole("ln2_out", c))
                if later(c):
                    pe.wait_ge(sem["eT_sb"], upto("eT_sb", c - 1, 6))
                for q in range(SEQ):
                    ins = turn(m0[:, q * T:(q + 1) * T], x2[:, q, :])
                ins.then_inc(sem["x2T"], 1)

            def c_router_shared(c):
                pe.wait_ge(sem["x2T_sb"], upto("x2T_sb", c))
                if later(c):
                    pe.wait_ge(sem["moe_sum"], whole("moe_sum", c - 1))
                for k, dst in enumerate((m1, m0)):
                    for q in (2 * k, 2 * k + 1):
                        ins = mm(dst[:, (q % 2) * RS:(q % 2 + 1) * RS], x2T[:, q * T:(q + 1) * T], wrs[:], start=True, stop=True)
                    ins.then_inc(sem["rs"], 1)

            def c_shared_T(c):
                pe.wait_ge(sem["sh_act"], upto("sh_act", c, 1))
                settle(pe)
                for q in range(SEQ):
                    ins = turn(m1[0:I, q * T:(q + 1) * T], ash[:, q, :])
                ins.then_inc(sem["shT"], 1)

            def c_up(c, n):
                q, half = n // 2, (n % 2) * 512
                if n == 0:
                    pe.wait_ge(sem["shT_sb"], upto("shT_sb", c))
                elif n % 2:
                    pe.wait_ge(sem["e_act"], upto("e_act", c, n - 1))
                else:
                    pe.wait_ge(sem["eT_sb"], upto("eT_sb", c, n - 2))
                    pe.wait_ge(sem["moe_sum"], upto("moe_sum", c, q - 1))
                mm(m0[:], x2T[:, q * T:(q + 1) * T], wg[:, half:half + 512], start=True, stop=True).then_inc(sem["eg"], 1)
                mm(m1[:], x2T[:, q * T:(q + 1) * T], wu[:, half:half + 512], start=True, stop=True).then_inc(sem["eu"], 1)

            def c_act_T(c, q):
                pe.wait_ge(sem["e_weighted"], upto("e_weighted", c, 2 * q + 1))
                for j in range(E // 2):
                    ins = turn((m0, m1)[j // 4][:, (j % 4) * T:(j % 4 + 1) * T], ew[:, j * P:(j + 1) * P])
                    if j % 4 == 3:
                        ins.then_inc(sem["eT"], 1)

            def c_down(c, q):
                pe.wait_ge(sem["eT_sb"], upto("eT_sb", c, 2 * q + 1))
                for j in range(E // 2):
                    mm(m1[:, 0:P], eT[:, j, :], wd[:, j, :], start=(j == 0), stop=False)
                mm(m1[:, 0:P], sT[:, q * T:(q + 1) * T], wsd[:], start=False, stop=True).then_inc(sem["down"], 1)

            def body(a, b, c):
                A, B, C = a is not None, b is not None, c is not None
                if B:
                    b_project(b, 0, 4)
                if C:
                    c_x2_T(c)
                if B:
                    b_project(b, 4, 8)
                if C:
                    c_router_shared(c)
                if B:
                    b_project(b, 8, 10)
                    a_x1_T(b)
                    b_project(b, 10, 20)
                if C:
                    c_shared_T(c)
                if B:
                    b_project(b, 20, 24)
                for s in range(PAIRS + 1):
                    q = s // 2 - 1
                    even = s and s % 2 == 0
                    if C:
                        if even:
                            c_act_T(c, q)
                        else:
                            c_up(c, s)
                    if B and s > 1:
                        b_probs_T(b, s - 1)
                    if B and s < PAIRS:
                        b_scores(b, s)
                    if B and s == 1:
                        b_probs_T(b, 0)
                        if A:
                            a_pw(a)
                    if B and s:
                        b_pv(b, s - 1)
                    if C and even:
                        c_down(c, q)
                        if s < PAIRS:
                            c_up(c, s)
                    if A:
                        if s == 0:
                            a_norm_T(a, 0)
                        elif s == 1 and not B:
                            a_pw(a)
                        elif s == 3:
                            a_norm_T(a, 1)
                        elif s == 4:
                            a_gate(a)
                        elif s == 6:
                            a_norm_T(a, 2)
                    if B and even:
                        b_wo(b, q)
                    if A:
                        if s == 4:
                            a_hid(a)
                        elif s == 5:
                            a_scan_T(a)
                        elif s == 7:
                            for f in range(FCH):
                                a_ff1(a, f)
                        elif s == PAIRS:
                            a_ff2(a)

            pipeline(pe, body)

        @block.scalar
        def _(act):
            f = nc.scalar.activation
            act.wait_ge(sem["gammas"], 1)
            act.wait_ge(sem["bq8"], 1)

            def a_norm(a, n):
                act.wait_ge(sem["a_bank"], upto("a_bank", a, A_USE[f'T{n}']))
                gamma = c_(("g_conv", "g_gru", "g_ff")[n])
                if n == 0:
                    if later(a):
                        act.wait_ge(sem["conv0"], upto("conv0", a - 1))
                    dst = xc[:, :, 2:T + 2]
                else:
                    if n == 1:
                        if later(a):
                            act.wait_ge(sem["a_bank"], upto("a_bank", a - 1, A_USE['up3']))
                    else:
                        act.wait_ge(sem["a_bank"], upto("a_bank", a, A_USE['hid']))
                    dst = seqs(nT[:])
                f(dst, seqs(ma[:]), ACT.Identity, scale=gamma).then_inc(sem["normT"], 1)

            def a_gate(a):
                act.wait_ge(sem["a_bank"], upto("a_bank", a, A_USE['gate']))
                if later(a):
                    act.wait_ge(sem["inp"], upto("inp", a - 1))
                f(tg[:], ma[:], ACT.Tanh, scale=0.5).then_inc(sem["gate_tanh"], 1)

            def a_hid(a):
                act.wait_ge(sem["a_bank"], upto("a_bank", a, A_USE['hid']))
                if later(a):
                    act.wait_ge(sem["sig"], upto("sig", a - 1))
                f(th[:], ma[:], ACT.Tanh, scale=0.5).then_inc(sem["hid_tanh"], 1)

            def a_gelu(a, k):
                act.wait_ge(sem["a_bank"], upto("a_bank", a, A_USE[f'up{k}']))
                if k == 0:
                    if later(a):
                        act.wait_ge(sem["a_bank"], upto("a_bank", a - 1, A_USE['ff2']))
                f(hf[:, k, :], ma[:], ACT.Gelu, bias=c_(f"b1_{k}")).then_inc(sem["gelu"], 1)

            def a_x1T(a):
                act.wait_ge(sem["a_bank"], upto("a_bank", a, A_USE['Tx1']))
                if later(a):
                    act.wait_ge(sem["proj"], whole("proj", a - 1))
                f(x1T[:], ma[:], ACT.Copy).then_inc(sem["x1T"], 1)

            def b_project(b, lo, hi):
                for n in range(lo, hi):
                    if n % 2:
                        continue
                    act.wait_ge(sem["proj"], upto("proj", b, n))
                    src = proj_banks[n % 5]
                    if n < 8:
                        if n == 0:
                            if later(b):
                                act.wait_ge(sem["pv"], whole("pv", b - 1))
                        ins = f(vv[:, n // 2, 0:512], src[0:S, :], ACT.Copy)
                    elif n < 16:
                        if n == 8:
                            if later(b):
                                act.wait_ge(sem["scores"], whole("scores", b - 1))
                        ins = f(kT[:, n - 8, :], src[:, 0:SW], ACT.Identity, bias=c_(f"bk{n - 8}"))
                    else:
                        ins = f(qT[:, n - 16, :], src[:], ACT.Identity, bias=c_(f"bq{n - 16}"), scale=DK ** -0.5)
                    ins.then_inc(sem["proj_act"], 1)

            def b_probs(b, p):
                if p >= 2:
                    act.wait_ge(sem["probsT"], upto("probsT", b, 2 * (p - 2) + 1))
                else:
                    if later(b):
                        act.wait_ge(sem["probsT"], upto("probsT", b - 1, 2 * (p + PAIRS - 2) + 1))
                for r in range(2):
                    act.wait_ge(sem["negmax"], upto("negmax", b, 2 * p + r))
                    for i in range(4):
                        ins = f(pr[:, p % 2, r, i, :], score_banks[r][:, i * S:(i + 1) * S], ACT.Exp,
                                bias=nm[:, p % 2, r, i:i + 1], accum_out=rsum[:, p % 2, r, i, :])
                    ins.then_inc(sem["probs"], 1)

            def c_x2T(c):
                act.wait_ge(sem["x2T"], upto("x2T", c))
                if later(c):
                    act.wait_ge(sem["eu"], whole("eu", c - 1))
                f(x2T[:], m0[:], ACT.Copy).then_inc(sem["x2T_sb"], 1)

            def c_router(c):
                act.wait_ge(sem["logits"], upto("logits", c, 1))
                f(rt[:], lg[:], ACT.Tanh, scale=0.5).then_inc(sem["route_tanh"], 1)

            def c_shared(c):
                for k, src in enumerate((m1, m0)):
                    act.wait_ge(sem["rs"], upto("rs", c, k))
                    if k == 0:
                        if later(c):
                            act.wait_ge(sem["sh_gate"], upto("sh_gate", c - 1, 1))
                    v = seqs(src[:, 0:2 * RS], 2)[:, :, E:E + I]
                    f(tsh[:, 2 * k:2 * k + 2, :], v, ACT.Tanh, scale=0.5).then_inc(sem["sh_tanh"], 1)

            def c_sharedT(c):
                act.wait_ge(sem["shT"], upto("shT", c))
                if later(c):
                    act.wait_ge(sem["down"], whole("down", c - 1))
                f(sT[:], m1[0:I, :], ACT.Copy).then_inc(sem["shT_sb"], 1)

            def c_tanh(c, n):
                act.wait_ge(sem["eg"], upto("eg", c, n))
                if n:
                    act.wait_ge(sem["e_gate"], upto("e_gate", c, n - 1))
                f(et[:], m0[:], ACT.Tanh, scale=0.5).then_inc(sem["e_tanh"], 1)

            def c_actT(c, q):
                if q:
                    act.wait_ge(sem["down"], upto("down", c, q - 1))
                for k, src in enumerate((m0, m1)):
                    act.wait_ge(sem["eT"], upto("eT", c, 2 * q + k))
                    f(eT[:, 4 * k:4 * k + 4, :], seqs(src[:]), ACT.Copy).then_inc(sem["eT_sb"], 1)

            def body(a, b, c):
                A, B, C = a is not None, b is not None, c is not None
                if B:
                    b_project(b, 0, 4)
                if C:
                    c_x2T(c)
                if B:
                    b_project(b, 4, 8)
                if C:
                    c_shared(c)
                    c_router(c)
                if B:
                    b_project(b, 8, 10)
                    a_x1T(b)
                    b_project(b, 10, 20)
                if C:
                    c_sharedT(c)
                if B:
                    b_project(b, 20, 24)
                for s in range(PAIRS + 1):
                    q = s // 2 - 1
                    even = s and s % 2 == 0
                    if C:
                        if even:
                            c_actT(c, q)
                        else:
                            c_tanh(c, s)
                    if B and s < PAIRS:
                        b_probs(b, s)
                    if C and even and s < PAIRS:
                        c_tanh(c, s)
                    if A:
                        if s in (0, 3, 6):
                            a_norm(a, s // 3)
                        elif s == 4:
                            a_gate(a)
                            a_hid(a)
                        elif s == 7:
                            for k in range(FCH):
                                a_gelu(a, k)

            pipeline(act, body)

        @block.vector
        def _(dve):
            V = nc.vector

            dve.wait_ge(sem["weights"], WEIGHTS)
            V.memset(xc[:], 0.0).then_inc(sem["pads"], 1)
            dve.wait_ge(sem["pads"], 1)
            V.memset(eps[:], 1e-5).then_inc(sem["powers"], 1)
            V.memset(power[:], -0.5).then_inc(sem["powers"], 1)
            V.tensor_scalar(c_("g_conv", 3), c_("g_conv", 3), 1.0, None, ALU.add).then_inc(sem["gammas"], 1)
            dve.wait_ge(sem["gammas"], 1)
            V.tensor_scalar(c_("bq0", NCH), c_("bq0", NCH), DK ** -0.5, None, ALU.mult).then_inc(sem["bq8"], 1)
            dve.wait_ge(sem["bq8"], 1)
            dve.wait_ge(sem["iota"], 1)
            V.tensor_copy(iota[:], iota_i[:]).then_inc(sem["iotaf"], 1)
            dve.wait_ge(sem["iotaf"], 1)

            def a_sums(a, n):
                dve.wait_ge(sem["squares"], upto("squares", a, n))
                V.reduce_sum(ss[:], sq[:], AX_X).then_inc(sem["sums"], 1)
                dve.wait_ge(sem["sums"], upto("sums", a, n))
                V.tensor_scalar(ssf[:], ss[:], 1.0 / P, 1e-24 / P, ALU.mult, ALU.max).then_inc(sem["floored"], 1)

            def a_conv(a):
                dve.wait_ge(sem["normT"], upto("normT", a, 0))
                if later(a):
                    dve.wait_ge(sem["a_bank"], upto("a_bank", a - 1, A_USE['pw']))
                V.tensor_scalar(cv2[:], xc[:, :, 2:T + 2], c_("dw2"), c_("dwb"), ALU.mult, ALU.add).then_inc(sem["conv2"], 1)
                dve.wait_ge(sem["conv2"], upto("conv2", a))
                V.scalar_tensor_tensor(cv1[:], xc[:, :, 1:T + 1], c_("dw1"), cv2[:], ALU.mult, ALU.add).then_inc(sem["conv1"], 1)
                dve.wait_ge(sem["conv1"], upto("conv1", a))
                V.scalar_tensor_tensor(cv[:], xc[:, :, 0:T], c_("dw0"), cv1[:], ALU.mult, ALU.add).then_inc(sem["conv0"], 1)

            def a_mixed(a):
                dve.wait_ge(sem["a_bank"], upto("a_bank", a, A_USE['pw']))
                dve.wait_ge(sem["x_bpw"], upto("x_bpw", a))
                if later(a):
                    dve.wait_ge(sem["normed"], upto("normed", a - 1, 1))
                V.tensor_tensor(xm[:], seqs(ma[:]), xb[:], ALU.add).then_inc(sem["mixed"], 1)
                a_sums(a, 1)

            def a_gru(a):
                dve.wait_ge(sem["gate_tanh"], upto("gate_tanh", a))
                V.tensor_scalar(keep[:], seqs(tg[:]), -0.5, 0.5, ALU.mult, ALU.add).then_inc(sem["keep"], 1)
                V.tensor_scalar(inp[:], tg[:], 0.5, 0.5, ALU.mult, ALU.add).then_inc(sem["inp"], 1)
                dve.wait_ge(sem["keep"], upto("keep", a))
                V.memset(keep[:, :, 0:1], 0.0).then_inc(sem["keep0"], 1)
                dve.wait_ge(sem["hid_tanh"], upto("hid_tanh", a))
                V.tensor_scalar(sg[:], th[:], 0.5, 0.5, ALU.mult, ALU.add).then_inc(sem["sig"], 1)
                dve.wait_ge(sem["sig"], upto("sig", a))
                V.scalar_tensor_tensor(cand[:], ma[:], 0.5, sg[:], ALU.add, ALU.max).then_inc(sem["cand"], 1)
                dve.wait_ge(sem["cand"], upto("cand", a))
                dve.wait_ge(sem["inp"], upto("inp", a))
                V.tensor_tensor(drive[:], inp[:], cand[:], ALU.mult).then_inc(sem["drive"], 1)
                dve.wait_ge(sem["drive"], upto("drive", a))
                dve.wait_ge(sem["keep0"], upto("keep0", a))
                if later(a):
                    dve.wait_ge(sem["a_bank"], upto("a_bank", a - 1, A_USE['Th']))
                V.tensor_tensor_scan(hs[:], keep[:].rearrange("p b t -> p (b t)"), drive[:], 0.0,
                                     ALU.mult, ALU.add).then_inc(sem["scan"], 1)

            def a_gru_sum(a):
                dve.wait_ge(sem["a_bank"], upto("a_bank", a, A_USE['Th']))
                if later(a):
                    dve.wait_ge(sem["x_all"], upto("x_all", a - 1))
                V.tensor_tensor(xg[:], seqs(ma[:]), xm[:], ALU.add).then_inc(sem["gru_sum"], 1)
                a_sums(a, 2)

            def a_mixer(a):
                dve.wait_ge(sem["a_bank"], upto("a_bank", a, A_USE['ff2']))
                dve.wait_ge(sem["x_all"], upto("x_all", a))
                V.tensor_tensor(xr[:], seqs(ma[:]), xz[:], ALU.add).then_inc(sem["mixer"], 1)
                dve.wait_ge(sem["mixer"], upto("mixer", a))
                for q in range(SEQ):
                    V.bn_stats(st1[:, q, :], xr[:, q, :]).then_inc(sem["ln1_stats"], 1)
                for q in range(SEQ):
                    dve.wait_ge(sem["ln1_stats"], upto("ln1_stats", a, q))
                    settle(dve)
                    V.bn_aggr(mv1[:, q, :], st1[:, q, :]).then_inc(sem["ln1_mv"], 1)

            def a_ln1(a):
                dve.wait_ge(sem["ln1_rstd"], upto("ln1_rstd", a))
                if later(a):
                    dve.wait_ge(sem["a_bank"], whole("a_bank", a - 1))
                if later(a):
                    dve.wait_ge(sem["x1_bo"], upto("x1_bo", a - 1))
                for q in range(SEQ):
                    V.tensor_scalar(x1[:, q, :], xr[:, q, :], mv1[:, q, 0:1], rs1[:, q:q + 1],
                                    ALU.subtract, ALU.mult).then_inc(sem["ln1_out"], 1)

            def b_project(b, lo, hi):
                for n in range(lo, hi):
                    if n % 2 == 0:
                        continue
                    dve.wait_ge(sem["proj"], upto("proj", b, n))
                    src = proj_banks[n % 5]
                    if n < 8:
                        if n == 1:
                            if later(b):
                                dve.wait_ge(sem["pv"], whole("pv", b - 1))
                        ins = V.tensor_copy(vv[:, n // 2, 512:1024], src[0:S, :])
                    elif n < 16:
                        if n == 9:
                            if later(b):
                                dve.wait_ge(sem["scores"], whole("scores", b - 1))
                        ins = V.tensor_scalar(kT[:, n - 8, :], src[:, 0:SW], c_(f"bk{n - 8}"), None, ALU.add)
                    else:
                        ins = V.tensor_scalar(qT[:, n - 16, :], src[:], DK ** -0.5, c_(f"bq{n - 16}"), ALU.mult, ALU.add)
                    ins.then_inc(sem["proj_dve"], 1)

            def b_max(b, p):
                for r in range(2):
                    dve.wait_ge(sem["scores"], upto("scores", b, 2 * p + r))
                    V.tensor_reduce(nm[:, p % 2, r, :], seqs(score_banks[r][:, 0:4 * S]), AX_X, ALU.max,
                                    negate=True).then_inc(sem["negmax"], 1)

            def b_probs_T(b, p):
                if p:
                    dve.wait_ge(sem["pv"], upto("pv", b, p - 1))
                else:
                    if later(b):
                        dve.wait_ge(sem["pv"], whole("pv", b - 1))
                for k in range(2):
                    dve.wait_ge(sem["probsT"], upto("probsT", b, 2 * p + k))
                    V.tensor_copy(pT[:, 4 * k:4 * k + 4, :], seqs((t0, t1)[k][0:S, :])).then_inc(sem["probsT_sb"], 1)

            def b_recips(b, p, r):
                dve.wait_ge(sem["probs"], upto("probs", b, 2 * p + r))
                V.reciprocal(ri[:, p % 2, r, :, :], rsum[:, p % 2, r, :, :]).then_inc(sem["rinv"], 1)

            def b_heads_T(b, p):
                half = p % 2
                dve.wait_ge(sem["pv"], upto("pv", b, p))
                if p > 1:
                    dve.wait_ge(sem["wo"], upto("wo", b, p // 2 - 1))
                elif later(b):
                    dve.wait_ge(sem["wo"], whole("wo", b - 1))
                V.tensor_tensor(hT[:, 4 * half:4 * half + 4, :], seqs(pvb[:]),
                                c_(f"bv{4 * half}", 4).unsqueeze(2).to_broadcast([P, 4, T]),
                                ALU.add).then_inc(sem["headsT_sb"], 1)

            def b_sum(b, q):
                dve.wait_ge(sem["wo"], upto("wo", b, q))
                dve.wait_ge(sem["x1_bo"], upto("x1_bo", b))
                V.tensor_tensor(xa[:], pvb[:, 0:P], x1b[:, q, :], ALU.add).then_inc(sem["attn_sum"], 1)
                dve.wait_ge(sem["attn_sum"], upto("attn_sum", b, q))
                V.bn_stats(st2[:], xa[:]).then_inc(sem["ln2_stats"], 1)
                dve.wait_ge(sem["ln2_stats"], upto("ln2_stats", b, q))
                settle(dve)
                V.bn_aggr(mv2[:], st2[:]).then_inc(sem["ln2_mv"], 1)

            def b_ln2(b, q):
                dve.wait_ge(sem["ln2_rstd"], upto("ln2_rstd", b, q))
                if later(b):
                    dve.wait_ge(sem["x2T"], whole("x2T", b - 1))
                V.tensor_scalar(x2[:, q, :], xa[:], mv2[:, 0:1], rs2[:], ALU.subtract, ALU.mult).then_inc(sem["ln2_out"], 1)

            def c_logits(c):
                for k, src in enumerate((m1, m0)):
                    dve.wait_ge(sem["sh_tanh"], upto("sh_tanh", c, k))
                    V.tensor_tensor(lg[:, 2 * k:2 * k + 2, :], seqs(src[:, 0:2 * RS], 2)[:, :, 0:E],
                                    brow["gate"].unsqueeze(1).to_broadcast([P, 2, E]), ALU.add).then_inc(sem["logits"], 1)

            def c_shared(c):
                for k, src in enumerate((m1, m0)):
                    dve.wait_ge(sem["sh_tanh"], upto("sh_tanh", c, k))
                    v = seqs(src[:, 0:2 * RS], 2)
                    sl = slice(2 * k, 2 * k + 2)
                    if k == 0:
                        if later(c):
                            dve.wait_ge(sem["shT"], whole("shT", c - 1))
                    V.scalar_tensor_tensor(gsh[:, sl, :], tsh[:, sl, :], 1.0, v[:, :, E:E + I], ALU.add, ALU.mult).then_inc(sem["sh_gate"], 1)
                    dve.wait_ge(sem["sh_gate"], upto("sh_gate", c, k))
                    V.scalar_tensor_tensor(ash[:, sl, :], gsh[:, sl, :], 0.5, v[:, :, E + I:RS],
                                           ALU.mult, ALU.mult).then_inc(sem["sh_act"], 1)

            def c_route(c):
                dve.wait_ge(sem["route_tanh"], upto("route_tanh", c))
                V.tensor_scalar(sg8[:], rt[:], 0.5, 0.5, ALU.mult, ALU.add).then_inc(sem["route_sig"], 1)
                dve.wait_ge(sem["route_sig"], upto("route_sig", c))
                settle(dve)
                for q in range(SEQ):
                    V.max(mx[:, q, :], sg8[:, q, :]).then_inc(sem["top"], 1)
                for q in range(SEQ):
                    dve.wait_ge(sem["top"], upto("top", c, q))
                    settle(dve)
                    V.max_index(mi[:, q, :], mx[:, q, :], sg8[:, q, :]).then_inc(sem["top_at"], 1)
                V.tensor_tensor(tsum[:], mx[:, :, 0:1], mx[:, :, 1:2], ALU.add).then_inc(sem["top_sum"], 1)
                dve.wait_ge(sem["top_sum"], upto("top_sum", c))
                dve.wait_ge(sem["top_at"], whole("top_at", c))
                V.tensor_copy(mf[:], mi[:, :, 0:2]).then_inc(sem["top_f"], 1)
                V.reciprocal(trec[:], tsum[:]).then_inc(sem["top_rec"], 1)
                dve.wait_ge(sem["top_rec"], upto("top_rec", c))
                V.scalar_tensor_tensor(tw[:], mx[:, :, 0:2], 0.5, trec[:].to_broadcast([P, SEQ, 2]),
                                       ALU.mult, ALU.mult).then_inc(sem["top_w"], 1)
                dve.wait_ge(sem["top_f"], upto("top_f", c))
                for o, k in ((o0, 0), (o1, 1)):
                    V.tensor_tensor(o[:], over_seqs(iota[:]), mf[:, :, k:k + 1].to_broadcast([P, SEQ, E]),
                                    ALU.is_equal).then_inc(sem[f"one{k}"], 1)
                dve.wait_ge(sem["top_w"], upto("top_w", c))
                for o, w, k in ((o0, q0, 0), (o1, q1, 1)):
                    dve.wait_ge(sem[f"one{k}"], upto(f"one{k}", c))
                    V.tensor_tensor(w[:], o[:], tw[:, :, k:k + 1].to_broadcast([P, SEQ, E]), ALU.mult).then_inc(sem[f"w{k}"], 1)
                dve.wait_ge(sem["w0"], upto("w0", c))
                dve.wait_ge(sem["w1"], upto("w1", c))
                if later(c):
                    dve.wait_ge(sem["e_weighted"], whole("e_weighted", c - 1))
                V.tensor_tensor(gw[:], q0[:], q1[:], ALU.add).then_inc(sem["gates"], 1)

            def c_experts(c, n):
                dve.wait_ge(sem["e_tanh"], upto("e_tanh", c, n))
                V.scalar_tensor_tensor(e1[:], et[:], 1.0, m0[:], ALU.add, ALU.mult).then_inc(sem["e_gate"], 1)
                dve.wait_ge(sem["e_gate"], upto("e_gate", c, n))
                dve.wait_ge(sem["eu"], upto("eu", c, n))
                if n >= 2:
                    dve.wait_ge(sem["e_weighted"], upto("e_weighted", c, n - 2))
                else:
                    if later(c):
                        dve.wait_ge(sem["e_weighted"], upto("e_weighted", c - 1, n + 6))
                V.tensor_tensor(e3[:, n % 2, :], e1[:], m1[:], ALU.mult).then_inc(sem["e_act"], 1)

            def c_sum(c, q):
                dve.wait_ge(sem["down"], upto("down", c, q))
                V.scalar_tensor_tensor(ys[:], x2[:, q, :], 2.0, m1[:, 0:P], ALU.mult, ALU.add).then_inc(sem["moe_sum"], 1)
                dve.wait_ge(sem["moe_sum"], upto("moe_sum", c, q))
                V.bn_stats(st3[:], ys[:]).then_inc(sem["ln3_stats"], 1)
                dve.wait_ge(sem["ln3_stats"], upto("ln3_stats", c, q))
                settle(dve)
                V.bn_aggr(mv3[:], st3[:]).then_inc(sem["ln3_mv"], 1)

            def c_ln3(c, q):
                dve.wait_ge(sem["ln3_rstd"], upto("ln3_rstd", c, q))
                if later(c):
                    dve.wait_ge(sem[f"out{q}_stored"], upto(f"out{q}_stored", c - 1))
                V.tensor_scalar(y[:, q, :], ys[:], mv3[:, 0:1], rs3[:], ALU.subtract, ALU.mult).then_inc(sem["ln3_out"], 1)

            def body(a, b, c):
                A, B, C = a is not None, b is not None, c is not None
                if B:
                    b_project(b, 0, 8)
                if A:
                    a_sums(a, 0)
                if C:
                    c_logits(c)
                    c_shared(c)
                if B:
                    b_project(b, 8, 16)
                if C:
                    c_route(c)
                if B:
                    b_project(b, 16, 24)
                for s in range(PAIRS + 1):
                    q = s // 2 - 1
                    even = s and s % 2 == 0
                    if C and not even:
                        c_experts(c, s)
                    if B and s > 1:
                        b_probs_T(b, s - 1)
                    if B and s < PAIRS:
                        b_max(b, s)
                        if s == 1:
                            b_probs_T(b, 0)
                        b_recips(b, s, 0)
                    if B and s:
                        b_heads_T(b, s - 1)
                    if B and s < PAIRS:
                        b_recips(b, s, 1)
                    if C and even:
                        c_sum(c, q)
                        if s < PAIRS:
                            c_experts(c, s)
                    if B and even:
                        b_sum(b, q)
                    if C and even:
                        c_ln3(c, q)
                    if B and even:
                        b_ln2(b, q)
                    if A:
                        if s == 0:
                            a_conv(a)
                        elif s == 1:
                            a_mixed(a)
                        elif s == 4:
                            a_gru(a)
                        elif s == 5:
                            a_gru_sum(a)
                        elif s == 8:
                            a_mixer(a)
                            a_ln1(a)

            pipeline(dve, body)

        @block.gpsimd
        def _(pool):
            GP = nc.gpsimd
            GP.memset(ident[:], 0.0).then_inc(sem["ones"], 1)
            GP.memset(maskb[:], 0.0).then_inc(sem["mask0"], 1)
            pool.wait_ge(sem["ones"], 1)
            GP.affine_select(out=ident[:], in_=ident[:], pattern=[[-1, P]], compare_op=ALU.not_equal, fill=1.0,
                             base=0, channel_multiplier=1).then_inc(sem["ident"], 1)
            pool.wait_ge(sem["ident"], 1)
            GP.tensor_copy(identb[:], ident[:]).then_inc(sem["identb"], 1)
            pool.wait_ge(sem["mask0"], 1)
            GP.affine_select(out=maskb[:], in_=maskb[:], pattern=[[-1, S]], compare_op=ALU.is_ge, fill=-1e10,
                             base=0, channel_multiplier=1).then_inc(sem["mask"], 1)
            GP.iota(iota_i[:], pattern=[[1, E]], base=0, channel_multiplier=0).then_inc(sem["iota"], 1)
            pool.wait_ge(sem["weights"], WEIGHTS)
            pool.wait_ge(sem["powers"], 2)

            def a_squares(a, n):
                src = (xt, xm, xg)[n]
                if n == 0:
                    pool.wait_ge(sem["x_loaded"], whole("x_loaded", a))
                    if later(a):
                        pool.wait_ge(sem["sums"], whole("sums", a - 1))
                else:
                    pool.wait_ge(sem[("mixed", "gru_sum")[n - 1]], upto(("mixed", "gru_sum")[n - 1], a))
                    pool.wait_ge(sem["sums"], upto("sums", a, n - 1))
                GP.tensor_tensor(sq[:], src[:], src[:], ALU.mult).then_inc(sem["squares"], 1)

            def a_normed(a, n):
                src = (xt, xm, xg)[n]
                pool.wait_ge(sem["floored"], upto("floored", a, n))
                GP.tensor_tensor(rr[:], ssf[:], power[:], ALU.pow).then_inc(sem["rms"], 1)
                pool.wait_ge(sem["rms"], upto("rms", a, n))
                if n:
                    pool.wait_ge(sem["a_bank"], upto("a_bank", a, A_USE[f'T{n - 1}']))
                else:
                    if later(a):
                        pool.wait_ge(sem["a_bank"], upto("a_bank", a - 1, A_USE['T2']))
                GP.tensor_tensor(xn[:], src[:], rr[:].unsqueeze(2).to_broadcast([P, SEQ, P]), ALU.mult).then_inc(sem["normed"], 1)

            def a_residuals(a):
                if later(a):
                    pool.wait_ge(sem["mixed"], upto("mixed", a - 1))
                GP.tensor_tensor(xb[:], xt[:], over_seqs(brow["pw"]), ALU.add).then_inc(sem["x_bpw"], 1)
                GP.tensor_tensor(xf[:], xt[:], over_seqs(brow["ff2"]), ALU.add).then_inc(sem["x_bff"], 1)

            def a_all(a):
                pool.wait_ge(sem["gru_sum"], upto("gru_sum", a))
                pool.wait_ge(sem["x_bff"], upto("x_bff", a))
                if later(a):
                    pool.wait_ge(sem["mixer"], upto("mixer", a - 1))
                GP.tensor_tensor(xz[:], xf[:], xg[:], ALU.add).then_inc(sem["x_all"], 1)

            def a_ln1(a):
                pool.wait_ge(sem["ln1_mv"], whole("ln1_mv", a))
                GP.tensor_tensor(ve1[:], mv1[:, :, 1], eps[:], ALU.add).then_inc(sem["ln1_eps"], 1)
                pool.wait_ge(sem["ln1_eps"], upto("ln1_eps", a))
                GP.tensor_tensor(rs1[:], ve1[:], power[:], ALU.pow).then_inc(sem["ln1_rstd"], 1)

            def a_x1_bo(a):
                pool.wait_ge(sem["ln1_out"], whole("ln1_out", a))
                if later(a):
                    pool.wait_ge(sem["attn_sum"], whole("attn_sum", a - 1))
                GP.tensor_tensor(x1b[:], x1[:], over_seqs(brow["bo"]), ALU.add).then_inc(sem["x1_bo"], 1)

            def b_normal(b, p):
                for r in range(2):
                    pool.wait_ge(sem["rinv"], upto("rinv", b, 2 * p + r))
                    GP.tensor_tensor(pr[:, p % 2, r, :, :], pr[:, p % 2, r, :, :],
                                     ri[:, p % 2, r, :, :].to_broadcast([P, 4, S]), ALU.mult).then_inc(sem["normal"], 1)

            def ln(g, q, n, mv, ve, rs):
                pool.wait_ge(sem[f"ln{n}_mv"], upto(f"ln{n}_mv", g, q))
                GP.tensor_tensor(ve[:], mv[:, 1:2], eps[:, 0:1], ALU.add).then_inc(sem[f"ln{n}_eps"], 1)
                pool.wait_ge(sem[f"ln{n}_eps"], upto(f"ln{n}_eps", g, q))
                GP.tensor_tensor(rs[:], ve[:], power[:, 0:1], ALU.pow).then_inc(sem[f"ln{n}_rstd"], 1)

            def c_weight(c, n):
                pool.wait_ge(sem["gates"], upto("gates", c))
                pool.wait_ge(sem["e_act"], upto("e_act", c, n))
                if n >= 2:
                    pool.wait_ge(sem["eT"], upto("eT", c, 2 * (n // 2 - 1) + 1))
                else:
                    if later(c):
                        pool.wait_ge(sem["eT"], whole("eT", c - 1))
                half = n % 2
                GP.tensor_tensor(seqs(ew[:, half * 512:(half + 1) * 512], 8), seqs(e3[:, n % 2, :], 8),
                                 gw[:, n // 2, 8 * half:8 * half + 8].unsqueeze(2).to_broadcast([P, 8, I]),
                                 ALU.mult).then_inc(sem["e_weighted"], 1)

            def body(a, b, c):
                A, B, C = a is not None, b is not None, c is not None
                if A:
                    a_squares(a, 0)
                    a_normed(a, 0)
                    a_residuals(a)
                for s in range(PAIRS + 1):
                    q = s // 2 - 1
                    even = s and s % 2 == 0
                    if C and (not even):
                        c_weight(c, s)
                    if B and s < PAIRS:
                        b_normal(b, s)
                    if C and even:
                        ln(c, q, 3, mv3, ve3, rs3)
                        if s < PAIRS:
                            c_weight(c, s)
                    if B and even:
                        ln(b, q, 2, mv2, ve2, rs2)
                    if A:
                        if s == 1:
                            a_squares(a, 1)
                            a_normed(a, 1)
                        elif s == 5:
                            a_squares(a, 2)
                            a_normed(a, 2)
                            a_all(a)
                        elif s == 8:
                            a_ln1(a)
                            a_x1_bo(a)

            pipeline(pool, body)


def kernel(**inputs):
    import numpy as np
    import concourse.bacc as bacc
    from concourse.bass_utils import run_bass_kernel_spmd

    a = {n: np.asarray(v) for n, v in inputs.items()}
    L, X, M = "L0_attn_", "L0_xattn_", "L0_ffn_"

    def chunks(v):
        return v.reshape(-1, P, *v.shape[1:]).swapaxes(0, 1)

    laid = {
        "x": a["x"],
        "ctxT": a["ctx_1024"].reshape(G, SEQ, S, P).transpose(0, 3, 1, 2).reshape(G, P, SW),
        "w_pw": a[L + "conv_pw_w"].T,
        "w_gru": a[L + "gru_w"].T,
        "w_ff1": a[L + "ff_w1"].T,
        "w_ff2": chunks(a[L + "ff_w2"].T),
        "cols": np.concatenate([a[L + "conv_dw_w"][:, 0, :], a[L + "conv_dw_b"][:, None], a[L + "conv_norm_g"][:, None],
                                a[L + "gru_norm_g"][:, None], a[L + "ff_norm_g"][:, None], chunks(a[L + "ff_b1"]),
                                chunks(a[X + "bq"]), chunks(a[X + "bk"]), chunks(a[X + "bv"])], axis=1),
        "rows": np.concatenate([a[L + "conv_pw_b"], a[L + "ff_b2"], a[X + "bo"], a[M + "gate_b"]])[None, :],
        "w_q": a[X + "Wq"], "w_k": a[X + "Wk"], "w_v": a[X + "Wv"], "w_o": chunks(a[X + "Wo"]),
        "w_g": a[M + "experts_wg"].transpose(1, 0, 2).reshape(P, E * I),
        "w_u": a[M + "experts_wu"].transpose(1, 0, 2).reshape(P, E * I),
        "w_rs": np.concatenate([a[M + "gate_w"], a[M + "shared_wg"], a[M + "shared_wu"]], axis=1),
        "w_d": chunks(a[M + "experts_wd"].reshape(E * I, P)),
        "w_sd": a[M + "shared_wd"],
    }
    nc = bacc.Bacc("TRN2", target_bir_lowering=False, num_devices=1)
    arrays, aps = {}, {}
    for name, v in laid.items():
        arrays[f"in_{name}"] = np.ascontiguousarray(v)
        aps[name] = nc.dram_tensor(f"in_{name}", v.shape, F32, kind="ExternalInput").ap()
    aps["out"] = nc.dram_tensor("out_y", [NSEQ, T, P], F32, kind="ExternalOutput").ap()
    layer_kernel(nc, **aps)
    r = run_bass_kernel_spmd(nc, [arrays], core_ids=[0])
    return r.results[0]["out_y"]
```

```python
from contextlib import ExitStack

import concourse.bass as bass
from concourse import mybir

ALU = mybir.AluOpType
ACT = mybir.ActivationFunctionType
F32 = mybir.dt.float32
BF16 = mybir.dt.bfloat16
U32 = mybir.dt.uint32
AX_X = mybir.AxisListType.X

P = 128
T = 128
NSEQ = 64
SEQ = 4
G = NSEQ // SEQ
S = 120
H = 16
DK = 64
NCH = H * DK // P
E = 16
I = 64
F = 512
FCH = F // P
W = SEQ * T
SW = SEQ * S
PAIRS = 2 * SEQ
LAG = 2
RING = 2 * LAG
RS = E + 2 * I

COLS = ["dw0", "dw1", "dw2", "dwb", "g_conv", "g_gru", "g_ff"] + [f"b1_{c}" for c in range(FCH)] + \
    [f"bq{j}" for j in range(NCH)] + [f"bk{j}" for j in range(NCH)] + [f"bv{j}" for j in range(NCH)]
ROWS = 3 * P + E

PER_GROUP = {
    "x_loaded": 16, "ctx_loaded": 16, "out0_stored": 16, "out1_stored": 16, "out2_stored": 16, "out3_stored": 16,
    "sums": 3, "floored": 3, "rms": 3, "normed": 3, "x_bpw": 1, "x_bff": 1, "x_all": 1,
    "a_bank": 13, "normT": 3, "conv2": 1, "conv1": 1, "conv0": 1, "mixed": 1,
    "gate_tanh": 1, "hid_tanh": 1, "keep": 1, "keep0": 1, "inp": 1, "sig": 1, "cand": 1, "drive": 1, "scan": 1,
    "gru_sum": 1, "gelu": 4, "mixer": 1,
    "ln1_stats": 4, "ln1_mv": 4, "ln1_eps": 1, "ln1_rstd": 1, "ln1_out": 4, "x1T": 1, "x1_bo": 1,
    "proj": 24, "proj_act": 12, "proj_dve": 12, "scores": 16, "negmax": 16, "probs": 16,
    "probsT": 16, "probsT_sb": 16, "rinv": 16, "normal": 16, "pv": 8, "headsT_sb": 8,
    "wo": 4, "attn_sum": 4, "ln2_stats": 4, "ln2_mv": 4, "ln2_eps": 4, "ln2_rstd": 4, "ln2_out": 4,
    "x2T": 1, "x2T_sb": 1, "rs": 2, "logits": 2, "route_tanh": 1, "route_sig": 1, "top": 4, "top_at": 4,
    "top_f": 1, "top_sum": 1, "top_rec": 1, "top_w": 1, "one0": 1, "one1": 1, "w0": 1, "w1": 1, "gates": 1,
    "sh_tanh": 2, "sh_gate": 2, "sh_act": 2, "shT": 1, "shT_sb": 1,
    "eg": 8, "eu": 8, "e_tanh": 8, "e_gate": 8, "e_act": 8, "e_weighted": 8, "eT": 8, "eT_sb": 8,
    "down": 4, "moe_sum": 4, "ln3_stats": 4, "ln3_mv": 4, "ln3_eps": 4, "ln3_rstd": 4, "ln3_out": 4,
}
ONCE = ["waits_held", "weights", "ident", "identb", "mask0", "mask", "iota", "iotaf", "ones", "gammas", "bq8", "powers", "pads"]

A_USE = {n: k for k, n in enumerate(
    ["T0", "pw", "T1", "gate", "hid", "Th", "T2"] + [f"up{k}" for k in range(FCH)] + ["ff2", "Tx1"])}


def layer_kernel(nc, x, ctxT, w_pw, w_gru, w_ff1, w_ff2, cols, rows, w_q, w_k, w_v, w_o, w_g, w_u, w_rs, w_d, w_sd, out):
    with ExitStack() as ctx:
        def sb(name, shape, dt=F32):
            return ctx.enter_context(nc.sbuf_tensor(name, shape, dt))

        sem = {n: ctx.enter_context(nc.semaphore(n)) for n in [*PER_GROUP, *ONCE]}

        def later(g):
            return not (isinstance(g, int) and g == 0)

        def upto(name, g, k=0):
            return g * PER_GROUP[name] + (k + 1) * (16 if name.endswith(("loaded", "stored")) else 1)

        def whole(name, g):
            return g * PER_GROUP[name] + PER_GROUP[name]

        def settle(eng):
            eng.sem_inc(sem["waits_held"], 1)

        pw = sb("pw", [P, P]); gru = sb("gru", [P, 2 * P]); ff1 = sb("ff1", [P, F]); ff2 = sb("ff2", [P, FCH, P])
        wq = sb("wq", [P, H * DK]); wk = sb("wk", [P, H * DK]); wv = sb("wv", [P, H * DK]); wo = sb("wo", [P, NCH, P])
        wg = sb("wg", [P, E * I]); wu = sb("wu", [P, E * I]); wrs = sb("wrs", [P, RS])
        wd = sb("wd", [P, E // 2, P]); wsd = sb("wsd", [I, P])
        col = sb("col", [P, len(COLS)]); row = sb("row", [P, ROWS])
        ident = sb("ident_f", [P, P]); identb = sb("ident_b", [P, P], BF16); maskb = sb("mask_b", [P, S], BF16)
        iota_i = sb("iota_i", [P, E], mybir.dt.int32); iota = sb("iota_f", [P, E])
        power = sb("power", [P, SEQ])

        eps = sb("eps", [P, SEQ])
        xt = sb("xt", [P, SEQ, P]); sq = sb("sq", [P, SEQ, P]); ss = sb("ss", [P, SEQ]); ssf = sb("ssf", [P, SEQ])
        rr = sb("rr", [P, SEQ]); xn = sb("xn", [P, SEQ, P]); xb = sb("xb", [P, SEQ, P]); xf = sb("xf", [P, SEQ, P])
        xc = sb("xc", [P, SEQ, T + 2])
        cv2 = sb("cv2", [P, SEQ, T]); cv1 = sb("cv1", [P, SEQ, T]); cv = sb("cv", [P, SEQ, T])
        xm = sb("xm", [P, SEQ, P]); nT = sb("nT", [P, W])
        tg = sb("tg", [P, W]); th = sb("th", [P, W]); keep = sb("keep_sb", [P, SEQ, T]); inp = sb("inp_sb", [P, W])
        sg = sb("sg", [P, W]); cand = sb("cand_sb", [P, W]); drive = sb("drive_sb", [P, W]); hs = sb("hs", [P, W])
        xg = sb("xg", [P, SEQ, P]); xz = sb("xz", [P, SEQ, P]); hf = sb("hf", [P, FCH, W]); xr = sb("xr", [P, SEQ, P])
        st1 = sb("st1", [P, SEQ, 6]); mv1 = sb("mv1", [P, SEQ, 2]); ve1 = sb("ve1", [P, SEQ]); rs1 = sb("rs1", [P, SEQ])
        x1 = sb("x1", [P, SEQ, P]); x1T = sb("x1T_s", [P, W]); x1b = sb("x1b", [P, SEQ, P])
        cT = sb("cT", [P, SW]); vv = sb("vv", [S, SEQ, H * DK]); kT = sb("kT", [P, NCH, SW]); qT = sb("qT", [P, NCH, W])
        nm = sb("nm", [P, 2, 2, 4]); pr = sb("pr", [P, RING, 2, 4, S]); rsum = sb("rsum", [P, 2, 2, 4, 1])
        pT = sb("pT", [S, 8, T]); ri = sb("ri", [P, 2, 2, 4, 1]); hT = sb("hT", [P, NCH, T])
        xa = sb("xa", [P, P]); st2 = sb("st2", [P, 6]); mv2 = sb("mv2", [P, 2]); ve2 = sb("ve2", [P, 1]); rs2 = sb("rs2", [P, 1])
        x2 = sb("x2", [P, SEQ, P])
        x2T = sb("x2T_s", [P, W]); lg = sb("lg", [P, SEQ, E]); rt = sb("rt", [P, SEQ, E]); sg8 = sb("sg8", [P, SEQ, E])
        mx = sb("mx", [P, SEQ, 8]); mi = sb("mi", [P, SEQ, 8], U32); mf = sb("mf", [P, SEQ, 2])
        tsum = sb("tsum", [P, SEQ, 1]); trec = sb("trec", [P, SEQ, 1]); tw = sb("tw", [P, SEQ, 2])
        o0 = sb("o0", [P, SEQ, E]); o1 = sb("o1", [P, SEQ, E]); q0 = sb("q0", [P, SEQ, E]); q1 = sb("q1", [P, SEQ, E])
        gw = sb("gw", [P, SEQ, E])
        tsh = sb("tsh", [P, SEQ, I]); gsh = sb("gsh", [P, SEQ, I]); ash = sb("ash", [P, SEQ, I]); sT = sb("sT", [I, W])
        et = sb("et", [P, 512]); e1 = sb("e1", [P, 512]); e3 = sb("e3", [P, 2, 512]); ew = sb("ew", [P, E * I])
        eT = sb("eT_s", [P, E // 2, T]); ys = sb("ys", [P, P])
        st3 = sb("st3", [P, 6]); mv3 = sb("mv3", [P, 2]); ve3 = sb("ve3", [P, 1]); rs3 = sb("rs3", [P, 1])
        y = sb("y", [P, SEQ, P])

        def bank(name):
            return ctx.enter_context(nc.psum_tensor(name, [P, 512], F32))

        sE, sO, t0, t1, pvb = bank("sE"), bank("sO"), bank("t0"), bank("t1"), bank("pvb")
        m0, m1 = bank("m0"), bank("m1")
        ma = bank("ma")
        projections = [("k", j) for j in range(8)] + [("v", j) for j in range(2)] + \
            [("q", j) for j in range(8)] + [("v", j) for j in range(2, 8)]
        proj_banks = [sE, sO, sE, sO] + [(t0, t1, pvb, sE, sO)[n % 5] for n in range(10)] + [(t0, t1, pvb)[n % 3] for n in range(10)]
        ff1_banks = [ma, sE, sO, ma]
        score_banks = [sE, sO]

        def seqs(ap, n=SEQ):
            return ap.rearrange("p (b n) -> p b n", b=n)

        def c_(name, n=1):
            k = COLS.index(name)
            return col[:, k:k + n]

        brow = {"pw": row[:, 0:P], "ff2": row[:, P:2 * P], "bo": row[:, 2 * P:3 * P], "gate": row[:, 3 * P:3 * P + E]}

        def over_seqs(ap):
            return ap.unsqueeze(1).to_broadcast([P, SEQ, ap.shape[1]])

        weight_loads = [(pw[:], w_pw), (gru[:], w_gru), (ff1[:], w_ff1), (ff2[:], w_ff2), (wq[:], w_q), (wk[:], w_k),
                        (wv[:], w_v), (wo[:], w_o), (wg[:], w_g), (wu[:], w_u), (wrs[:], w_rs), (wd[:], w_d),
                        (wsd[:], w_sd), (col[:], cols), (row[:], rows.to_broadcast([P, ROWS]))]
        NWL = len(weight_loads)
        WEIGHTS = 16 * NWL

        block = ctx.enter_context(nc.Block())

        def pipeline(eng, body):
            body(0, None, None)
            body(1, 0, None)
            body(2, 1, 0)
            with eng.Fori(2, G - 1) as i:
                body(i + 1, i, i - 1)
            body(None, G - 1, G - 2)
            body(None, None, G - 1)

        @block.sync
        def _(sp):
            for dst, src in weight_loads:
                sp.dma_start(dst, src).then_inc(sem["weights"], 16)

            def body(a, b, c):
                if a is not None:
                    for n in ("sums", "normed", "x_bpw", "x_bff"):
                        if later(a):
                            sp.wait_ge(sem[n], upto(n, a - 1, 0))
                        settle(sp)
                    sp.dma_start(xt[:], x[bass.ds(a * SEQ, SEQ)].rearrange("b t d -> t b d")).then_inc(sem["x_loaded"], 16)
                    if later(a):
                        sp.wait_ge(sem["proj"], whole("proj", a - 1))
                    settle(sp)
                    sp.dma_start(cT[:], ctxT[bass.ds(a, 1)].rearrange("o d s -> d (o s)")).then_inc(sem["ctx_loaded"], 16)
                if c is not None:
                    for q in range(SEQ):
                        sp.wait_ge(sem["ln3_out"], upto("ln3_out", c, q))
                        settle(sp)
                        sp.dma_start(out[bass.ds(c * SEQ + q, 1)].rearrange("b t d -> (b t) d"),
                                     y[:, q, :]).then_inc(sem[f"out{q}_stored"], 16)

            pipeline(sp, body)
            for q in range(SEQ):
                if later(G):
                    sp.wait_ge(sem[f"out{q}_stored"], whole(f"out{q}_stored", G - 1))

        @block.tensor
        def _(pe):
            mm = nc.tensor.matmul
            pe.wait_ge(sem["weights"], WEIGHTS)
            pe.wait_ge(sem["ident"], 1)
            pe.wait_ge(sem["identb"], 1)
            pe.wait_ge(sem["mask"], 1)

            def turn(dst, src):
                return nc.tensor.transpose(dst, src, ident[0:src.shape[0], 0:src.shape[0]])

            def a_norm_T(a, n):
                pe.wait_ge(sem["normed"], upto("normed", a, n))
                if n == 0:
                    if later(a):
                        pe.wait_ge(sem["x1T"], whole("x1T", a - 1))
                elif n == 1:
                    pe.wait_ge(sem["mixed"], upto("mixed", a))
                else:
                    pe.wait_ge(sem["gru_sum"], upto("gru_sum", a))
                for q in range(SEQ):
                    ins = turn(ma[:, q * P:(q + 1) * P], xn[:, q, :])
                ins.then_inc(sem["a_bank"], 1)

            def a_pw(a):
                pe.wait_ge(sem["conv0"], upto("conv0", a))
                pe.wait_ge(sem["normT"], upto("normT", a, 0))
                for q in range(SEQ):
                    ins = mm(ma[:, q * P:(q + 1) * P], cv[:, q, :], pw[:], start=True, stop=True)
                ins.then_inc(sem["a_bank"], 1)

            def a_gate(a):
                pe.wait_ge(sem["normT"], upto("normT", a, 1))
                mm(ma[:], gru[:, P:2 * P], nT[:], start=True, stop=True).then_inc(sem["a_bank"], 1)

            def a_hid(a):
                pe.wait_ge(sem["gate_tanh"], upto("gate_tanh", a))
                mm(ma[:], gru[:, 0:P], nT[:], start=True, stop=True).then_inc(sem["a_bank"], 1)

            def a_scan_T(a):
                pe.wait_ge(sem["scan"], upto("scan", a))
                pe.wait_ge(sem["hid_tanh"], upto("hid_tanh", a))
                for q in range(SEQ):
                    ins = turn(ma[:, q * P:(q + 1) * P], hs[:, q * T:(q + 1) * T])
                ins.then_inc(sem["a_bank"], 1)

            def a_ff1(a, f):
                if f == 0:
                    pe.wait_ge(sem["normT"], upto("normT", a, 2))
                elif f == 1:
                    pe.wait_ge(sem["proj_act"], upto("proj_act", a, 1))
                elif f == 2:
                    pe.wait_ge(sem["proj_dve"], upto("proj_dve", a, 1))
                else:
                    pe.wait_ge(sem["gelu"], upto("gelu", a, 0))
                mm(ff1_banks[f][:], ff1[:, f * P:(f + 1) * P], nT[:], start=True, stop=True).then_inc(sem["a_bank"], 1)

            def a_ff2(a):
                pe.wait_ge(sem["gelu"], whole("gelu", a))
                for q in range(SEQ):
                    for f in range(FCH):
                        ins = mm(ma[:, q * P:(q + 1) * P], hf[:, f, q * T:(q + 1) * T], ff2[:, f, :],
                                 start=(f == 0), stop=(f == FCH - 1))
                ins.then_inc(sem["a_bank"], 1)

            def a_x1_T(a):
                pe.wait_ge(sem["ln1_out"], whole("ln1_out", a))
                for q in range(SEQ):
                    ins = turn(ma[:, q * P:(q + 1) * P], x1[:, q, :])
                ins.then_inc(sem["a_bank"], 1)

            def proj_free(b, n):
                former = [m for m in range(n) if proj_banks[m] is proj_banks[n]]
                if n in (7, 8):
                    pe.wait_ge(sem["gelu"], upto("gelu", b, n - 6))
                elif former:
                    other = "proj_dve" if former[-1] % 2 else "proj_act"
                    pe.wait_ge(sem[other], upto(other, b, former[-1] // 2))
                elif n < 2:
                    if later(b):
                        pe.wait_ge(sem["probs"], upto("probs", b - 1, 14 + n))
                elif n < 6:
                    if later(b):
                        pe.wait_ge(sem["probsT_sb"], upto("probsT_sb", b - 1, 14 + n - 4))
                else:
                    if later(b):
                        pe.wait_ge(sem["attn_sum"], whole("attn_sum", b - 1))

            def b_project(b, lo, hi):
                for n in range(lo, hi):
                    proj_free(b, n)
                    dst = proj_banks[n]
                    kind, j = projections[n]
                    if n == 0:
                        pe.wait_ge(sem["ctx_loaded"], whole("ctx_loaded", b))
                    if kind == "v":
                        q, half = j // 2, (j % 2) * 512
                        ins = mm(dst[0:S, :], cT[:, q * S:(q + 1) * S], wv[:, half:half + 512], start=True, stop=True)
                    elif kind == "k":
                        ins = mm(dst[:, 0:SW], wk[:, j * P:(j + 1) * P], cT[:], start=True, stop=True)
                    else:
                        if j == 0:
                            pe.wait_ge(sem["x1T"], whole("x1T", b))
                        ins = mm(dst[:], wq[:, j * P:(j + 1) * P], x1T[:], start=True, stop=True)
                    ins.then_inc(sem["proj"], 1)

            def b_scores(b, p):
                q, half = p // 2, p % 2
                if p == 0:
                    pe.wait_ge(sem["proj_act"], upto("proj_act", b, 12 // 2))
                    pe.wait_ge(sem["proj_dve"], upto("proj_dve", b, 13 // 2))
                elif p == 1:
                    pe.wait_ge(sem["proj_act"], upto("proj_act", b, 16 // 2))
                    pe.wait_ge(sem["proj_dve"], upto("proj_dve", b, 17 // 2))
                if p:
                    pe.wait_ge(sem["probs"], upto("probs", b, 2 * p - 1))
                for r in range(2):
                    mm(score_banks[r][:, 0:4 * S], identb[:], maskb[:].unsqueeze(1).to_broadcast([P, 4, S]),
                       start=True, stop=False, skip_group_check=True)
                for i in range(4):
                    j = 4 * half + i
                    for r in range(2):
                        ins = mm(score_banks[r][:, i * S:(i + 1) * S], qT[r * DK:(r + 1) * DK, j, q * T:(q + 1) * T],
                                 kT[r * DK:(r + 1) * DK, j, q * S:(q + 1) * S], start=False, stop=True,
                                 skip_group_check=True)
                        if i == 3:
                            ins.then_inc(sem["scores"], 1)

            def b_probs_T(b, p):
                for r in range(2):
                    if p:
                        pe.wait_ge(sem["probsT_sb"], upto("probsT_sb", b, 2 * p - 2 + r))
                    elif r == 0:
                        pe.wait_ge(sem["proj_dve"], upto("proj_dve", b, 23 // 2))
                    else:
                        pe.wait_ge(sem["proj_dve"], upto("proj_dve", b, 21 // 2))
                    pe.wait_ge(sem["normal"], upto("normal", b, 2 * p + r))
                    for i in range(4):
                        ins = turn((t0, t1)[r][0:S, i * T:(i + 1) * T], pr[:, p % RING, r, i, :])
                    ins.then_inc(sem["probsT"], 1)

            def b_pv(b, p):
                q, half = p // 2, p % 2
                pe.wait_ge(sem["probsT_sb"], upto("probsT_sb", b, 2 * p + 1))
                if half:
                    pe.wait_ge(sem["headsT_sb"], upto("headsT_sb", b, p - 1))
                elif p:
                    pe.wait_ge(sem["attn_sum"], upto("attn_sum", b, q - 1))
                else:
                    pe.wait_ge(sem["proj_act"], whole("proj_act", b))
                    pe.wait_ge(sem["proj_dve"], whole("proj_dve", b))
                for k in range(8):
                    h, r = 8 * half + k, k % 2
                    ins = mm(pvb[r * DK:(r + 1) * DK, (k // 2) * T:(k // 2 + 1) * T], vv[:, q, h * DK:(h + 1) * DK],
                             pT[:, 4 * r + k // 2, :], start=True, stop=True)
                ins.then_inc(sem["pv"], 1)

            def b_wo(b, q):
                pe.wait_ge(sem["headsT_sb"], upto("headsT_sb", b, 2 * q + 1))
                for j in range(NCH):
                    ins = mm(pvb[:, 0:P], hT[:, j, :], wo[:, j, :], start=(j == 0), stop=(j == NCH - 1))
                ins.then_inc(sem["wo"], 1)

            def c_x2_T(c):
                pe.wait_ge(sem["ln2_out"], whole("ln2_out", c))
                if later(c):
                    pe.wait_ge(sem["eT_sb"], upto("eT_sb", c - 1, 6))
                for q in range(SEQ):
                    ins = turn(m0[:, q * T:(q + 1) * T], x2[:, q, :])
                ins.then_inc(sem["x2T"], 1)

            def c_router_shared(c):
                pe.wait_ge(sem["x2T_sb"], upto("x2T_sb", c))
                if later(c):
                    pe.wait_ge(sem["moe_sum"], whole("moe_sum", c - 1))
                for k, dst in enumerate((m1, m0)):
                    for q in (2 * k, 2 * k + 1):
                        ins = mm(dst[:, (q % 2) * RS:(q % 2 + 1) * RS], x2T[:, q * T:(q + 1) * T], wrs[:], start=True, stop=True)
                    ins.then_inc(sem["rs"], 1)

            def c_shared_T(c):
                pe.wait_ge(sem["sh_act"], upto("sh_act", c, 1))
                settle(pe)
                for q in range(SEQ):
                    ins = turn(m1[0:I, q * T:(q + 1) * T], ash[:, q, :])
                ins.then_inc(sem["shT"], 1)

            def c_up(c, n):
                q, half = n // 2, (n % 2) * 512
                if n == 0:
                    pe.wait_ge(sem["shT_sb"], upto("shT_sb", c))
                elif n % 2:
                    pe.wait_ge(sem["e_gate"], upto("e_gate", c, n - 1))
                else:
                    pe.wait_ge(sem["eT_sb"], upto("eT_sb", c, n - 2))
                mm(m0[:], x2T[:, q * T:(q + 1) * T], wg[:, half:half + 512], start=True, stop=True).then_inc(sem["eg"], 1)
                if n % 2:
                    pe.wait_ge(sem["e_act"], upto("e_act", c, n - 1))
                elif n:
                    pe.wait_ge(sem["moe_sum"], upto("moe_sum", c, q - 1))
                mm(m1[:], x2T[:, q * T:(q + 1) * T], wu[:, half:half + 512], start=True, stop=True).then_inc(sem["eu"], 1)

            def c_act_T(c, q):
                pe.wait_ge(sem["e_weighted"], upto("e_weighted", c, 2 * q + 1))
                for j in range(E // 2):
                    ins = turn((m0, m1)[j // 4][:, (j % 4) * T:(j % 4 + 1) * T], ew[:, j * P:(j + 1) * P])
                    if j % 4 == 3:
                        ins.then_inc(sem["eT"], 1)

            def c_down(c, q):
                pe.wait_ge(sem["eT_sb"], upto("eT_sb", c, 2 * q + 1))
                for j in range(E // 2):
                    mm(m1[:, 0:P], eT[:, j, :], wd[:, j, :], start=(j == 0), stop=False)
                mm(m1[:, 0:P], sT[:, q * T:(q + 1) * T], wsd[:], start=False, stop=True).then_inc(sem["down"], 1)

            def body(a, b, c):
                A, B, C = a is not None, b is not None, c is not None

                if B:
                    b_project(b, 4, 5)
                    a_ff2(b)
                if C:
                    c_x2_T(c)
                if B:
                    b_project(b, 5, 8)
                if C:
                    c_router_shared(c)
                if B:
                    b_project(b, 8, 9)
                    a_x1_T(b)
                    b_project(b, 9, 16)
                if C:
                    c_shared_T(c)
                if B:
                    b_project(b, 16, 18)
                if A:
                    a_norm_T(a, 0)
                for s in range(PAIRS + LAG):
                    odd = s % 2
                    if B and s >= LAG:
                        b_probs_T(b, s - LAG)
                    if C and s > 1 and not odd:
                        c_act_T(c, s // 2 - 1)
                    if B and s < PAIRS:
                        b_scores(b, s)
                    if A and s == 8:
                        b_project(a, 0, 2)
                    if A and s == 5:
                        a_hid(a)
                    if A and s == 9:
                        a_ff1(a, 0)
                        a_ff1(a, 1)
                    if B and s >= LAG:
                        b_pv(b, s - LAG)
                    if A and s == 8:
                        a_norm_T(a, 2)
                    if B and s < 2:
                        b_project(b, 18 + 3 * s, 21 + 3 * s)
                    if C and s > 1 and not odd:
                        c_down(c, s // 2 - 1)
                    if C and s < PAIRS:
                        c_up(c, s)
                    if A:
                        if s == 1:
                            a_pw(a)
                        elif s == 3:
                            a_norm_T(a, 1)
                        elif s == 4:
                            a_gate(a)
                        elif s == 6:
                            a_scan_T(a)
                        elif s == 8:
                            b_project(a, 2, 4)
                        elif s == 9:
                            a_ff1(a, 2)
                            a_ff1(a, 3)
                    if B and s > LAG and odd:
                        b_wo(b, (s - LAG) // 2)

            pipeline(pe, body)

        @block.scalar
        def _(act):
            f = nc.scalar.activation
            act.wait_ge(sem["gammas"], 1)
            act.wait_ge(sem["bq8"], 1)

            def a_sums(a, n):
                src = (xt, xm, xg)[n]
                if n == 0:
                    act.wait_ge(sem["x_loaded"], whole("x_loaded", a))
                    if later(a):
                        act.wait_ge(sem["floored"], whole("floored", a - 1))
                else:
                    act.wait_ge(sem[("mixed", "gru_sum")[n - 1]], upto(("mixed", "gru_sum")[n - 1], a))
                    act.wait_ge(sem["floored"], upto("floored", a, n - 1))
                for q in range(SEQ):
                    ins = f(sq[:, q, :], src[:, q, :], ACT.Square, accum_out=ss[:, q:q + 1])
                ins.then_inc(sem["sums"], 1)

            def a_norm(a, n):
                act.wait_ge(sem["a_bank"], upto("a_bank", a, A_USE[f'T{n}']))
                gamma = c_(("g_conv", "g_gru", "g_ff")[n])
                if n == 0:
                    if later(a):
                        act.wait_ge(sem["conv0"], upto("conv0", a - 1))
                    dst = xc[:, :, 2:T + 2]
                else:
                    if n == 1:
                        if later(a):
                            act.wait_ge(sem["a_bank"], upto("a_bank", a - 1, A_USE['up3']))
                    else:
                        act.wait_ge(sem["a_bank"], upto("a_bank", a, A_USE['hid']))
                    dst = seqs(nT[:])
                f(dst, seqs(ma[:]), ACT.Identity, scale=gamma).then_inc(sem["normT"], 1)

            def a_gate(a):
                act.wait_ge(sem["a_bank"], upto("a_bank", a, A_USE['gate']))
                if later(a):
                    act.wait_ge(sem["inp"], upto("inp", a - 1))
                f(tg[:], ma[:], ACT.Tanh, scale=0.5).then_inc(sem["gate_tanh"], 1)

            def a_hid(a):
                act.wait_ge(sem["a_bank"], upto("a_bank", a, A_USE['hid']))
                if later(a):
                    act.wait_ge(sem["sig"], upto("sig", a - 1))
                f(th[:], ma[:], ACT.Tanh, scale=0.5).then_inc(sem["hid_tanh"], 1)

            def a_gelu(a, k):
                act.wait_ge(sem["a_bank"], upto("a_bank", a, A_USE[f'up{k}']))
                if k == 0:
                    if later(a):
                        act.wait_ge(sem["a_bank"], upto("a_bank", a - 1, A_USE['ff2']))
                f(hf[:, k, :], ff1_banks[k][:], ACT.Gelu, bias=c_(f"b1_{k}")).then_inc(sem["gelu"], 1)

            def a_x1T(a):
                act.wait_ge(sem["a_bank"], upto("a_bank", a, A_USE['Tx1']))
                if later(a):
                    act.wait_ge(sem["proj"], whole("proj", a - 1))
                f(x1T[:], ma[:], ACT.Copy).then_inc(sem["x1T"], 1)

            def b_project(b, lo, hi):
                for n in range(lo, hi):
                    if n % 2:
                        continue
                    act.wait_ge(sem["proj"], upto("proj", b, n))
                    src = proj_banks[n]
                    kind, j = projections[n]
                    if n == 0:
                        if later(b):
                            act.wait_ge(sem["scores"], whole("scores", b - 1))
                    if n == 8:
                        if later(b):
                            act.wait_ge(sem["pv"], whole("pv", b - 1))
                    if kind == "v":
                        ins = f(vv[:, j // 2, (j % 2) * 512:(j % 2) * 512 + 512], src[0:S, :], ACT.Copy)
                    elif kind == "k":
                        ins = f(kT[:, j, :], src[:, 0:SW], ACT.Identity, bias=c_(f"bk{j}"))
                    else:
                        ins = f(qT[:, j, :], src[:], ACT.Identity, bias=c_(f"bq{j}"), scale=DK ** -0.5)
                    ins.then_inc(sem["proj_act"], 1)

            def b_probs(b, p, r):
                if p >= RING:
                    act.wait_ge(sem["probsT"], upto("probsT", b, 2 * (p - RING) + 1))
                else:
                    if later(b):
                        act.wait_ge(sem["probsT"], upto("probsT", b - 1, 2 * (p + PAIRS - RING) + 1))
                act.wait_ge(sem["negmax"], upto("negmax", b, 2 * p + r))
                for i in range(4):
                    ins = f(pr[:, p % RING, r, i, :], score_banks[r][:, i * S:(i + 1) * S], ACT.Exp,
                            bias=nm[:, p % 2, r, i:i + 1], accum_out=rsum[:, p % 2, r, i, :])
                ins.then_inc(sem["probs"], 1)

            def c_x2T(c):
                act.wait_ge(sem["x2T"], upto("x2T", c))
                if later(c):
                    act.wait_ge(sem["eu"], whole("eu", c - 1))
                f(x2T[:], m0[:], ACT.Copy).then_inc(sem["x2T_sb"], 1)

            def c_router(c):
                act.wait_ge(sem["logits"], upto("logits", c, 1))
                f(rt[:], lg[:], ACT.Tanh, scale=0.5).then_inc(sem["route_tanh"], 1)

            def c_shared(c):
                for k, src in enumerate((m1, m0)):
                    act.wait_ge(sem["rs"], upto("rs", c, k))
                    if k == 0:
                        if later(c):
                            act.wait_ge(sem["sh_gate"], upto("sh_gate", c - 1, 1))
                    v = seqs(src[:, 0:2 * RS], 2)[:, :, E:E + I]
                    f(tsh[:, 2 * k:2 * k + 2, :], v, ACT.Tanh, scale=0.5).then_inc(sem["sh_tanh"], 1)

            def c_sharedT(c):
                act.wait_ge(sem["shT"], upto("shT", c))
                if later(c):
                    act.wait_ge(sem["down"], whole("down", c - 1))
                f(sT[:], m1[0:I, :], ACT.Copy).then_inc(sem["shT_sb"], 1)

            def c_tanh(c, n):
                act.wait_ge(sem["eg"], upto("eg", c, n))
                if n:
                    act.wait_ge(sem["e_gate"], upto("e_gate", c, n - 1))
                f(et[:], m0[:], ACT.Tanh, scale=0.5).then_inc(sem["e_tanh"], 1)

            def c_actT(c, q):
                if q:
                    act.wait_ge(sem["down"], upto("down", c, q - 1))
                for k, src in enumerate((m0, m1)):
                    act.wait_ge(sem["eT"], upto("eT", c, 2 * q + k))
                    f(eT[:, 4 * k:4 * k + 4, :], seqs(src[:]), ACT.Copy).then_inc(sem["eT_sb"], 1)

            def body(a, b, c):
                A, B, C = a is not None, b is not None, c is not None

                if B:
                    b_project(b, 4, 6)
                if C:
                    c_x2T(c)
                if A:
                    a_sums(a, 0)
                if B:
                    b_project(b, 6, 8)
                if C:
                    c_shared(c)
                if B:
                    b_project(b, 8, 9)
                    a_x1T(b)
                    b_project(b, 9, 11)
                if C:
                    c_router(c)
                if B:
                    b_project(b, 11, 16)
                if C:
                    c_sharedT(c)
                if B:
                    b_project(b, 16, 18)
                if A:
                    a_norm(a, 0)
                for s in range(PAIRS + LAG):
                    even = s > 1 and s % 2 == 0
                    if C and even:
                        c_actT(c, s // 2 - 1)
                    if B and s < PAIRS:
                        b_probs(b, s, 0)
                    if B and s < 2:
                        b_project(b, 18 + 4 * s, 19 + 4 * s)
                    if C and s < PAIRS and s % 2:
                        c_tanh(c, s)
                    if B and s < PAIRS:
                        b_probs(b, s, 1)
                    if B and s == 0:
                        b_project(b, 20, 21)
                    if C and s < PAIRS and s % 2 == 0:
                        c_tanh(c, s)
                    if A:
                        if s == 2:
                            a_sums(a, 1)
                        elif s == 3:
                            a_norm(a, 1)
                        elif s == 4:
                            a_gate(a)
                        elif s == 5:
                            a_hid(a)
                        elif s == 7:
                            a_sums(a, 2)
                        elif s == 8:
                            b_project(a, 0, 2)
                            a_norm(a, 2)
                            b_project(a, 2, 4)
                        elif s == 9:
                            for k in range(FCH):
                                a_gelu(a, k)

            pipeline(act, body)

        @block.vector
        def _(dve):
            V = nc.vector

            dve.wait_ge(sem["weights"], WEIGHTS)
            V.memset(xc[:], 0.0).then_inc(sem["pads"], 1)
            dve.wait_ge(sem["pads"], 1)
            V.memset(eps[:], 1e-5).then_inc(sem["powers"], 1)
            V.memset(power[:], -0.5).then_inc(sem["powers"], 1)
            V.tensor_scalar(c_("g_conv", 3), c_("g_conv", 3), 1.0, None, ALU.add).then_inc(sem["gammas"], 1)
            dve.wait_ge(sem["gammas"], 1)
            V.tensor_scalar(c_("bq0", NCH), c_("bq0", NCH), DK ** -0.5, None, ALU.mult).then_inc(sem["bq8"], 1)
            dve.wait_ge(sem["bq8"], 1)
            dve.wait_ge(sem["iota"], 1)
            V.tensor_copy(iota[:], iota_i[:]).then_inc(sem["iotaf"], 1)
            dve.wait_ge(sem["iotaf"], 1)

            def a_floored(a, n):
                dve.wait_ge(sem["sums"], upto("sums", a, n))
                if n:
                    dve.wait_ge(sem["rms"], upto("rms", a, n - 1))
                elif later(a):
                    dve.wait_ge(sem["rms"], whole("rms", a - 1))
                V.tensor_scalar(ssf[:], ss[:], 1.0 / P, 1e-24 / P, ALU.mult, ALU.max).then_inc(sem["floored"], 1)

            def a_conv(a):
                dve.wait_ge(sem["normT"], upto("normT", a, 0))
                if later(a):
                    dve.wait_ge(sem["a_bank"], upto("a_bank", a - 1, A_USE['pw']))
                V.tensor_scalar(cv2[:], xc[:, :, 2:T + 2], c_("dw2"), c_("dwb"), ALU.mult, ALU.add).then_inc(sem["conv2"], 1)
                dve.wait_ge(sem["conv2"], upto("conv2", a))
                V.scalar_tensor_tensor(cv1[:], xc[:, :, 1:T + 1], c_("dw1"), cv2[:], ALU.mult, ALU.add).then_inc(sem["conv1"], 1)
                dve.wait_ge(sem["conv1"], upto("conv1", a))
                V.scalar_tensor_tensor(cv[:], xc[:, :, 0:T], c_("dw0"), cv1[:], ALU.mult, ALU.add).then_inc(sem["conv0"], 1)

            def a_mixed(a):
                dve.wait_ge(sem["a_bank"], upto("a_bank", a, A_USE['pw']))
                dve.wait_ge(sem["x_bpw"], upto("x_bpw", a))
                if later(a):
                    dve.wait_ge(sem["normed"], upto("normed", a - 1, 1))
                V.tensor_tensor(xm[:], seqs(ma[:]), xb[:], ALU.add).then_inc(sem["mixed"], 1)

            def a_gru_keep(a):
                dve.wait_ge(sem["gate_tanh"], upto("gate_tanh", a))
                V.tensor_scalar(keep[:], seqs(tg[:]), -0.5, 0.5, ALU.mult, ALU.add).then_inc(sem["keep"], 1)
                V.tensor_scalar(inp[:], tg[:], 0.5, 0.5, ALU.mult, ALU.add).then_inc(sem["inp"], 1)
                dve.wait_ge(sem["keep"], upto("keep", a))
                V.memset(keep[:, :, 0:1], 0.0).then_inc(sem["keep0"], 1)

            def a_gru_drive(a):
                dve.wait_ge(sem["hid_tanh"], upto("hid_tanh", a))
                V.tensor_scalar(sg[:], th[:], 0.5, 0.5, ALU.mult, ALU.add).then_inc(sem["sig"], 1)
                dve.wait_ge(sem["sig"], upto("sig", a))
                V.scalar_tensor_tensor(cand[:], ma[:], 0.5, sg[:], ALU.add, ALU.max).then_inc(sem["cand"], 1)
                dve.wait_ge(sem["cand"], upto("cand", a))
                dve.wait_ge(sem["inp"], upto("inp", a))
                V.tensor_tensor(drive[:], inp[:], cand[:], ALU.mult).then_inc(sem["drive"], 1)
                dve.wait_ge(sem["drive"], upto("drive", a))

            def a_gru_scan(a):
                dve.wait_ge(sem["keep0"], upto("keep0", a))
                if later(a):
                    dve.wait_ge(sem["a_bank"], upto("a_bank", a - 1, A_USE['Th']))
                V.tensor_tensor_scan(hs[:], keep[:].rearrange("p b t -> p (b t)"), drive[:], 0.0,
                                     ALU.mult, ALU.add).then_inc(sem["scan"], 1)

            def a_gru_sum(a):
                dve.wait_ge(sem["a_bank"], upto("a_bank", a, A_USE['Th']))
                if later(a):
                    dve.wait_ge(sem["x_all"], upto("x_all", a - 1))
                V.tensor_tensor(xg[:], seqs(ma[:]), xm[:], ALU.add).then_inc(sem["gru_sum"], 1)

            def a_mixer(a):
                dve.wait_ge(sem["a_bank"], upto("a_bank", a, A_USE['ff2']))
                dve.wait_ge(sem["x_all"], upto("x_all", a))
                V.tensor_tensor(xr[:], seqs(ma[:]), xz[:], ALU.add).then_inc(sem["mixer"], 1)
                dve.wait_ge(sem["mixer"], upto("mixer", a))
                for q in range(SEQ):
                    V.bn_stats(st1[:, q, :], xr[:, q, :]).then_inc(sem["ln1_stats"], 1)
                for q in range(SEQ):
                    dve.wait_ge(sem["ln1_stats"], upto("ln1_stats", a, q))
                    settle(dve)
                    V.bn_aggr(mv1[:, q, :], st1[:, q, :]).then_inc(sem["ln1_mv"], 1)

            def a_ln1(a):
                dve.wait_ge(sem["ln1_rstd"], upto("ln1_rstd", a))
                if later(a):
                    dve.wait_ge(sem["a_bank"], whole("a_bank", a - 1))
                if later(a):
                    dve.wait_ge(sem["x1_bo"], upto("x1_bo", a - 1))
                for q in range(SEQ):
                    V.tensor_scalar(x1[:, q, :], xr[:, q, :], mv1[:, q, 0:1], rs1[:, q:q + 1],
                                    ALU.subtract, ALU.mult).then_inc(sem["ln1_out"], 1)

            def b_project(b, lo, hi):
                for n in range(lo, hi):
                    if n % 2 == 0:
                        continue
                    dve.wait_ge(sem["proj"], upto("proj", b, n))
                    src = proj_banks[n]
                    kind, j = projections[n]
                    if n == 1:
                        if later(b):
                            dve.wait_ge(sem["scores"], whole("scores", b - 1))
                    if n == 9:
                        if later(b):
                            dve.wait_ge(sem["pv"], whole("pv", b - 1))
                    if kind == "v":
                        ins = V.tensor_copy(vv[:, j // 2, (j % 2) * 512:(j % 2) * 512 + 512], src[0:S, :])
                    elif kind == "k":
                        ins = V.tensor_scalar(kT[:, j, :], src[:, 0:SW], c_(f"bk{j}"), None, ALU.add)
                    else:
                        ins = V.tensor_scalar(qT[:, j, :], src[:], DK ** -0.5, c_(f"bq{j}"), ALU.mult, ALU.add)
                    ins.then_inc(sem["proj_dve"], 1)

            def b_max(b, p):
                for r in range(2):
                    dve.wait_ge(sem["scores"], upto("scores", b, 2 * p + r))
                    V.tensor_reduce(nm[:, p % 2, r, :], seqs(score_banks[r][:, 0:4 * S]), AX_X, ALU.max,
                                    negate=True).then_inc(sem["negmax"], 1)

            def b_probs_T(b, p):
                if p:
                    dve.wait_ge(sem["pv"], upto("pv", b, p - 1))
                else:
                    if later(b):
                        dve.wait_ge(sem["pv"], whole("pv", b - 1))
                for k in range(2):
                    dve.wait_ge(sem["probsT"], upto("probsT", b, 2 * p + k))
                    V.tensor_copy(pT[:, 4 * k:4 * k + 4, :], seqs((t0, t1)[k][0:S, :])).then_inc(sem["probsT_sb"], 1)

            def b_recips(b, p, r):
                dve.wait_ge(sem["probs"], upto("probs", b, 2 * p + r))
                V.reciprocal(ri[:, p % 2, r, :, :], rsum[:, p % 2, r, :, :]).then_inc(sem["rinv"], 1)

            def b_heads_T(b, p):
                half = p % 2
                dve.wait_ge(sem["pv"], upto("pv", b, p))
                if p > 1:
                    dve.wait_ge(sem["wo"], upto("wo", b, p // 2 - 1))
                elif later(b):
                    dve.wait_ge(sem["wo"], whole("wo", b - 1))
                V.tensor_tensor(hT[:, 4 * half:4 * half + 4, :], seqs(pvb[:]),
                                c_(f"bv{4 * half}", 4).unsqueeze(2).to_broadcast([P, 4, T]),
                                ALU.add).then_inc(sem["headsT_sb"], 1)

            def b_sum(b, q):
                dve.wait_ge(sem["wo"], upto("wo", b, q))
                dve.wait_ge(sem["x1_bo"], upto("x1_bo", b))
                V.tensor_tensor(xa[:], pvb[:, 0:P], x1b[:, q, :], ALU.add).then_inc(sem["attn_sum"], 1)
                dve.wait_ge(sem["attn_sum"], upto("attn_sum", b, q))
                V.bn_stats(st2[:], xa[:]).then_inc(sem["ln2_stats"], 1)
                dve.wait_ge(sem["ln2_stats"], upto("ln2_stats", b, q))
                settle(dve)
                V.bn_aggr(mv2[:], st2[:]).then_inc(sem["ln2_mv"], 1)

            def b_ln2(b, q):
                dve.wait_ge(sem["ln2_rstd"], upto("ln2_rstd", b, q))
                if later(b):
                    dve.wait_ge(sem["x2T"], whole("x2T", b - 1))
                V.tensor_scalar(x2[:, q, :], xa[:], mv2[:, 0:1], rs2[:], ALU.subtract, ALU.mult).then_inc(sem["ln2_out"], 1)

            def c_logits(c):
                for k, src in enumerate((m1, m0)):
                    dve.wait_ge(sem["sh_tanh"], upto("sh_tanh", c, k))
                    V.tensor_tensor(lg[:, 2 * k:2 * k + 2, :], seqs(src[:, 0:2 * RS], 2)[:, :, 0:E],
                                    brow["gate"].unsqueeze(1).to_broadcast([P, 2, E]), ALU.add).then_inc(sem["logits"], 1)

            def c_shared(c):
                for k, src in enumerate((m1, m0)):
                    dve.wait_ge(sem["sh_tanh"], upto("sh_tanh", c, k))
                    v = seqs(src[:, 0:2 * RS], 2)
                    sl = slice(2 * k, 2 * k + 2)
                    if k == 0:
                        if later(c):
                            dve.wait_ge(sem["shT"], whole("shT", c - 1))
                    V.scalar_tensor_tensor(gsh[:, sl, :], tsh[:, sl, :], 1.0, v[:, :, E:E + I], ALU.add, ALU.mult).then_inc(sem["sh_gate"], 1)
                    dve.wait_ge(sem["sh_gate"], upto("sh_gate", c, k))
                    V.scalar_tensor_tensor(ash[:, sl, :], gsh[:, sl, :], 0.5, v[:, :, E + I:RS],
                                           ALU.mult, ALU.mult).then_inc(sem["sh_act"], 1)

            def c_route(c):
                dve.wait_ge(sem["route_tanh"], upto("route_tanh", c))
                V.tensor_scalar(sg8[:], rt[:], 0.5, 0.5, ALU.mult, ALU.add).then_inc(sem["route_sig"], 1)
                dve.wait_ge(sem["route_sig"], upto("route_sig", c))
                settle(dve)
                for q in range(SEQ):
                    V.max(mx[:, q, :], sg8[:, q, :]).then_inc(sem["top"], 1)
                for q in range(SEQ):
                    dve.wait_ge(sem["top"], upto("top", c, q))
                    settle(dve)
                    V.max_index(mi[:, q, :], mx[:, q, :], sg8[:, q, :]).then_inc(sem["top_at"], 1)

            def c_gates(c):
                V.tensor_tensor(tsum[:], mx[:, :, 0:1], mx[:, :, 1:2], ALU.add).then_inc(sem["top_sum"], 1)
                dve.wait_ge(sem["top_sum"], upto("top_sum", c))
                dve.wait_ge(sem["top"], whole("top", c))
                dve.wait_ge(sem["top_at"], whole("top_at", c))
                V.tensor_copy(mf[:], mi[:, :, 0:2]).then_inc(sem["top_f"], 1)
                V.reciprocal(trec[:], tsum[:]).then_inc(sem["top_rec"], 1)
                dve.wait_ge(sem["top_rec"], upto("top_rec", c))
                V.scalar_tensor_tensor(tw[:], mx[:, :, 0:2], 0.5, trec[:].to_broadcast([P, SEQ, 2]),
                                       ALU.mult, ALU.mult).then_inc(sem["top_w"], 1)
                dve.wait_ge(sem["top_f"], upto("top_f", c))
                for o, k in ((o0, 0), (o1, 1)):
                    V.tensor_tensor(o[:], over_seqs(iota[:]), mf[:, :, k:k + 1].to_broadcast([P, SEQ, E]),
                                    ALU.is_equal).then_inc(sem[f"one{k}"], 1)
                dve.wait_ge(sem["top_w"], upto("top_w", c))
                for o, w, k in ((o0, q0, 0), (o1, q1, 1)):
                    dve.wait_ge(sem[f"one{k}"], upto(f"one{k}", c))
                    V.tensor_tensor(w[:], o[:], tw[:, :, k:k + 1].to_broadcast([P, SEQ, E]), ALU.mult).then_inc(sem[f"w{k}"], 1)
                dve.wait_ge(sem["w0"], upto("w0", c))
                dve.wait_ge(sem["w1"], upto("w1", c))
                if later(c):
                    dve.wait_ge(sem["e_weighted"], whole("e_weighted", c - 1))
                V.tensor_tensor(gw[:], q0[:], q1[:], ALU.add).then_inc(sem["gates"], 1)

            def c_experts(c, n):
                dve.wait_ge(sem["e_tanh"], upto("e_tanh", c, n))
                if n:
                    dve.wait_ge(sem["e_act"], upto("e_act", c, n - 1))
                V.scalar_tensor_tensor(e1[:], et[:], 1.0, m0[:], ALU.add, ALU.mult).then_inc(sem["e_gate"], 1)
                dve.wait_ge(sem["e_gate"], upto("e_gate", c, n))
                dve.wait_ge(sem["eu"], upto("eu", c, n))
                if n >= 2:
                    dve.wait_ge(sem["e_weighted"], upto("e_weighted", c, n - 2))
                else:
                    if later(c):
                        dve.wait_ge(sem["e_weighted"], upto("e_weighted", c - 1, n + 6))
                V.tensor_tensor(e3[:, n % 2, :], e1[:], m1[:], ALU.mult).then_inc(sem["e_act"], 1)

            def c_sum(c, q):
                dve.wait_ge(sem["down"], upto("down", c, q))
                V.scalar_tensor_tensor(ys[:], x2[:, q, :], 2.0, m1[:, 0:P], ALU.mult, ALU.add).then_inc(sem["moe_sum"], 1)
                dve.wait_ge(sem["moe_sum"], upto("moe_sum", c, q))
                V.bn_stats(st3[:], ys[:]).then_inc(sem["ln3_stats"], 1)
                dve.wait_ge(sem["ln3_stats"], upto("ln3_stats", c, q))
                settle(dve)
                V.bn_aggr(mv3[:], st3[:]).then_inc(sem["ln3_mv"], 1)

            def c_ln3(c, q):
                dve.wait_ge(sem["ln3_rstd"], upto("ln3_rstd", c, q))
                if later(c):
                    dve.wait_ge(sem[f"out{q}_stored"], upto(f"out{q}_stored", c - 1))
                V.tensor_scalar(y[:, q, :], ys[:], mv3[:, 0:1], rs3[:], ALU.subtract, ALU.mult).then_inc(sem["ln3_out"], 1)

            def body(a, b, c):
                A, B, C = a is not None, b is not None, c is not None

                if B:
                    a_mixer(b)
                    b_project(b, 4, 8)
                    a_ln1(b)
                if A:
                    a_floored(a, 0)
                if B:
                    b_project(b, 8, 10)
                if C:
                    c_logits(c)
                    c_shared(c)
                if B:
                    b_project(b, 10, 16)
                if C:
                    c_route(c)
                if B:
                    b_project(b, 16, 18)
                if C:
                    c_gates(c)
                for s in range(PAIRS + LAG):
                    odd = s % 2
                    if B and s >= LAG:
                        b_probs_T(b, s - LAG)
                    if B and s < PAIRS:
                        b_max(b, s)
                    if B and s > LAG + 1 and not odd:
                        b_ln2(b, (s - LAG) // 2 - 1)
                    if A and s == 0:
                        a_conv(a)
                    if A and s == 8:
                        b_project(a, 0, 2)
                    if B and s < 2:
                        b_project(b, 19 + 2 * s, 20 + 2 * s)
                    if A and s == 6:
                        a_gru_scan(a)
                    if B and s >= LAG:
                        b_heads_T(b, s - LAG)
                    if B and s < PAIRS:
                        b_recips(b, s, 0)
                    if C and s > 1 and not odd:
                        c_sum(c, s // 2 - 1)
                    if B and s == 1:
                        b_project(b, 23, 24)
                    if C and odd and s < PAIRS:
                        c_experts(c, s)
                    if B and s < PAIRS:
                        b_recips(b, s, 1)
                    if C and not odd and s < PAIRS:
                        c_experts(c, s)
                    if C and s > 1 and not odd:
                        c_ln3(c, s // 2 - 1)
                    if A:
                        if s == 1:
                            a_mixed(a)
                        elif s == 2:
                            a_floored(a, 1)
                        elif s == 4:
                            a_gru_keep(a)
                        elif s == 5:
                            a_gru_drive(a)
                        elif s == 6:
                            a_gru_sum(a)
                        elif s == 7:
                            a_floored(a, 2)
                        elif s == 8:
                            b_project(a, 2, 4)
                    if B and s > LAG and odd:
                        b_sum(b, (s - LAG) // 2)
                if B:
                    b_ln2(b, SEQ - 1)

            pipeline(dve, body)

        @block.gpsimd
        def _(pool):
            GP = nc.gpsimd
            GP.memset(ident[:], 0.0).then_inc(sem["ones"], 1)
            GP.memset(maskb[:], 0.0).then_inc(sem["mask0"], 1)
            pool.wait_ge(sem["ones"], 1)
            GP.affine_select(out=ident[:], in_=ident[:], pattern=[[-1, P]], compare_op=ALU.not_equal, fill=1.0,
                             base=0, channel_multiplier=1).then_inc(sem["ident"], 1)
            pool.wait_ge(sem["ident"], 1)
            GP.tensor_copy(identb[:], ident[:]).then_inc(sem["identb"], 1)
            pool.wait_ge(sem["mask0"], 1)
            GP.affine_select(out=maskb[:], in_=maskb[:], pattern=[[-1, S]], compare_op=ALU.is_ge, fill=-1e10,
                             base=0, channel_multiplier=1).then_inc(sem["mask"], 1)
            GP.iota(iota_i[:], pattern=[[1, E]], base=0, channel_multiplier=0).then_inc(sem["iota"], 1)
            pool.wait_ge(sem["weights"], WEIGHTS)
            pool.wait_ge(sem["powers"], 2)

            def a_normed(a, n):
                src = (xt, xm, xg)[n]
                pool.wait_ge(sem["floored"], upto("floored", a, n))
                GP.tensor_tensor(rr[:], ssf[:], power[:], ALU.pow).then_inc(sem["rms"], 1)
                pool.wait_ge(sem["rms"], upto("rms", a, n))
                if n:
                    pool.wait_ge(sem["a_bank"], upto("a_bank", a, A_USE[f'T{n - 1}']))
                else:
                    if later(a):
                        pool.wait_ge(sem["a_bank"], upto("a_bank", a - 1, A_USE['T2']))
                GP.tensor_tensor(xn[:], src[:], rr[:].unsqueeze(2).to_broadcast([P, SEQ, P]), ALU.mult).then_inc(sem["normed"], 1)

            def a_residuals(a):
                if later(a):
                    pool.wait_ge(sem["mixed"], upto("mixed", a - 1))
                GP.tensor_tensor(xb[:], xt[:], over_seqs(brow["pw"]), ALU.add).then_inc(sem["x_bpw"], 1)
                GP.tensor_tensor(xf[:], xt[:], over_seqs(brow["ff2"]), ALU.add).then_inc(sem["x_bff"], 1)

            def a_all(a):
                pool.wait_ge(sem["gru_sum"], upto("gru_sum", a))
                pool.wait_ge(sem["x_bff"], upto("x_bff", a))
                if later(a):
                    pool.wait_ge(sem["mixer"], upto("mixer", a - 1))
                GP.tensor_tensor(xz[:], xf[:], xg[:], ALU.add).then_inc(sem["x_all"], 1)

            def a_ln1(a):
                pool.wait_ge(sem["ln1_mv"], whole("ln1_mv", a))
                GP.tensor_tensor(ve1[:], mv1[:, :, 1], eps[:], ALU.add).then_inc(sem["ln1_eps"], 1)
                pool.wait_ge(sem["ln1_eps"], upto("ln1_eps", a))
                GP.tensor_tensor(rs1[:], ve1[:], power[:], ALU.pow).then_inc(sem["ln1_rstd"], 1)

            def a_x1_bo(a):
                pool.wait_ge(sem["ln1_out"], whole("ln1_out", a))
                if later(a):
                    pool.wait_ge(sem["attn_sum"], whole("attn_sum", a - 1))
                GP.tensor_tensor(x1b[:], x1[:], over_seqs(brow["bo"]), ALU.add).then_inc(sem["x1_bo"], 1)

            def b_normal(b, p, r):
                pool.wait_ge(sem["rinv"], upto("rinv", b, 2 * p + r))
                GP.tensor_tensor(pr[:, p % RING, r, :, :], pr[:, p % RING, r, :, :],
                                 ri[:, p % 2, r, :, :].to_broadcast([P, 4, S]), ALU.mult).then_inc(sem["normal"], 1)

            def ln(g, q, n, mv, ve, rs):
                pool.wait_ge(sem[f"ln{n}_mv"], upto(f"ln{n}_mv", g, q))
                GP.tensor_tensor(ve[:], mv[:, 1:2], eps[:, 0:1], ALU.add).then_inc(sem[f"ln{n}_eps"], 1)
                pool.wait_ge(sem[f"ln{n}_eps"], upto(f"ln{n}_eps", g, q))
                GP.tensor_tensor(rs[:], ve[:], power[:, 0:1], ALU.pow).then_inc(sem[f"ln{n}_rstd"], 1)

            def c_weight(c, n):
                pool.wait_ge(sem["gates"], upto("gates", c))
                pool.wait_ge(sem["e_act"], upto("e_act", c, n))
                if n >= 2:
                    pool.wait_ge(sem["eT"], upto("eT", c, 2 * (n // 2 - 1) + 1))
                else:
                    if later(c):
                        pool.wait_ge(sem["eT"], whole("eT", c - 1))
                half = n % 2
                GP.tensor_tensor(seqs(ew[:, half * 512:(half + 1) * 512], 8), seqs(e3[:, n % 2, :], 8),
                                 gw[:, n // 2, 8 * half:8 * half + 8].unsqueeze(2).to_broadcast([P, 8, I]),
                                 ALU.mult).then_inc(sem["e_weighted"], 1)

            def body(a, b, c):
                A, B, C = a is not None, b is not None, c is not None
                if B:
                    a_ln1(b)
                if A:
                    a_normed(a, 0)
                if B:
                    a_x1_bo(b)
                if A:
                    a_residuals(a)
                for s in range(PAIRS + LAG):
                    odd = s % 2
                    if B and s < PAIRS:
                        b_normal(b, s, 0)
                    if C and odd and s < PAIRS:
                        c_weight(c, s)
                    if B and s < PAIRS:
                        b_normal(b, s, 1)
                    if C and s > 1 and not odd:
                        ln(c, s // 2 - 1, 3, mv3, ve3, rs3)
                    if C and not odd and s < PAIRS:
                        c_weight(c, s)
                    if B and s > LAG and odd:
                        ln(b, (s - LAG) // 2, 2, mv2, ve2, rs2)
                    if A:
                        if s == 2:
                            a_normed(a, 1)
                        elif s == 7:
                            a_normed(a, 2)
                            a_all(a)

            pipeline(pool, body)


def kernel(**inputs):
    import numpy as np
    import concourse.bacc as bacc
    from concourse.bass_utils import run_bass_kernel_spmd

    a = {n: np.asarray(v) for n, v in inputs.items()}
    L, X, M = "L0_attn_", "L0_xattn_", "L0_ffn_"

    def chunks(v):
        return v.reshape(-1, P, *v.shape[1:]).swapaxes(0, 1)

    laid = {
        "x": a["x"],
        "ctxT": a["ctx_1024"].reshape(G, SEQ, S, P).transpose(0, 3, 1, 2).reshape(G, P, SW),
        "w_pw": a[L + "conv_pw_w"].T,
        "w_gru": a[L + "gru_w"].T,
        "w_ff1": a[L + "ff_w1"].T,
        "w_ff2": chunks(a[L + "ff_w2"].T),
        "cols": np.concatenate([a[L + "conv_dw_w"][:, 0, :], a[L + "conv_dw_b"][:, None], a[L + "conv_norm_g"][:, None],
                                a[L + "gru_norm_g"][:, None], a[L + "ff_norm_g"][:, None], chunks(a[L + "ff_b1"]),
                                chunks(a[X + "bq"]), chunks(a[X + "bk"]), chunks(a[X + "bv"])], axis=1),
        "rows": np.concatenate([a[L + "conv_pw_b"], a[L + "ff_b2"], a[X + "bo"], a[M + "gate_b"]])[None, :],
        "w_q": a[X + "Wq"], "w_k": a[X + "Wk"], "w_v": a[X + "Wv"], "w_o": chunks(a[X + "Wo"]),
        "w_g": a[M + "experts_wg"].transpose(1, 0, 2).reshape(P, E * I),
        "w_u": a[M + "experts_wu"].transpose(1, 0, 2).reshape(P, E * I),
        "w_rs": np.concatenate([a[M + "gate_w"], a[M + "shared_wg"], a[M + "shared_wu"]], axis=1),
        "w_d": chunks(a[M + "experts_wd"].reshape(E * I, P)),
        "w_sd": a[M + "shared_wd"],
    }
    nc = bacc.Bacc("TRN2", target_bir_lowering=False, num_devices=1)
    arrays, aps = {}, {}
    for name, v in laid.items():
        arrays[f"in_{name}"] = np.ascontiguousarray(v)
        aps[name] = nc.dram_tensor(f"in_{name}", v.shape, F32, kind="ExternalInput").ap()
    aps["out"] = nc.dram_tensor("out_y", [NSEQ, T, P], F32, kind="ExternalOutput").ap()
    layer_kernel(nc, **aps)
    r = run_bass_kernel_spmd(nc, [arrays], core_ids=[0])
    return r.results[0]["out_y"]
```

```python
from contextlib import ExitStack

import concourse.bass as bass
from concourse import mybir

ALU = mybir.AluOpType
ACT = mybir.ActivationFunctionType
F32 = mybir.dt.float32
BF16 = mybir.dt.bfloat16
U32 = mybir.dt.uint32
F32R = mybir.dt.float32r
AX_X = mybir.AxisListType.X

P = 128
T = 128
NSEQ = 64
SEQ = 4
G = NSEQ // SEQ
S = 120
H = 16
DK = 64
NCH = H * DK // P
E = 16
I = 64
F = 512
FCH = F // P
W = SEQ * T
SW = SEQ * S
PAIRS = 2 * SEQ
LAG = 2
RING = LAG + 1
RS = E + 2 * I

COLS = ["dw0", "dw1", "dw2", "dwb", "g_conv", "g_gru", "g_ff"] + [f"b1_{c}" for c in range(FCH)] + \
    [f"bq{j}" for j in range(NCH)] + [f"bk{j}" for j in range(NCH)] + [f"bv{j}" for j in range(NCH)]
ROWS = 3 * P + E

PER_GROUP = {
    "x_loaded": 16, "ctx_loaded": 16, "out0_stored": 16, "out1_stored": 16, "out2_stored": 16, "out3_stored": 16,
    "sums": 3, "floored": 3, "rms": 3, "normed": 3, "x_bpw": 1, "x_bff": 1, "x_all": 1,
    "a_bank": 14, "normT": 3, "normT_lo": 2, "conv2": 1, "conv1": 1, "conv0": 1, "mixed": 1,
    "gate_tanh": 1, "hid_tanh": 1, "keep": 1, "keep0": 1, "inp": 1, "sig": 1, "cand": 1, "drive": 1, "scan": 1,
    "gru_sum": 1, "gelu": 4, "mixer": 2,
    "ln1_stats": 4, "ln1_mv": 4, "ln1_eps": 1, "ln1_rstd": 1, "ln1_out": 4, "x1T_hi": 1, "x1T": 1, "x1_bo": 1,
    "ctx_hi": 1, "ctx_split": 1, "proj": 24, "proj_act": 12, "proj_dve": 12, "scores": 16, "negmax": 16, "probs": 16,
    "probsT": 16, "probsT_sb": 16, "rinv": 16, "normal": 16, "pv": 8, "headsT_sb": 8,
    "wo": 4, "attn_sum": 4, "ln2_stats": 4, "ln2_mv": 4, "ln2_eps": 4, "ln2_rstd": 4, "ln2_out": 4,
    "x2T": 1, "x2T_hi": 1, "x2T_sb": 1, "rs": 2, "logits": 2, "route_tanh": 1, "route_sig": 1, "top": 4, "top_at": 4,
    "top_f": 1, "top_sum": 1, "top_rec": 1, "top_w": 1, "one0": 1, "one1": 1, "w0": 1, "w1": 1, "gates": 1,
    "sh_tanh": 2, "sh_gate": 2, "sh_act": 2, "shT": 1, "shT_sb": 1,
    "eg": 8, "eu": 8, "e_tanh": 8, "e_gate": 8, "e_act": 8, "e_weighted": 8, "eT": 8, "eT_sb": 8,
    "down": 4, "moe_sum": 4, "ln3_stats": 4, "ln3_mv": 4, "ln3_eps": 4, "ln3_rstd": 4, "ln3_out": 4,
}
SPLIT = ["gru", "ff1", "wk", "wv", "wq", "wrs", "wg", "wu"]
LATE_LOADS = ["wk", "wv", "wq", "ff2", "wo", "wrs", "wg", "wu", "wd", "wsd"]
ONCE = ["waits_held", "mixer_weights", *[f"{n}_in" for n in LATE_LOADS], "w_hi", "w_lo", "ident", "identb", "mask0", "mask", "iota", "iotaf", "ones", "gammas", "bq8", "powers", "pads"]

A_USE = {n: k for k, n in enumerate(
    ["T0", "pw", "T1", "gate", "hid", "Th", "T2"] + [f"up{k}" for k in range(FCH)] + ["ff2_0", "ff2_1", "Tx1"])}


def layer_kernel(nc, x, ctxT, w_pw, w_gru, w_ff1, w_ff2, cols, rows, w_q, w_k, w_v, w_o, w_g, w_u, w_rs, w_d, w_sd, out):
    with ExitStack() as ctx:
        def sb(name, shape, dt=F32):
            return ctx.enter_context(nc.sbuf_tensor(name, shape, dt))

        sem = {n: ctx.enter_context(nc.semaphore(n)) for n in [*PER_GROUP, *ONCE]}

        def later(g):
            return not (isinstance(g, int) and g == 0)

        def upto(name, g, k=0):
            return g * PER_GROUP[name] + (k + 1) * (16 if name.endswith(("loaded", "stored")) else 1)

        def whole(name, g):
            return g * PER_GROUP[name] + PER_GROUP[name]

        def settle(eng):
            eng.sem_inc(sem["waits_held"], 1)

        def pair(name, shape):
            return sb(f"{name}_hi", shape, F32R), sb(f"{name}_lo", shape, F32R)

        pw = sb("pw", [P, P]); ff2 = sb("ff2", [P, FCH, P])
        wo = sb("wo", [P, NCH, P])
        wd = sb("wd", [P, E // 2, P]); wsd = sb("wsd", [I, P])
        width = {"gru": 2 * P, "ff1": F, "wk": H * DK, "wv": H * DK, "wq": H * DK, "wrs": RS, "wg": E * I, "wu": E * I}
        split = {n: pair(f"{n}_s", [P, width[n]]) for n in SPLIT}
        col = sb("col", [P, len(COLS)]); row = sb("row", [P, ROWS])
        ident = sb("ident_f", [P, P]); identb = sb("ident_b", [P, P], BF16); maskb = sb("mask_b", [P, S], BF16)
        iota_i = sb("iota_i", [P, E], mybir.dt.int32); iota = sb("iota_f", [P, E])
        power = sb("power", [P, SEQ])

        eps = sb("eps", [P, SEQ])
        xt = sb("xt", [P, SEQ, P]); ss = sb("ss", [P, SEQ]); ssf = sb("ssf", [P, SEQ])
        rr = sb("rr", [P, SEQ]); xn = sb("xn", [P, SEQ, P]); xz = sb("xz", [P, SEQ, P])
        xc = sb("xc", [P, SEQ, T + 2])
        cv = sb("cv", [P, SEQ, T])
        xm = sb("xm", [P, SEQ, P]); nT = pair("nT", [P, W])
        gin = sb("gin", [P, W])
        hin = sb("hin", [P, W])
        keep = sb("keep_sb", [P, SEQ, T]); hs = sb("hs", [P, W])
        xg = sb("xg", [P, SEQ, P]); hf = sb("hf", [P, FCH, W])
        st1 = sb("st1", [P, SEQ, 6]); mv1 = sb("mv1", [P, SEQ, 2]); ve1 = sb("ve1", [P, SEQ]); rs1 = sb("rs1", [P, SEQ])
        x1 = sb("x1", [P, SEQ, P]); x1T = pair("x1T_s", [P, W]); x1b = sb("x1b", [P, SEQ, P])
        cT = sb("cT", [P, SW]); cS = pair("cS", [P, SW])
        vv = sb("vv", [S, SEQ, H * DK]); kT = sb("kT", [P, NCH, SW]); qT = sb("qT", [P, NCH, W])
        nm = sb("nm", [P, 2, 2, 4]); pr = sb("pr", [P, RING, 2, 4, S]); rsum = sb("rsum", [P, 2, 2, 4, 1])
        pT = sb("pT", [S, 8, T]); ri = sb("ri", [P, 2, 2, 4, 1]); hT = sb("hT", [P, NCH, T])
        xa = sb("xa", [P, P]); st2 = sb("st2", [P, 6]); mv2 = sb("mv2", [P, 2]); ve2 = sb("ve2", [P, 1]); rs2 = sb("rs2", [P, 1])
        x2 = sb("x2", [P, SEQ, P])
        x2T = pair("x2T_s", [P, W]); lg = sb("lg", [P, SEQ, E]); rt = sb("rt", [P, SEQ, E]); sg8 = sb("sg8", [P, SEQ, E])
        mx = sb("mx", [P, SEQ, 8]); mi = sb("mi", [P, SEQ, 8], U32); mf = sb("mf", [P, SEQ, 2])
        tsum = sb("tsum", [P, SEQ, 1]); trec = sb("trec", [P, SEQ, 1]); tw = sb("tw", [P, SEQ, 2])
        o0 = sb("o0", [P, SEQ, E]); o1 = sb("o1", [P, SEQ, E]); q0 = sb("q0", [P, SEQ, E]); q1 = sb("q1", [P, SEQ, E])
        gw = sb("gw", [P, SEQ, E])
        ash = sb("ash", [P, SEQ, I]); sT = sb("sT", [I, W])
        et = sb("et", [P, 512]); e3 = sb("e3", [P, 2, 512]); ew = sb("ew", [P, E * I])
        eT = sb("eT_s", [P, E // 2, T]); ys = sb("ys", [P, P])
        st3 = sb("st3", [P, 6]); mv3 = sb("mv3", [P, 2]); ve3 = sb("ve3", [P, 1]); rs3 = sb("rs3", [P, 1])
        y = sb("y", [P, SEQ, P])

        raw, flat = {}, lambda tile: tile[:].rearrange("p b n -> p (b n)")
        for buffer, names in ((flat(qT), ("wv", "wq", "wg", "wu")), (flat(hT), ("wk",)), (flat(eT), ("gru", "ff1", "wrs"))):
            at = 0
            for n in names:
                raw[n] = buffer[:, at:at + width[n]]
                at += width[n]

        def bank(name):
            return ctx.enter_context(nc.psum_tensor(name, [P, 512], F32))

        sE, sO, t0, t1, pvb = bank("sE"), bank("sO"), bank("t0"), bank("t1"), bank("pvb")
        m0, m1 = bank("m0"), bank("m1")
        ma = bank("ma")
        projections = [("k", j) for j in range(8)] + [("v", j) for j in range(4)] + \
            [("q", j) for j in range(8)] + [("v", j) for j in range(4, 8)]
        proj_banks = [sE, sO, sE, sO] + [(t0, t1, pvb, sE, sO)[n % 5] for n in range(10)] + [(t0, t1, pvb)[n % 3] for n in range(10)]
        ff1_banks = [ma, sE, sO, m0]
        ff2_banks = [sE, ma]
        score_banks = [sE, sO]

        def seqs(ap, n=SEQ):
            return ap.rearrange("p (b n) -> p b n", b=n)

        def c_(name, n=1):
            k = COLS.index(name)
            return col[:, k:k + n]

        brow = {"pw": row[:, 0:P], "ff2": row[:, P:2 * P], "bo": row[:, 2 * P:3 * P], "gate": row[:, 3 * P:3 * P + E]}

        def over_seqs(ap):
            return ap.unsqueeze(1).to_broadcast([P, SEQ, ap.shape[1]])

        def staged(name, src):
            return raw[name], src

        mixer_loads = [(col[:], cols), (row[:], rows.to_broadcast([P, ROWS])), (pw[:], w_pw),
                       staged("gru", w_gru), staged("ff1", w_ff1)]
        MIXER_WEIGHTS = 16 * len(mixer_loads)
        late_loads = {"wk": staged("wk", w_k), "wv": staged("wv", w_v), "wq": staged("wq", w_q),
                      "ff2": (ff2[:], w_ff2), "wo": (wo[:], w_o),
                      "wrs": staged("wrs", w_rs), "wg": staged("wg", w_g), "wu": staged("wu", w_u), "wd": (wd[:], w_d), "wsd": (wsd[:], w_sd)}

        block = ctx.enter_context(nc.Block())

        def pipeline(eng, body):
            body(0, None, None)
            body(1, 0, None)
            body(2, 1, 0)
            with eng.Fori(2, G - 1) as i:
                body(i + 1, i, i - 1)
            body(None, G - 1, G - 2)
            body(None, None, G - 1)

        @block.sync
        def _(sp):
            for dst, src in mixer_loads:
                sp.dma_start(dst, src).then_inc(sem["mixer_weights"], 16)

            def body(a, b, c):
                if a is not None:
                    for n in ("sums", "normed", "x_bpw", "x_bff"):
                        if later(a):
                            sp.wait_ge(sem[n], upto(n, a - 1, 0))
                        settle(sp)
                    sp.dma_start(xt[:], x[bass.ds(a * SEQ, SEQ)].rearrange("b t d -> t b d")).then_inc(sem["x_loaded"], 16)
                    if later(a):
                        sp.wait_ge(sem["ctx_split"], whole("ctx_split", a - 1))
                    settle(sp)
                    sp.dma_start(cT[:], ctxT[bass.ds(a, 1)].rearrange("o d s -> d (o s)")).then_inc(sem["ctx_loaded"], 16)
                    if not later(a):
                        for n in LATE_LOADS:
                            dst, src = late_loads[n]
                            sp.dma_start(dst, src).then_inc(sem[f"{n}_in"], 16)
                if c is not None:
                    for q in range(SEQ):
                        sp.wait_ge(sem["ln3_out"], upto("ln3_out", c, q))
                        settle(sp)
                        sp.dma_start(out[bass.ds(c * SEQ + q, 1)].rearrange("b t d -> (b t) d"),
                                     y[:, q, :]).then_inc(sem[f"out{q}_stored"], 16)

            pipeline(sp, body)
            for q in range(SEQ):
                sp.wait_ge(sem[f"out{q}_stored"], whole(f"out{q}_stored", G - 1))

        @block.tensor
        def _(pe):
            mm = nc.tensor.matmul
            pe.wait_ge(sem["mixer_weights"], MIXER_WEIGHTS)
            pe.wait_ge(sem["ident"], 1)
            pe.wait_ge(sem["identb"], 1)
            pe.wait_ge(sem["mask"], 1)

            def turn(dst, src):
                return nc.tensor.transpose(dst, src, ident[0:src.shape[0], 0:src.shape[0]])

            def product(dst, lhsT, rhs):
                mm(dst, lhsT[0], rhs[0], start=True, stop=False)
                mm(dst, lhsT[0], rhs[1], start=False, stop=False)
                return mm(dst, lhsT[1], rhs[0], start=False, stop=True)

            def cols_of(operand, lo, hi):
                return [part[:, lo:hi] for part in operand]

            def a_norm_T(a, n):
                pe.wait_ge(sem["normed"], upto("normed", a, n))
                if n == 0:
                    if later(a):
                        pe.wait_ge(sem["x1T"], whole("x1T", a - 1))
                elif n == 1:
                    pe.wait_ge(sem["mixed"], upto("mixed", a))
                else:
                    pe.wait_ge(sem["gru_sum"], upto("gru_sum", a))
                for q in range(SEQ):
                    ins = turn(ma[:, q * P:(q + 1) * P], xn[:, q, :])
                ins.then_inc(sem["a_bank"], 1)

            def a_pw(a):
                pe.wait_ge(sem["conv0"], upto("conv0", a))
                pe.wait_ge(sem["normT"], upto("normT", a, 0))
                for q in range(SEQ):
                    ins = mm(ma[:, q * P:(q + 1) * P], cv[:, q, :], pw[:], start=True, stop=True)
                ins.then_inc(sem["a_bank"], 1)

            def a_gate(a):
                if not later(a):
                    pe.wait_ge(sem["w_lo"], SPLIT.index("gru") + 1)
                pe.wait_ge(sem["normT_lo"], upto("normT_lo", a, 0))
                product(ma[:], cols_of(split["gru"], P, 2 * P), cols_of(nT, 0, W)).then_inc(sem["a_bank"], 1)

            def a_hid(a):
                pe.wait_ge(sem["gate_tanh"], upto("gate_tanh", a))
                product(ma[:], cols_of(split["gru"], 0, P), cols_of(nT, 0, W)).then_inc(sem["a_bank"], 1)

            def a_scan_T(a):
                pe.wait_ge(sem["scan"], upto("scan", a))
                pe.wait_ge(sem["hid_tanh"], upto("hid_tanh", a))
                for q in range(SEQ):
                    ins = turn(ma[:, q * P:(q + 1) * P], hs[:, q * T:(q + 1) * T])
                ins.then_inc(sem["a_bank"], 1)

            def a_ff1(a, f, c=None):
                if f == 0:
                    if not later(a):
                        pe.wait_ge(sem["w_lo"], SPLIT.index("ff1") + 1)
                    pe.wait_ge(sem["normT_lo"], upto("normT_lo", a, 1))
                elif f == 1:
                    pe.wait_ge(sem["proj_act"], upto("proj_act", a, 1))
                elif f == 2:
                    pe.wait_ge(sem["proj_dve"], upto("proj_dve", a, 1))
                elif c is not None:
                    pe.wait_ge(sem["eT_sb"], upto("eT_sb", c, 6))
                product(ff1_banks[f][:], cols_of(split["ff1"], f * P, (f + 1) * P), cols_of(nT, 0, W)).then_inc(sem["a_bank"], 1)

            def a_ff2(a):
                if not later(a):
                    pe.wait_ge(sem["ff2_in"], 16)
                pe.wait_ge(sem["gelu"], whole("gelu", a))
                for q in range(SEQ):
                    for f in range(FCH):
                        ins = mm(ff2_banks[q // 2][:, q * P:(q + 1) * P], hf[:, f, q * T:(q + 1) * T], ff2[:, f, :],
                                 start=(f == 0), stop=(f == FCH - 1))
                    if q % 2:
                        ins.then_inc(sem["a_bank"], 1)

            def a_x1_T(a):
                for q in range(SEQ):
                    pe.wait_ge(sem["ln1_out"], upto("ln1_out", a, q))
                    ins = turn(ma[:, q * P:(q + 1) * P], x1[:, q, :])
                ins.then_inc(sem["a_bank"], 1)

            def proj_free(b, n):
                former = [m for m in range(n) if proj_banks[m] is proj_banks[n]]
                if n == 7:
                    pe.wait_ge(sem["mixer"], upto("mixer", b, 0))
                elif n == 8:
                    pe.wait_ge(sem["gelu"], upto("gelu", b, 2))
                elif former:
                    other = "proj_dve" if former[-1] % 2 else "proj_act"
                    pe.wait_ge(sem[other], upto(other, b, former[-1] // 2))
                elif n < 2:
                    if later(b):
                        pe.wait_ge(sem["probs"], upto("probs", b - 1, 14 + n))
                elif n < 6:
                    if later(b):
                        pe.wait_ge(sem["probsT_sb"], upto("probsT_sb", b - 1, 14 + n - 4))
                else:
                    if later(b):
                        pe.wait_ge(sem["attn_sum"], whole("attn_sum", b - 1))

            def b_project(b, lo, hi):
                for n in range(lo, hi):
                    proj_free(b, n)
                    dst = proj_banks[n]
                    kind, j = projections[n]
                    if n == 0:
                        pe.wait_ge(sem["ctx_split"], whole("ctx_split", b))
                    if j == 0 and not later(b):
                        pe.wait_ge(sem["w_lo"], SPLIT.index(f"w{kind}") + 1)
                    if kind == "v":
                        q, half = j // 2, (j % 2) * 512
                        ins = product(dst[0:S, :], cols_of(cS, q * S, (q + 1) * S), cols_of(split["wv"], half, half + 512))
                    elif kind == "k":
                        ins = product(dst[:, 0:SW], cols_of(split["wk"], j * P, (j + 1) * P), cols_of(cS, 0, SW))
                    else:
                        if j == 0:
                            pe.wait_ge(sem["x1T"], whole("x1T", b))
                        ins = product(dst[:], cols_of(split["wq"], j * P, (j + 1) * P), cols_of(x1T, 0, W))
                    ins.then_inc(sem["proj"], 1)

            def b_scores(b, p):
                q, half = p // 2, p % 2
                if p == 0:
                    pe.wait_ge(sem["proj_act"], upto("proj_act", b, 14 // 2))
                    pe.wait_ge(sem["proj_dve"], upto("proj_dve", b, 15 // 2))
                elif p == 1:
                    pe.wait_ge(sem["proj_act"], upto("proj_act", b, 18 // 2))
                    pe.wait_ge(sem["proj_dve"], upto("proj_dve", b, 19 // 2))
                if p:
                    pe.wait_ge(sem["probs"], upto("probs", b, 2 * p - 1))
                for r in range(2):
                    mm(score_banks[r][:, 0:4 * S], identb[:], maskb[:].unsqueeze(1).to_broadcast([P, 4, S]),
                       start=True, stop=False, skip_group_check=True)
                for i in range(4):
                    j = 4 * half + i
                    for r in range(2):
                        ins = mm(score_banks[r][:, i * S:(i + 1) * S], qT[r * DK:(r + 1) * DK, j, q * T:(q + 1) * T],
                                 kT[r * DK:(r + 1) * DK, j, q * S:(q + 1) * S], start=False, stop=True,
                                 skip_group_check=True)
                        if i == 3:
                            ins.then_inc(sem["scores"], 1)

            def b_probs_T(b, p):
                for r in range(2):
                    if p:
                        pe.wait_ge(sem["probsT_sb"], upto("probsT_sb", b, 2 * p - 2 + r))
                    elif r == 0:
                        pe.wait_ge(sem["proj_dve"], upto("proj_dve", b, 23 // 2))
                    else:
                        pe.wait_ge(sem["proj_dve"], upto("proj_dve", b, 21 // 2))
                    pe.wait_ge(sem["normal"], upto("normal", b, 2 * p + r))
                    for i in range(4):
                        ins = turn((t0, t1)[r][0:S, i * T:(i + 1) * T], pr[:, p % RING, r, i, :])
                    ins.then_inc(sem["probsT"], 1)

            def b_pv(b, p):
                q, half = p // 2, p % 2
                pe.wait_ge(sem["probsT_sb"], upto("probsT_sb", b, 2 * p + 1))
                if half:
                    pe.wait_ge(sem["headsT_sb"], upto("headsT_sb", b, p - 1))
                elif p:
                    pe.wait_ge(sem["attn_sum"], upto("attn_sum", b, q - 1))
                else:
                    pe.wait_ge(sem["proj_act"], whole("proj_act", b))
                    pe.wait_ge(sem["proj_dve"], whole("proj_dve", b))
                for k in range(8):
                    h, r = 8 * half + k, k % 2
                    ins = mm(pvb[r * DK:(r + 1) * DK, (k // 2) * T:(k // 2 + 1) * T], vv[:, q, h * DK:(h + 1) * DK],
                             pT[:, 4 * r + k // 2, :], start=True, stop=True)
                ins.then_inc(sem["pv"], 1)

            def b_wo(b, q):
                if q == 0 and not later(b):
                    pe.wait_ge(sem["wo_in"], 16)
                pe.wait_ge(sem["headsT_sb"], upto("headsT_sb", b, 2 * q + 1))
                for j in range(NCH):
                    ins = mm(pvb[:, 0:P], hT[:, j, :], wo[:, j, :], start=(j == 0), stop=(j == NCH - 1))
                ins.then_inc(sem["wo"], 1)

            def c_x2_T(c):
                pe.wait_ge(sem["ln2_out"], whole("ln2_out", c))
                if later(c):
                    pe.wait_ge(sem["eT_sb"], upto("eT_sb", c - 1, 6))
                for q in range(SEQ):
                    ins = turn(m0[:, q * T:(q + 1) * T], x2[:, q, :])
                ins.then_inc(sem["x2T"], 1)

            def c_router_shared(c):
                if not later(c):
                    pe.wait_ge(sem["w_lo"], SPLIT.index("wrs") + 1)
                pe.wait_ge(sem["x2T_sb"], upto("x2T_sb", c))
                if later(c):
                    pe.wait_ge(sem["moe_sum"], whole("moe_sum", c - 1))
                for k, dst in enumerate((m1, m0)):
                    for q in (2 * k, 2 * k + 1):
                        ins = product(dst[:, (q % 2) * RS:(q % 2 + 1) * RS], cols_of(x2T, q * T, (q + 1) * T),
                                      cols_of(split["wrs"], 0, RS))
                    ins.then_inc(sem["rs"], 1)

            def c_shared_T(c):
                pe.wait_ge(sem["sh_act"], upto("sh_act", c, 1))
                settle(pe)
                for q in range(SEQ):
                    ins = turn(m1[0:I, q * T:(q + 1) * T], ash[:, q, :])
                ins.then_inc(sem["shT"], 1)

            def c_up(c, n):
                q, half = n // 2, (n % 2) * 512
                if n == 0:
                    if not later(c):
                        pe.wait_ge(sem["w_lo"], SPLIT.index("wu") + 1)
                    pe.wait_ge(sem["shT_sb"], upto("shT_sb", c))
                elif n % 2:
                    pe.wait_ge(sem["e_gate"], upto("e_gate", c, n - 1))
                else:
                    pe.wait_ge(sem["eT_sb"], upto("eT_sb", c, n - 2))
                product(m0[:], cols_of(x2T, q * T, (q + 1) * T), cols_of(split["wg"], half, half + 512)).then_inc(sem["eg"], 1)
                if n % 2:
                    pe.wait_ge(sem["e_act"], upto("e_act", c, n - 1))
                elif n:
                    pe.wait_ge(sem["moe_sum"], upto("moe_sum", c, q - 1))
                product(m1[:], cols_of(x2T, q * T, (q + 1) * T), cols_of(split["wu"], half, half + 512)).then_inc(sem["eu"], 1)

            def c_act_T(c, q):
                pe.wait_ge(sem["e_weighted"], upto("e_weighted", c, 2 * q + 1))
                for j in range(E // 2):
                    ins = turn((m0, m1)[j // 4][:, (j % 4) * T:(j % 4 + 1) * T], ew[:, j * P:(j + 1) * P])
                    if j % 4 == 3:
                        ins.then_inc(sem["eT"], 1)

            def c_down(c, q):
                if q == 0 and not later(c):
                    pe.wait_ge(sem["wd_in"], 16)
                    pe.wait_ge(sem["wsd_in"], 16)
                pe.wait_ge(sem["eT_sb"], upto("eT_sb", c, 2 * q + 1))
                for j in range(E // 2):
                    mm(m1[:, 0:P], eT[:, j, :], wd[:, j, :], start=(j == 0), stop=False)
                mm(m1[:, 0:P], sT[:, q * T:(q + 1) * T], wsd[:], start=False, stop=True).then_inc(sem["down"], 1)

            def body(a, b, c):
                A, B, C = a is not None, b is not None, c is not None

                if B:
                    b_project(b, 4, 5)
                    a_ff2(b)
                if C:
                    c_x2_T(c)
                if B:
                    b_project(b, 5, 10)
                    a_x1_T(b)
                if C:
                    c_router_shared(c)
                if B:
                    b_project(b, 10, 18)
                    b_scores(b, 0)
                if C:
                    c_shared_T(c)
                if B:
                    b_project(b, 18, 20)
                if A:
                    a_norm_T(a, 0)
                for s in range(PAIRS + LAG):
                    odd = s % 2
                    if B and s >= LAG:
                        b_probs_T(b, s - LAG)
                    if C and s > 1 and not odd:
                        c_act_T(c, s // 2 - 1)
                    if B and 0 < s < PAIRS:
                        b_scores(b, s)
                    if A and s == 8:
                        b_project(a, 0, 2)
                    if A and s == 5:
                        a_hid(a)
                    if A and s == 9:
                        a_ff1(a, 0)
                        a_ff1(a, 1)
                        a_ff1(a, 2)
                    if B and s >= LAG:
                        b_pv(b, s - LAG)
                    if B and s < 2:
                        b_project(b, 20 + 2 * s, 22 + 2 * s)
                    if C and s > 1 and not odd:
                        c_down(c, s // 2 - 1)
                    if A and s == 8:
                        a_norm_T(a, 2)
                    if C and s < PAIRS:
                        c_up(c, s)
                    if A:
                        if s == 1:
                            a_pw(a)
                        elif s == 3:
                            a_norm_T(a, 1)
                        elif s == 4:
                            a_gate(a)
                        elif s == 6:
                            a_scan_T(a)
                        elif s == 8:
                            b_project(a, 2, 4)
                        elif s == 9:
                            a_ff1(a, 3, c)
                    if B and s > LAG and odd:
                        b_wo(b, (s - LAG) // 2)

            pipeline(pe, body)

        @block.scalar
        def _(act):
            f = nc.scalar.activation
            act.wait_ge(sem["gammas"], 1)
            act.wait_ge(sem["bq8"], 1)

            def w_high(names):
                for n in names:
                    if n in LATE_LOADS:
                        act.wait_ge(sem[f"{n}_in"], 16)
                    f(split[n][0][:], raw[n], ACT.Copy).then_inc(sem["w_hi"], 1)

            act.wait_ge(sem["mixer_weights"], MIXER_WEIGHTS)
            w_high(SPLIT[0:2])

            def a_sums(a, n):
                src = (xt, xm, xg)[n]
                if n == 0:
                    act.wait_ge(sem["x_loaded"], whole("x_loaded", a))
                    if later(a):
                        act.wait_ge(sem["floored"], whole("floored", a - 1))
                else:
                    act.wait_ge(sem[("mixed", "gru_sum")[n - 1]], upto(("mixed", "gru_sum")[n - 1], a))
                    act.wait_ge(sem["floored"], upto("floored", a, n - 1))
                if n:
                    act.wait_ge(sem["a_bank"], upto("a_bank", a, A_USE[f'T{n - 1}']))
                elif later(a):
                    act.wait_ge(sem["a_bank"], upto("a_bank", a - 1, A_USE['T2']))
                for q in range(SEQ):
                    ins = f(xn[:, q, :], src[:, q, :], ACT.Square, accum_out=ss[:, q:q + 1])
                ins.then_inc(sem["sums"], 1)

            def a_norm(a, n):
                act.wait_ge(sem["a_bank"], upto("a_bank", a, A_USE[f'T{n}']))
                gamma = c_(("g_conv", "g_gru", "g_ff")[n])
                if n == 0:
                    if later(a):
                        act.wait_ge(sem["conv0"], upto("conv0", a - 1))
                    dst = xc[:, :, 2:T + 2]
                else:
                    if n == 1:
                        if later(a):
                            act.wait_ge(sem["a_bank"], upto("a_bank", a - 1, A_USE['up3']))
                    else:
                        act.wait_ge(sem["a_bank"], upto("a_bank", a, A_USE['hid']))
                    dst = seqs(nT[0][:])
                f(dst, seqs(ma[:]), ACT.Identity, scale=gamma).then_inc(sem["normT"], 1)

            def a_conv(a):
                act.wait_ge(sem["normT"], upto("normT", a, 0))
                if later(a):
                    act.wait_ge(sem["a_bank"], upto("a_bank", a - 1, A_USE['pw']))
                f(cv[:], xc[:, :, 2:T + 2], ACT.Identity, scale=c_("dw2"), bias=c_("dwb")).then_inc(sem["conv2"], 1)

            def a_gate(a):
                act.wait_ge(sem["a_bank"], upto("a_bank", a, A_USE['gate']))
                if later(a):
                    act.wait_ge(sem["scan"], upto("scan", a - 1))
                f(gin[:], ma[:], ACT.Tanh, scale=0.5).then_inc(sem["gate_tanh"], 1)

            def a_hid(a):
                act.wait_ge(sem["a_bank"], upto("a_bank", a, A_USE['hid']))
                if later(a):
                    act.wait_ge(sem["drive"], upto("drive", a - 1))
                f(hin[:], ma[:], ACT.Tanh, scale=0.5).then_inc(sem["hid_tanh"], 1)

            def a_gelu(a, k):
                act.wait_ge(sem["a_bank"], upto("a_bank", a, A_USE[f'up{k}']))
                if k == 0:
                    if later(a):
                        act.wait_ge(sem["a_bank"], upto("a_bank", a - 1, A_USE['ff2_1']))
                f(hf[:, k, :], ff1_banks[k][:], ACT.Gelu, bias=c_(f"b1_{k}")).then_inc(sem["gelu"], 1)

            def a_x1T(a):
                act.wait_ge(sem["a_bank"], upto("a_bank", a, A_USE['Tx1']))
                if later(a):
                    act.wait_ge(sem["proj"], whole("proj", a - 1))
                f(x1T[0][:], ma[:], ACT.Copy).then_inc(sem["x1T_hi"], 1)

            def b_project(b, lo, hi):
                for n in range(lo, hi):
                    if n % 2:
                        continue
                    act.wait_ge(sem["proj"], upto("proj", b, n))
                    src = proj_banks[n]
                    kind, j = projections[n]
                    if n == 12 and not later(b):
                        act.wait_ge(sem["w_lo"], len(SPLIT))
                    if n == 0:
                        if later(b):
                            act.wait_ge(sem["scores"], whole("scores", b - 1))
                    if n == 8:
                        if later(b):
                            act.wait_ge(sem["pv"], whole("pv", b - 1))
                    if kind == "v":
                        ins = f(vv[:, j // 2, (j % 2) * 512:(j % 2) * 512 + 512], src[0:S, :], ACT.Copy)
                    elif kind == "k":
                        ins = f(kT[:, j, :], src[:, 0:SW], ACT.Identity, bias=c_(f"bk{j}"))
                    else:
                        ins = f(qT[:, j, :], src[:], ACT.Identity, bias=c_(f"bq{j}"), scale=DK ** -0.5)
                    ins.then_inc(sem["proj_act"], 1)

            def b_probs(b, p, r):
                if p >= RING:
                    act.wait_ge(sem["probsT"], upto("probsT", b, 2 * (p - RING) + 1))
                else:
                    if later(b):
                        former = max(m for m in range(PAIRS) if m % RING == p)
                        act.wait_ge(sem["probsT"], upto("probsT", b - 1, 2 * former + 1))
                act.wait_ge(sem["negmax"], upto("negmax", b, 2 * p + r))
                for i in range(4):
                    ins = f(pr[:, p % RING, r, i, :], score_banks[r][:, i * S:(i + 1) * S], ACT.Exp,
                            bias=nm[:, p % 2, r, i:i + 1], accum_out=rsum[:, p % 2, r, i, :])
                ins.then_inc(sem["probs"], 1)

            def c_x2T(c):
                act.wait_ge(sem["x2T"], upto("x2T", c))
                if later(c):
                    act.wait_ge(sem["eu"], whole("eu", c - 1))
                f(x2T[0][:], m0[:], ACT.Copy).then_inc(sem["x2T_hi"], 1)

            def c_router(c):
                act.wait_ge(sem["logits"], upto("logits", c, 1))
                f(rt[:], lg[:], ACT.Tanh, scale=0.5).then_inc(sem["route_tanh"], 1)

            def c_shared(c):
                for k, src in enumerate((m1, m0)):
                    act.wait_ge(sem["rs"], upto("rs", c, k))
                    if k == 0:
                        if later(c):
                            act.wait_ge(sem["shT"], whole("shT", c - 1))
                    v = seqs(src[:, 0:2 * RS], 2)[:, :, E:E + I]
                    f(ash[:, 2 * k:2 * k + 2, :], v, ACT.Tanh, scale=0.5).then_inc(sem["sh_tanh"], 1)

            def c_sharedT(c):
                act.wait_ge(sem["shT"], upto("shT", c))
                if later(c):
                    act.wait_ge(sem["down"], whole("down", c - 1))
                f(sT[:], m1[0:I, :], ACT.Copy).then_inc(sem["shT_sb"], 1)

            def c_tanh(c, n):
                act.wait_ge(sem["eg"], upto("eg", c, n))
                if n:
                    act.wait_ge(sem["e_act"], upto("e_act", c, n - 1))
                elif later(c):
                    act.wait_ge(sem["e_act"], whole("e_act", c - 1))
                f(et[:], m0[:], ACT.Tanh, scale=0.5).then_inc(sem["e_tanh"], 1)

            def c_actT(c, q):
                if q:
                    act.wait_ge(sem["down"], upto("down", c, q - 1))
                for k, src in enumerate((m0, m1)):
                    act.wait_ge(sem["eT"], upto("eT", c, 2 * q + k))
                    f(eT[:, 4 * k:4 * k + 4, :], seqs(src[:]), ACT.Copy).then_inc(sem["eT_sb"], 1)

            def body(a, b, c):
                A, B, C = a is not None, b is not None, c is not None

                if B:
                    b_project(b, 4, 6)
                if C:
                    c_x2T(c)
                if A:
                    a_sums(a, 0)
                if B:
                    b_project(b, 6, 8)
                if B:
                    b_project(b, 8, 9)
                    a_x1T(b)
                if C:
                    c_shared(c)
                if B:
                    b_project(b, 9, 13)
                if C:
                    c_router(c)
                if B:
                    b_project(b, 13, 18)
                    b_probs(b, 0, 0)
                    b_project(b, 18, 20)
                if C:
                    c_sharedT(c)
                if B:
                    b_probs(b, 0, 1)
                if A:
                    a_norm(a, 0)
                for s in range(PAIRS + LAG):
                    even = s > 1 and s % 2 == 0
                    if C and even:
                        c_actT(c, s // 2 - 1)
                    if B and 0 < s < PAIRS:
                        b_probs(b, s, 0)
                    if C and s < PAIRS and s % 2:
                        c_tanh(c, s)
                    if B and s == 1:
                        b_project(b, 22, 23)
                    if B and 0 < s < PAIRS:
                        b_probs(b, s, 1)
                    if B and s == 0:
                        b_project(b, 20, 21)
                    if C and s < PAIRS and s % 2 == 0:
                        c_tanh(c, s)
                    if A:
                        if s == 0:
                            a_conv(a)
                        elif s == 2:
                            a_sums(a, 1)
                            if not later(a):
                                w_high(SPLIT[2:5])
                        elif s == 3:
                            a_norm(a, 1)
                        elif s == 4:
                            a_gate(a)
                        elif s == 5:
                            a_hid(a)
                        elif s == 7:
                            a_sums(a, 2)
                            if not later(a):
                                w_high(SPLIT[5:])
                        elif s == 8:
                            b_project(a, 0, 2)
                            a_norm(a, 2)
                            b_project(a, 2, 4)
                        elif s == 9:
                            for k in range(FCH):
                                a_gelu(a, k)

            pipeline(act, body)

        @block.vector
        def _(dve):
            V = nc.vector

            dve.wait_ge(sem["mixer_weights"], MIXER_WEIGHTS)
            V.memset(xc[:], 0.0).then_inc(sem["pads"], 1)
            dve.wait_ge(sem["pads"], 1)
            V.memset(eps[:], 1e-5).then_inc(sem["powers"], 1)
            V.memset(power[:], -0.5).then_inc(sem["powers"], 1)
            V.tensor_scalar(c_("g_conv", 3), c_("g_conv", 3), 1.0, None, ALU.add).then_inc(sem["gammas"], 1)
            dve.wait_ge(sem["gammas"], 1)
            V.tensor_scalar(c_("bq0", NCH), c_("bq0", NCH), DK ** -0.5, None, ALU.mult).then_inc(sem["bq8"], 1)
            dve.wait_ge(sem["bq8"], 1)
            dve.wait_ge(sem["iota"], 1)
            V.tensor_copy(iota[:], iota_i[:]).then_inc(sem["iotaf"], 1)
            dve.wait_ge(sem["iotaf"], 1)

            def a_floored(a, n):
                dve.wait_ge(sem["sums"], upto("sums", a, n))
                if n:
                    dve.wait_ge(sem["rms"], upto("rms", a, n - 1))
                elif later(a):
                    dve.wait_ge(sem["rms"], whole("rms", a - 1))
                V.tensor_scalar(ssf[:], ss[:], 1.0 / P, 1e-24 / P, ALU.mult, ALU.max).then_inc(sem["floored"], 1)

            def a_norm_low(a, n):
                dve.wait_ge(sem["normT"], upto("normT", a, n))
                if n == 1:
                    if later(a):
                        dve.wait_ge(sem["a_bank"], upto("a_bank", a - 1, A_USE['up3']))
                else:
                    dve.wait_ge(sem["a_bank"], upto("a_bank", a, A_USE['hid']))
                V.scalar_tensor_tensor(nT[1][:], ma[:], c_(("g_gru", "g_ff")[n - 1]), nT[0][:].bitcast(F32),
                                       ALU.mult, ALU.subtract).then_inc(sem["normT_lo"], 1)

            def a_x1_low(a):
                dve.wait_ge(sem["x1T_hi"], upto("x1T_hi", a))
                if later(a):
                    dve.wait_ge(sem["proj"], whole("proj", a - 1))
                V.tensor_tensor(x1T[1][:], ma[:], x1T[0][:].bitcast(F32), ALU.subtract).then_inc(sem["x1T"], 1)

            def a_conv(a):
                dve.wait_ge(sem["conv2"], upto("conv2", a))
                V.scalar_tensor_tensor(cv[:], xc[:, :, 1:T + 1], c_("dw1"), cv[:], ALU.mult, ALU.add).then_inc(sem["conv1"], 1)
                dve.wait_ge(sem["conv1"], upto("conv1", a))
                V.scalar_tensor_tensor(cv[:], xc[:, :, 0:T], c_("dw0"), cv[:], ALU.mult, ALU.add).then_inc(sem["conv0"], 1)

            def a_mixed(a):
                dve.wait_ge(sem["a_bank"], upto("a_bank", a, A_USE['pw']))
                dve.wait_ge(sem["x_bpw"], upto("x_bpw", a))
                V.tensor_tensor(xm[:], seqs(ma[:]), xm[:], ALU.add).then_inc(sem["mixed"], 1)

            def a_gru_keep(a):
                dve.wait_ge(sem["gate_tanh"], upto("gate_tanh", a))
                V.tensor_scalar(keep[:], seqs(gin[:]), -0.5, 0.5, ALU.mult, ALU.add).then_inc(sem["keep"], 1)
                dve.wait_ge(sem["keep"], upto("keep", a))
                V.tensor_scalar(gin[:], gin[:], 0.5, 0.5, ALU.mult, ALU.add).then_inc(sem["inp"], 1)
                V.memset(keep[:, :, 0:1], 0.0).then_inc(sem["keep0"], 1)

            def a_gru_drive(a):
                dve.wait_ge(sem["hid_tanh"], upto("hid_tanh", a))
                V.tensor_scalar(hin[:], hin[:], 0.5, 0.5, ALU.mult, ALU.add).then_inc(sem["sig"], 1)
                dve.wait_ge(sem["sig"], upto("sig", a))
                V.scalar_tensor_tensor(hin[:], ma[:], 0.5, hin[:], ALU.add, ALU.max).then_inc(sem["cand"], 1)
                dve.wait_ge(sem["cand"], upto("cand", a))
                dve.wait_ge(sem["inp"], upto("inp", a))
                V.tensor_tensor(gin[:], gin[:], hin[:], ALU.mult).then_inc(sem["drive"], 1)
                dve.wait_ge(sem["drive"], upto("drive", a))

            def a_gru_scan(a):
                dve.wait_ge(sem["keep0"], upto("keep0", a))
                if later(a):
                    dve.wait_ge(sem["a_bank"], upto("a_bank", a - 1, A_USE['Th']))
                V.tensor_tensor_scan(hs[:], keep[:].rearrange("p b t -> p (b t)"), gin[:], 0.0,
                                     ALU.mult, ALU.add).then_inc(sem["scan"], 1)

            def a_gru_sum(a):
                dve.wait_ge(sem["a_bank"], upto("a_bank", a, A_USE['Th']))
                if later(a):
                    dve.wait_ge(sem["x_all"], upto("x_all", a - 1))
                V.tensor_tensor(xg[:], seqs(ma[:]), xm[:], ALU.add).then_inc(sem["gru_sum"], 1)

            def a_mixer(a):
                dve.wait_ge(sem["x_all"], upto("x_all", a))
                for k in range(2):
                    two = slice(2 * k, 2 * k + 2)
                    dve.wait_ge(sem["a_bank"], upto("a_bank", a, A_USE[f'ff2_{k}']))
                    V.tensor_tensor(xz[:, two, :], seqs(ff2_banks[k][:])[:, two, :], xz[:, two, :], ALU.add).then_inc(sem["mixer"], 1)
                    dve.wait_ge(sem["mixer"], upto("mixer", a, k))
                    for q in (2 * k, 2 * k + 1):
                        V.bn_stats(st1[:, q, :], xz[:, q, :]).then_inc(sem["ln1_stats"], 1)
                    for q in (2 * k, 2 * k + 1):
                        dve.wait_ge(sem["ln1_stats"], upto("ln1_stats", a, q))
                        settle(dve)
                        V.bn_aggr(mv1[:, q, :], st1[:, q, :]).then_inc(sem["ln1_mv"], 1)

            def a_ln1(a):
                dve.wait_ge(sem["ln1_rstd"], upto("ln1_rstd", a))
                if later(a):
                    dve.wait_ge(sem["a_bank"], whole("a_bank", a - 1))
                if later(a):
                    dve.wait_ge(sem["x1_bo"], upto("x1_bo", a - 1))
                for q in range(SEQ):
                    V.tensor_scalar(x1[:, q, :], xz[:, q, :], mv1[:, q, 0:1], rs1[:, q:q + 1],
                                    ALU.subtract, ALU.mult).then_inc(sem["ln1_out"], 1)

            def b_project(b, lo, hi):
                for n in range(lo, hi):
                    if n % 2 == 0:
                        continue
                    dve.wait_ge(sem["proj"], upto("proj", b, n))
                    src = proj_banks[n]
                    kind, j = projections[n]
                    if n == 13 and not later(b):
                        dve.wait_ge(sem["w_lo"], len(SPLIT))
                    if n == 1:
                        if later(b):
                            dve.wait_ge(sem["scores"], whole("scores", b - 1))
                    if n == 9:
                        if later(b):
                            dve.wait_ge(sem["pv"], whole("pv", b - 1))
                    if kind == "v":
                        ins = V.tensor_copy(vv[:, j // 2, (j % 2) * 512:(j % 2) * 512 + 512], src[0:S, :])
                    elif kind == "k":
                        ins = V.tensor_scalar(kT[:, j, :], src[:, 0:SW], c_(f"bk{j}"), None, ALU.add)
                    else:
                        ins = V.tensor_scalar(qT[:, j, :], src[:], DK ** -0.5, c_(f"bq{j}"), ALU.mult, ALU.add)
                    ins.then_inc(sem["proj_dve"], 1)

            def b_max(b, p):
                for r in range(2):
                    dve.wait_ge(sem["scores"], upto("scores", b, 2 * p + r))
                    V.tensor_reduce(nm[:, p % 2, r, :], seqs(score_banks[r][:, 0:4 * S]), AX_X, ALU.max,
                                    negate=True).then_inc(sem["negmax"], 1)

            def b_probs_T(b, p):
                if p:
                    dve.wait_ge(sem["pv"], upto("pv", b, p - 1))
                else:
                    if later(b):
                        dve.wait_ge(sem["pv"], whole("pv", b - 1))
                for k in range(2):
                    dve.wait_ge(sem["probsT"], upto("probsT", b, 2 * p + k))
                    V.tensor_copy(pT[:, 4 * k:4 * k + 4, :], seqs((t0, t1)[k][0:S, :])).then_inc(sem["probsT_sb"], 1)

            def b_recips(b, p, r):
                dve.wait_ge(sem["probs"], upto("probs", b, 2 * p + r))
                V.reciprocal(ri[:, p % 2, r, :, :], rsum[:, p % 2, r, :, :]).then_inc(sem["rinv"], 1)

            def b_heads_T(b, p):
                half = p % 2
                dve.wait_ge(sem["pv"], upto("pv", b, p))
                if p > 1:
                    dve.wait_ge(sem["wo"], upto("wo", b, p // 2 - 1))
                elif later(b):
                    dve.wait_ge(sem["wo"], whole("wo", b - 1))
                V.tensor_tensor(hT[:, 4 * half:4 * half + 4, :], seqs(pvb[:]),
                                c_(f"bv{4 * half}", 4).unsqueeze(2).to_broadcast([P, 4, T]),
                                ALU.add).then_inc(sem["headsT_sb"], 1)

            def b_sum(b, q):
                dve.wait_ge(sem["wo"], upto("wo", b, q))
                dve.wait_ge(sem["x1_bo"], upto("x1_bo", b))
                V.tensor_tensor(xa[:], pvb[:, 0:P], x1b[:, q, :], ALU.add).then_inc(sem["attn_sum"], 1)
                dve.wait_ge(sem["attn_sum"], upto("attn_sum", b, q))
                V.bn_stats(st2[:], xa[:]).then_inc(sem["ln2_stats"], 1)
                dve.wait_ge(sem["ln2_stats"], upto("ln2_stats", b, q))
                settle(dve)
                V.bn_aggr(mv2[:], st2[:]).then_inc(sem["ln2_mv"], 1)

            def b_ln2(b, q):
                dve.wait_ge(sem["ln2_rstd"], upto("ln2_rstd", b, q))
                if later(b):
                    dve.wait_ge(sem["x2T"], whole("x2T", b - 1))
                V.tensor_scalar(x2[:, q, :], xa[:], mv2[:, 0:1], rs2[:], ALU.subtract, ALU.mult).then_inc(sem["ln2_out"], 1)

            def c_x2_low(c):
                dve.wait_ge(sem["x2T_hi"], upto("x2T_hi", c))
                if later(c):
                    dve.wait_ge(sem["eu"], whole("eu", c - 1))
                V.tensor_tensor(x2T[1][:], m0[:], x2T[0][:].bitcast(F32), ALU.subtract).then_inc(sem["x2T_sb"], 1)

            def c_logits(c):
                for k, src in enumerate((m1, m0)):
                    dve.wait_ge(sem["sh_tanh"], upto("sh_tanh", c, k))
                    V.tensor_tensor(lg[:, 2 * k:2 * k + 2, :], seqs(src[:, 0:2 * RS], 2)[:, :, 0:E],
                                    brow["gate"].unsqueeze(1).to_broadcast([P, 2, E]), ALU.add).then_inc(sem["logits"], 1)

            def c_shared(c):
                for k, src in enumerate((m1, m0)):
                    dve.wait_ge(sem["sh_tanh"], upto("sh_tanh", c, k))
                    v = seqs(src[:, 0:2 * RS], 2)
                    sl = slice(2 * k, 2 * k + 2)
                    V.scalar_tensor_tensor(ash[:, sl, :], ash[:, sl, :], 1.0, v[:, :, E:E + I], ALU.add, ALU.mult).then_inc(sem["sh_gate"], 1)
                    dve.wait_ge(sem["sh_gate"], upto("sh_gate", c, k))
                    V.scalar_tensor_tensor(ash[:, sl, :], ash[:, sl, :], 0.5, v[:, :, E + I:RS],
                                           ALU.mult, ALU.mult).then_inc(sem["sh_act"], 1)

            def c_route(c):
                dve.wait_ge(sem["route_tanh"], upto("route_tanh", c))
                V.tensor_scalar(sg8[:], rt[:], 0.5, 0.5, ALU.mult, ALU.add).then_inc(sem["route_sig"], 1)
                dve.wait_ge(sem["route_sig"], upto("route_sig", c))
                settle(dve)
                for q in range(SEQ):
                    V.max(mx[:, q, :], sg8[:, q, :]).then_inc(sem["top"], 1)
                for q in range(SEQ):
                    dve.wait_ge(sem["top"], upto("top", c, q))
                    settle(dve)
                    V.max_index(mi[:, q, :], mx[:, q, :], sg8[:, q, :]).then_inc(sem["top_at"], 1)

            def c_gates(c):
                V.tensor_tensor(tsum[:], mx[:, :, 0:1], mx[:, :, 1:2], ALU.add).then_inc(sem["top_sum"], 1)
                dve.wait_ge(sem["top_sum"], upto("top_sum", c))
                dve.wait_ge(sem["top"], whole("top", c))
                dve.wait_ge(sem["top_at"], whole("top_at", c))
                V.tensor_copy(mf[:], mi[:, :, 0:2]).then_inc(sem["top_f"], 1)
                V.reciprocal(trec[:], tsum[:]).then_inc(sem["top_rec"], 1)
                dve.wait_ge(sem["top_rec"], upto("top_rec", c))
                V.scalar_tensor_tensor(tw[:], mx[:, :, 0:2], 0.5, trec[:].to_broadcast([P, SEQ, 2]),
                                       ALU.mult, ALU.mult).then_inc(sem["top_w"], 1)
                dve.wait_ge(sem["top_f"], upto("top_f", c))
                for o, k in ((o0, 0), (o1, 1)):
                    V.tensor_tensor(o[:], over_seqs(iota[:]), mf[:, :, k:k + 1].to_broadcast([P, SEQ, E]),
                                    ALU.is_equal).then_inc(sem[f"one{k}"], 1)
                dve.wait_ge(sem["top_w"], upto("top_w", c))
                for o, w, k in ((o0, q0, 0), (o1, q1, 1)):
                    dve.wait_ge(sem[f"one{k}"], upto(f"one{k}", c))
                    V.tensor_tensor(w[:], o[:], tw[:, :, k:k + 1].to_broadcast([P, SEQ, E]), ALU.mult).then_inc(sem[f"w{k}"], 1)
                dve.wait_ge(sem["w0"], upto("w0", c))
                dve.wait_ge(sem["w1"], upto("w1", c))
                if later(c):
                    dve.wait_ge(sem["e_weighted"], whole("e_weighted", c - 1))
                V.tensor_tensor(gw[:], q0[:], q1[:], ALU.add).then_inc(sem["gates"], 1)

            def c_experts(c, n):
                dve.wait_ge(sem["e_tanh"], upto("e_tanh", c, n))
                if n:
                    dve.wait_ge(sem["e_act"], upto("e_act", c, n - 1))
                V.scalar_tensor_tensor(et[:], et[:], 1.0, m0[:], ALU.add, ALU.mult).then_inc(sem["e_gate"], 1)
                dve.wait_ge(sem["e_gate"], upto("e_gate", c, n))
                dve.wait_ge(sem["eu"], upto("eu", c, n))
                if n >= 2:
                    dve.wait_ge(sem["e_weighted"], upto("e_weighted", c, n - 2))
                else:
                    if later(c):
                        dve.wait_ge(sem["e_weighted"], upto("e_weighted", c - 1, n + 6))
                V.tensor_tensor(e3[:, n % 2, :], et[:], m1[:], ALU.mult).then_inc(sem["e_act"], 1)

            def c_sum(c, q):
                dve.wait_ge(sem["down"], upto("down", c, q))
                V.scalar_tensor_tensor(ys[:], x2[:, q, :], 2.0, m1[:, 0:P], ALU.mult, ALU.add).then_inc(sem["moe_sum"], 1)
                dve.wait_ge(sem["moe_sum"], upto("moe_sum", c, q))
                V.bn_stats(st3[:], ys[:]).then_inc(sem["ln3_stats"], 1)
                dve.wait_ge(sem["ln3_stats"], upto("ln3_stats", c, q))
                settle(dve)
                V.bn_aggr(mv3[:], st3[:]).then_inc(sem["ln3_mv"], 1)

            def c_ln3(c, q):
                dve.wait_ge(sem["ln3_rstd"], upto("ln3_rstd", c, q))
                if later(c):
                    dve.wait_ge(sem[f"out{q}_stored"], upto(f"out{q}_stored", c - 1))
                V.tensor_scalar(y[:, q, :], ys[:], mv3[:, 0:1], rs3[:], ALU.subtract, ALU.mult).then_inc(sem["ln3_out"], 1)

            def body(a, b, c):
                A, B, C = a is not None, b is not None, c is not None

                if B:
                    a_mixer(b)
                if C:
                    c_x2_low(c)
                if B:
                    b_project(b, 4, 8)
                    a_ln1(b)
                if A:
                    a_floored(a, 0)
                if B:
                    b_project(b, 8, 10)
                    a_x1_low(b)
                if C:
                    c_logits(c)
                    c_shared(c)
                if B:
                    b_project(b, 10, 18)
                    b_max(b, 0)
                if C:
                    c_route(c)
                if B:
                    b_project(b, 18, 20)
                if C:
                    c_gates(c)
                for s in range(PAIRS + LAG):
                    odd = s % 2
                    if B and s >= LAG:
                        b_probs_T(b, s - LAG)
                    if B and 0 < s < PAIRS:
                        b_max(b, s)
                    if B and s > LAG + 1 and not odd:
                        b_ln2(b, (s - LAG) // 2 - 1)
                    if A and s == 1:
                        a_conv(a)
                    if A and s == 8:
                        b_project(a, 0, 2)
                    if B and s == 1:
                        b_project(b, 23, 24)
                    if A and s == 6:
                        a_gru_scan(a)
                    if A and s == 7:
                        a_gru_sum(a)
                    if B and s >= LAG:
                        b_heads_T(b, s - LAG)
                    if B and s < PAIRS:
                        b_recips(b, s, 0)
                    if C and s > 1 and not odd:
                        c_sum(c, s // 2 - 1)
                    if C and odd and s < PAIRS:
                        c_experts(c, s)
                    if B and s < PAIRS:
                        b_recips(b, s, 1)
                    if B and s == 0:
                        b_project(b, 20, 22)
                    if C and not odd and s < PAIRS:
                        c_experts(c, s)
                    if C and s > 1 and not odd:
                        c_ln3(c, s // 2 - 1)
                    if A:
                        if s == 1:
                            a_mixed(a)
                        elif s == 2:
                            a_floored(a, 1)
                        elif s == 3:
                            a_norm_low(a, 1)
                        elif s == 4:
                            a_gru_keep(a)
                        elif s == 5:
                            a_gru_drive(a)
                        elif s == 7:
                            a_floored(a, 2)
                        elif s == 8:
                            a_norm_low(a, 2)
                            b_project(a, 2, 4)
                    if B and s > LAG and odd:
                        b_sum(b, (s - LAG) // 2)
                if B:
                    b_ln2(b, SEQ - 1)

            pipeline(dve, body)

        @block.gpsimd
        def _(pool):
            GP = nc.gpsimd
            GP.memset(ident[:], 0.0).then_inc(sem["ones"], 1)
            GP.memset(maskb[:], 0.0).then_inc(sem["mask0"], 1)
            pool.wait_ge(sem["ones"], 1)
            GP.affine_select(out=ident[:], in_=ident[:], pattern=[[-1, P]], compare_op=ALU.not_equal, fill=1.0,
                             base=0, channel_multiplier=1).then_inc(sem["ident"], 1)
            pool.wait_ge(sem["ident"], 1)
            GP.tensor_copy(identb[:], ident[:]).then_inc(sem["identb"], 1)
            pool.wait_ge(sem["mask0"], 1)
            GP.affine_select(out=maskb[:], in_=maskb[:], pattern=[[-1, S]], compare_op=ALU.is_ge, fill=-1e10,
                             base=0, channel_multiplier=1).then_inc(sem["mask"], 1)
            GP.iota(iota_i[:], pattern=[[1, E]], base=0, channel_multiplier=0).then_inc(sem["iota"], 1)
            pool.wait_ge(sem["powers"], 2)
            pool.wait_ge(sem["mixer_weights"], MIXER_WEIGHTS)

            def w_low(names):
                for n in names:
                    pool.wait_ge(sem["w_hi"], SPLIT.index(n) + 1)
                    GP.tensor_tensor(split[n][1][:], raw[n], split[n][0][:].bitcast(F32), ALU.subtract).then_inc(sem["w_lo"], 1)

            w_low(SPLIT[0:2])

            def b_context(b):
                pool.wait_ge(sem["ctx_loaded"], whole("ctx_loaded", b))
                if later(b):
                    pool.wait_ge(sem["proj"], whole("proj", b - 1))
                settle(pool)
                GP.tensor_copy(cS[0][:], cT[:]).then_inc(sem["ctx_hi"], 1)
                pool.wait_ge(sem["ctx_hi"], upto("ctx_hi", b))
                GP.tensor_tensor(cS[1][:], cT[:], cS[0][:].bitcast(F32), ALU.subtract).then_inc(sem["ctx_split"], 1)

            def a_normed(a, n):
                src = (xt, xm, xg)[n]
                pool.wait_ge(sem["floored"], upto("floored", a, n))
                GP.tensor_tensor(rr[:], ssf[:], power[:], ALU.pow).then_inc(sem["rms"], 1)
                pool.wait_ge(sem["rms"], upto("rms", a, n))
                if n:
                    pool.wait_ge(sem["a_bank"], upto("a_bank", a, A_USE[f'T{n - 1}']))
                else:
                    if later(a):
                        pool.wait_ge(sem["a_bank"], upto("a_bank", a - 1, A_USE['T2']))
                GP.tensor_tensor(xn[:], src[:], rr[:].unsqueeze(2).to_broadcast([P, SEQ, P]), ALU.mult).then_inc(sem["normed"], 1)

            def a_residuals(a):
                if later(a):
                    pool.wait_ge(sem["gru_sum"], upto("gru_sum", a - 1))
                GP.tensor_tensor(xm[:], xt[:], over_seqs(brow["pw"]), ALU.add).then_inc(sem["x_bpw"], 1)
                if later(a):
                    pool.wait_ge(sem["ln1_out"], whole("ln1_out", a - 1))
                GP.tensor_tensor(xz[:], xt[:], over_seqs(brow["ff2"]), ALU.add).then_inc(sem["x_bff"], 1)

            def a_all(a):
                pool.wait_ge(sem["gru_sum"], upto("gru_sum", a))
                pool.wait_ge(sem["x_bff"], upto("x_bff", a))
                GP.tensor_tensor(xz[:], xz[:], xg[:], ALU.add).then_inc(sem["x_all"], 1)

            def a_ln1(a):
                pool.wait_ge(sem["ln1_mv"], whole("ln1_mv", a))
                GP.tensor_tensor(ve1[:], mv1[:, :, 1], eps[:], ALU.add).then_inc(sem["ln1_eps"], 1)
                pool.wait_ge(sem["ln1_eps"], upto("ln1_eps", a))
                GP.tensor_tensor(rs1[:], ve1[:], power[:], ALU.pow).then_inc(sem["ln1_rstd"], 1)

            def a_x1_bo(a):
                pool.wait_ge(sem["ln1_out"], whole("ln1_out", a))
                if later(a):
                    pool.wait_ge(sem["attn_sum"], whole("attn_sum", a - 1))
                GP.tensor_tensor(x1b[:], x1[:], over_seqs(brow["bo"]), ALU.add).then_inc(sem["x1_bo"], 1)

            def b_normal(b, p, r):
                pool.wait_ge(sem["rinv"], upto("rinv", b, 2 * p + r))
                GP.tensor_tensor(pr[:, p % RING, r, :, :], pr[:, p % RING, r, :, :],
                                 ri[:, p % 2, r, :, :].to_broadcast([P, 4, S]), ALU.mult).then_inc(sem["normal"], 1)

            def ln(g, q, n, mv, ve, rs):
                pool.wait_ge(sem[f"ln{n}_mv"], upto(f"ln{n}_mv", g, q))
                GP.tensor_tensor(ve[:], mv[:, 1:2], eps[:, 0:1], ALU.add).then_inc(sem[f"ln{n}_eps"], 1)
                pool.wait_ge(sem[f"ln{n}_eps"], upto(f"ln{n}_eps", g, q))
                GP.tensor_tensor(rs[:], ve[:], power[:, 0:1], ALU.pow).then_inc(sem[f"ln{n}_rstd"], 1)

            def c_weight(c, n):
                pool.wait_ge(sem["gates"], upto("gates", c))
                pool.wait_ge(sem["e_act"], upto("e_act", c, n))
                if n >= 2:
                    pool.wait_ge(sem["eT"], upto("eT", c, 2 * (n // 2 - 1) + 1))
                else:
                    if later(c):
                        pool.wait_ge(sem["eT"], whole("eT", c - 1))
                half = n % 2
                GP.tensor_tensor(seqs(ew[:, half * 512:(half + 1) * 512], 8), seqs(e3[:, n % 2, :], 8),
                                 gw[:, n // 2, 8 * half:8 * half + 8].unsqueeze(2).to_broadcast([P, 8, I]),
                                 ALU.mult).then_inc(sem["e_weighted"], 1)

            def body(a, b, c):
                A, B, C = a is not None, b is not None, c is not None
                if B:
                    a_ln1(b)
                if A:
                    a_normed(a, 0)
                if B:
                    a_x1_bo(b)
                if A:
                    a_residuals(a)
                for s in range(PAIRS + LAG):
                    odd = s % 2
                    if B and s < PAIRS:
                        b_normal(b, s, 0)
                    if C and odd and s < PAIRS:
                        c_weight(c, s)
                    if B and s < PAIRS:
                        b_normal(b, s, 1)
                    if C and s > 1 and not odd:
                        ln(c, s // 2 - 1, 3, mv3, ve3, rs3)
                    if C and not odd and s < PAIRS:
                        c_weight(c, s)
                    if B and s > LAG and odd:
                        ln(b, (s - LAG) // 2, 2, mv2, ve2, rs2)
                    if A:
                        if s == 2:
                            a_normed(a, 1)
                            if not later(a):
                                w_low(SPLIT[2:5])
                        elif s == 4:
                            b_context(a)
                        elif s == 7:
                            a_normed(a, 2)
                            a_all(a)
                            if not later(a):
                                w_low(SPLIT[5:])

            pipeline(pool, body)


def kernel(**inputs):
    import numpy as np
    import concourse.bacc as bacc
    from concourse.bass_utils import run_bass_kernel_spmd

    a = {n: np.asarray(v) for n, v in inputs.items()}
    L, X, M = "L0_attn_", "L0_xattn_", "L0_ffn_"

    def chunks(v):
        return v.reshape(-1, P, *v.shape[1:]).swapaxes(0, 1)

    laid = {
        "x": a["x"],
        "ctxT": a["ctx_1024"].reshape(G, SEQ, S, P).transpose(0, 3, 1, 2).reshape(G, P, SW),
        "w_pw": a[L + "conv_pw_w"].T,
        "w_gru": a[L + "gru_w"].T,
        "w_ff1": a[L + "ff_w1"].T,
        "w_ff2": chunks(a[L + "ff_w2"].T),
        "cols": np.concatenate([a[L + "conv_dw_w"][:, 0, :], a[L + "conv_dw_b"][:, None], a[L + "conv_norm_g"][:, None],
                                a[L + "gru_norm_g"][:, None], a[L + "ff_norm_g"][:, None], chunks(a[L + "ff_b1"]),
                                chunks(a[X + "bq"]), chunks(a[X + "bk"]), chunks(a[X + "bv"])], axis=1),
        "rows": np.concatenate([a[L + "conv_pw_b"], a[L + "ff_b2"], a[X + "bo"], a[M + "gate_b"]])[None, :],
        "w_q": a[X + "Wq"], "w_k": a[X + "Wk"], "w_v": a[X + "Wv"], "w_o": chunks(a[X + "Wo"]),
        "w_g": a[M + "experts_wg"].transpose(1, 0, 2).reshape(P, E * I),
        "w_u": a[M + "experts_wu"].transpose(1, 0, 2).reshape(P, E * I),
        "w_rs": np.concatenate([a[M + "gate_w"], a[M + "shared_wg"], a[M + "shared_wu"]], axis=1),
        "w_d": chunks(a[M + "experts_wd"].reshape(E * I, P)),
        "w_sd": a[M + "shared_wd"],
    }
    nc = bacc.Bacc("TRN2", target_bir_lowering=False, num_devices=1)
    arrays, aps = {}, {}
    for name, v in laid.items():
        arrays[f"in_{name}"] = np.ascontiguousarray(v)
        aps[name] = nc.dram_tensor(f"in_{name}", v.shape, F32, kind="ExternalInput").ap()
    aps["out"] = nc.dram_tensor("out_y", [NSEQ, T, P], F32, kind="ExternalOutput").ap()
    layer_kernel(nc, **aps)
    r = run_bass_kernel_spmd(nc, [arrays], core_ids=[0])
    return r.results[0]["out_y"]
```
